# Optimizing a Trainium2 kernel written in Bass

```python
import numpy as np
import jax
import jax.numpy as jnp

def _softmax(x, axis=-1):
    return jax.nn.softmax(x, axis=axis)

def _gelu(x):
    return jax.nn.gelu(x, approximate=True)

def _silu(x):
    return jax.nn.silu(x)

def _sigmoid(x):
    return jax.nn.sigmoid(x)

def _layernorm(x, axis=-1, eps=1e-05):
    m = jnp.mean(x, axis=axis, keepdims=True)
    v = jnp.var(x, axis=axis, keepdims=True)
    return (x - m) / jnp.sqrt(v + eps)

def _scatter_add(tgt, idx, src, axis=0):
    return tgt.at[idx].add(src)

def _segment_sum(src, seg, n):
    return jax.ops.segment_sum(src, seg, n)
kernel_name = 'mk_gnn_preln_d2_gnn_r8_2a121a'

def setup_inputs(seed: int=0):
    np.random.seed(seed)
    _w = jnp.asarray

    def _rec_inputs():
        import jax
        import jax.numpy as jnp
        _gk = jax.random.key(seed)
        x = -6.415e-05 + 1 * jax.random.normal(jax.random.fold_in(_gk, 1), (1250, 512), jnp.float32)
        src = jax.random.randint(jax.random.fold_in(_gk, 2), (40000,), 0, 1250, jnp.int32)
        dst = jax.random.randint(jax.random.fold_in(_gk, 3), (40000,), 0, 1250, jnp.int32)
        _o = jnp.argsort(dst, stable=True)
        src = src[_o]
        dst = dst[_o]
        edge_attr_64 = 0.000279952 + 1.00013 * jax.random.normal(jax.random.fold_in(_gk, 12), (40000, 64), jnp.float32)
        edge_weight = jax.random.uniform(jax.random.fold_in(_gk, 14), (40000,), jnp.float32, 0.0, 0.999999)
        return (x, src, dst, edge_attr_64, edge_weight)
    x, src, dst, edge_attr_64, edge_weight = _rec_inputs()

    def _L0_gnn_setup():
        import jax, jax.numpy as jnp
        import numpy as np
        N_NODES = 2500
        N_EDGES = 40000
        HIDDEN = 512
        EDGE_DIM = 64
        LN_EPS = 1e-05

        def mish(x):
            return x * jnp.tanh(jax.nn.softplus(x))
        key = jax.random.key(seed)
        ks = jax.random.split(key, 8)
        s = lambda fan_in: 1.0 / np.sqrt(fan_in)
        return {'x': jax.random.normal(ks[0], (N_NODES, HIDDEN), dtype=jnp.float32), 'edge_index': jax.random.randint(ks[1], (2, N_EDGES), 0, N_NODES, dtype=jnp.int64), 'edge_attr': jax.random.normal(ks[2], (N_EDGES, EDGE_DIM), dtype=jnp.float32), 'W1': jax.random.normal(ks[3], (2 * HIDDEN + EDGE_DIM, HIDDEN), dtype=jnp.float32) * s(2 * HIDDEN + EDGE_DIM), 'b1': jnp.zeros((HIDDEN,), dtype=jnp.float32), 'W2': jax.random.normal(ks[4], (HIDDEN, HIDDEN), dtype=jnp.float32) * s(HIDDEN), 'b2': jnp.zeros((HIDDEN,), dtype=jnp.float32), 'W3': jax.random.normal(ks[5], (2 * HIDDEN, HIDDEN), dtype=jnp.float32) * s(2 * HIDDEN), 'b3': jnp.zeros((HIDDEN,), dtype=jnp.float32), 'W4': jax.random.normal(ks[6], (HIDDEN, HIDDEN), dtype=jnp.float32) * s(HIDDEN), 'b4': jnp.zeros((HIDDEN,), dtype=jnp.float32), 'gamma': jnp.ones((HIDDEN,), dtype=jnp.float32), 'beta': jnp.zeros((HIDDEN,), dtype=jnp.float32)}
    _L0_gnn_all = _L0_gnn_setup()
    _L0_gnn_in = {k: v for k, v in _L0_gnn_all.items() if k in ('W1', 'b1', 'W2', 'b2', 'W3', 'b3', 'W4', 'b4', 'gamma', 'beta')}
    del _L0_gnn_all

    def _L1_gnn_setup():
        import jax, jax.numpy as jnp
        import numpy as np
        N_NODES = 12500
        N_EDGES = 400000
        IN_F = 512
        OUT_F = 512
        RANK = 64
        key = jax.random.key(seed)
        ks = jax.random.split(key, 8)
        inp = jax.random.normal(ks[0], (N_NODES, IN_F), dtype=jnp.float32)
        U = jax.random.normal(ks[1], (IN_F, RANK), dtype=jnp.float32) / np.sqrt(IN_F)
        s = jax.random.uniform(ks[2], (RANK,), dtype=jnp.float32)
        Vt = jax.random.normal(ks[3], (RANK, OUT_F), dtype=jnp.float32) / np.sqrt(RANK)
        bias = jax.random.normal(ks[4], (OUT_F,), dtype=jnp.float32) * 0.01
        edge_row = jax.random.randint(ks[5], (N_EDGES,), 0, N_NODES, dtype=jnp.int64 if jax.config.jax_enable_x64 else jnp.int32)
        edge_col = jax.random.randint(ks[6], (N_EDGES,), 0, N_NODES, dtype=jnp.int64 if jax.config.jax_enable_x64 else jnp.int32)
        edge_val = jax.random.uniform(ks[7], (N_EDGES,), dtype=jnp.float32)
        return {'input': inp, 'U': U, 's': s, 'Vt': Vt, 'bias': bias, 'edge_row': edge_row, 'edge_col': edge_col, 'edge_val': edge_val}
    _L1_gnn_all = _L1_gnn_setup()
    _L1_gnn_in = {k: v for k, v in _L1_gnn_all.items() if k in ('U', 's', 'Vt', 'bias')}
    del _L1_gnn_all
    return {'x': x, 'src': src, 'dst': dst, 'edge_attr_64': edge_attr_64, 'edge_weight': edge_weight, 'L0_gnn_W1': _L0_gnn_in['W1'], 'L0_gnn_b1': _L0_gnn_in['b1'], 'L0_gnn_W2': _L0_gnn_in['W2'], 'L0_gnn_b2': _L0_gnn_in['b2'], 'L0_gnn_W3': _L0_gnn_in['W3'], 'L0_gnn_b3': _L0_gnn_in['b3'], 'L0_gnn_W4': _L0_gnn_in['W4'], 'L0_gnn_b4': _L0_gnn_in['b4'], 'L0_gnn_gamma': _L0_gnn_in['gamma'], 'L0_gnn_beta': _L0_gnn_in['beta'], 'L1_gnn_U': _L1_gnn_in['U'], 'L1_gnn_s': _L1_gnn_in['s'], 'L1_gnn_Vt': _L1_gnn_in['Vt'], 'L1_gnn_bias': _L1_gnn_in['bias']}

def reference(x, src, dst, edge_attr_64, edge_weight, L0_gnn_W1, L0_gnn_b1, L0_gnn_W2, L0_gnn_b2, L0_gnn_W3, L0_gnn_b3, L0_gnn_W4, L0_gnn_b4, L0_gnn_gamma, L0_gnn_beta, L1_gnn_U, L1_gnn_s, L1_gnn_Vt, L1_gnn_bias):
    import jax
    import jax.numpy as jnp

    def _L0_gnn_ref(x, edge_index, edge_attr, W1, b1, W2, b2, W3, b3, W4, b4, gamma, beta):
        import jax, jax.numpy as jnp
        import numpy as np
        N_NODES = 2500
        N_EDGES = 40000
        HIDDEN = 512
        EDGE_DIM = 64
        LN_EPS = 1e-05

        def mish(x):
            return x * jnp.tanh(jax.nn.softplus(x))
        src, dst = (edge_index[0], edge_index[1])
        edge_feat = jnp.concatenate([x[src], x[dst], edge_attr], axis=-1)
        h = mish(edge_feat @ W1 + b1)
        messages = mish(h @ W2 + b2)
        agg = jax.ops.segment_sum(messages, dst, num_segments=x.shape[0])
        u = mish(jnp.concatenate([x, agg], axis=-1) @ W3 + b3)
        out = u @ W4 + b4
        y = x + out
        mu = jnp.mean(y, axis=-1, keepdims=True)
        var = jnp.mean(jnp.square(y - mu), axis=-1, keepdims=True)
        return (y - mu) * jax.lax.rsqrt(var + LN_EPS) * gamma + beta

    def _L1_gnn_ref(input, U, s, Vt, bias, edge_row, edge_col, edge_val):
        import jax, jax.numpy as jnp
        import numpy as np
        N_NODES = 12500
        N_EDGES = 400000
        IN_F = 512
        OUT_F = 512
        RANK = 64
        support = input @ U * s
        support = support @ Vt
        gathered = support[edge_col] * edge_val[:, None]
        output = jax.ops.segment_sum(gathered, edge_row, num_segments=input.shape[0])
        output = output + bias
        return jax.nn.relu(output)
    edge_index = jnp.stack([src, dst])
    h = jnp.maximum(_layernorm(x, axis=-1), 0.0)
    x = x + _L0_gnn_ref(h, edge_index, edge_attr_64, L0_gnn_W1, L0_gnn_b1, L0_gnn_W2, L0_gnn_b2, L0_gnn_W3, L0_gnn_b3, L0_gnn_W4, L0_gnn_b4, L0_gnn_gamma, L0_gnn_beta)
    h = jnp.maximum(_layernorm(x, axis=-1), 0.0)
    x = x + _L1_gnn_ref(h, L1_gnn_U, L1_gnn_s, L1_gnn_Vt, L1_gnn_bias, src, dst, edge_weight)
    return x

_drawn_inputs = setup_inputs


def setup_inputs(seed=0):
    import zlib

    import numpy as np

    out = dict(_drawn_inputs(seed))
    spreads = {'L0_gnn_b1': (0.0, 0.1),
     'L0_gnn_b2': (0.0, 0.1),
     'L0_gnn_b3': (0.0, 0.73),
     'L0_gnn_b4': (0.0, 0.51),
     'L0_gnn_gamma': (1.0, 0.2),
     'L0_gnn_beta': (0.0, 0.1)}
    factors = {'L1_gnn_bias': 35.785}
    for name, (base, spread) in spreads.items():
        noise = np.random.default_rng([zlib.crc32(name.encode()), seed]).standard_normal(out[name].shape)
        drawn = base * np.exp(spread * noise) if base else spread * noise
        out[name] = jnp.asarray(drawn.astype(out[name].dtype))
    for name, factor in factors.items():
        out[name] = (out[name] * factor).astype(out[name].dtype)
    return out
```

```python
import concourse.bass as bass
from concourse import mybir
from concourse.alu_op_type import AluOpType as ALU
from contextlib import ExitStack

F32 = mybir.dt.float32
F32R = mybir.dt.float32r
I32 = mybir.dt.int32
ACT = mybir.ActivationFunctionType
AX = mybir.AxisListType

P = 128
H = 512
KC = H // P
N = 1250
NCH = -(-N // P)
NP = NCH * P
NTAIL = N - (NCH - 1) * P
E = 40000
SUB = 4
G = SUB * P
NG = -(-E // G)
FULL = E // G
ETAIL = E - FULL * G
ED = 64
R = 64
WIN = 32
LN_EPS = 1e-5
XMAX = 20.0
SQ = 2.0 ** 32
HALF = [(0, 64), (64, 128)]
NBLK = [(0, 512), (512, 512), (1024, 256)]
SBLK = [(0, 512), (512, 512), (1024, N - 1024)]


class At:

    def __init__(self, reg, const):
        self.reg, self.const = reg, const

    def __add__(self, n):
        return At(self.reg, self.const + n)

    def val(self, mult=1, add=0):
        c = self.const * mult + add
        return c if self.reg is None else self.reg * (2 * SUB * mult) + c

    def group(self, mult=1, add=0):
        c = self.const // SUB * mult + add
        return c if self.reg is None else self.reg * (2 * mult) + c

    def pair(self, mult, add=0):
        c = self.const // (2 * SUB) * mult + add
        return c if self.reg is None else self.reg * mult + c

    @property
    def j(self):
        return self.const % SUB

    @property
    def par(self):
        return self.const // SUB % 2

    def has(self, n):
        return self.reg is not None or 0 <= self.const < n


def slots(eng, first, head, tail, last, step):
    for s in range(first, head):
        step(At(None, s))
    with eng.Fori(head // (2 * SUB), tail // (2 * SUB)) as i:
        for k in range(2 * SUB):
            step(At(i, k))
    for s in range(tail, last):
        step(At(None, s))


class Line:

    def __init__(self, sem):
        self.sem, self.n = sem, 0

    def inc(self, ins, by=1):
        ins.then_inc(self.sem, by)
        self.n += by
        return self.n


def gnn_two_layers(nc, x, src_idx, dst_rows, src_cols, dst_cols, eaT, ew_cols, W1, b1, W2, b2, W3, b3, W4, b4,
                   gamma, beta, U, sv, Vt, bias, out):
    ctx = ExitStack()
    names = set()

    def sem(name):
        assert name not in names
        names.add(name)
        return ctx.enter_context(nc.semaphore(name))

    def scope():
        st = ExitStack()
        return (st, lambda n, s, d=F32: st.enter_context(nc.sbuf_tensor(n, s, d)),
                lambda n, s=(P, 512): st.enter_context(nc.psum_tensor(n, list(s), F32)))

    def dram(name, shape, dt=F32):
        return nc.dram_tensor(name, shape, dt, kind="Internal").ap()

    def row_bcast(ap, n, parts):
        return ap.rearrange("(a n) -> a n", a=1).to_broadcast([parts, n])

    A_d = dram("A_tab", (NP, H))
    Bh_d = dram("Bh_tab", (NP, H))
    Bl_d = dram("Bl_tab", (NP, H))
    h_d = dram("h_tab", (NP, H))
    agg_d = dram("agg_tab", (NP, H))
    Sh_d = dram("Sh_tab", (NP, R))
    Sl_d = dram("Sl_tab", (NP, R))
    win_d = dram("win_tab", (NG, 2))

    with ctx:
        pst, sb, _ = scope()
        ctx.enter_context(pst)
        ident = sb("ident", [P, P])
        iota_w = sb("iota_w", [P, WIN])
        iota_p = sb("iota_p", [P, 1])
        base_b = sb("base_b", [P, NG, 2])
        base_i = sb("base_i", [1, NG], I32)
        wide_i = sb("wide_i", [1, 1], I32)
        dcol = sb("dcol", [P, NG * SUB])
        nTh = sb("nTh", [P, KC, NP], F32R)
        nTl = sb("nTl", [P, KC, NP], F32R)
        est, sb, _ = scope()
        W2h = sb("W2h", [P, KC, H], F32R)
        W2l = sb("W2l", [P, KC, H], F32R)
        b2r = sb("b2r", [64, H], F32R)
        ones = sb("ones", [64, P], F32R)
        eaW2 = sb("eaW2", [P, H], F32R)
        eaW1 = [sb(f"eaW1_{i}", [P, H], F32R) for i in range(2)]

        def newton(e, link, var, r, t):
            link(e.tensor_tensor(t, r, r, ALU.mult))
            link(e.tensor_tensor(t, t, var, ALU.mult))
            link(e.tensor_scalar(t, t, -0.5, 1.5, ALU.mult, ALU.add))
            link(e.tensor_tensor(r, r, t, ALU.mult))

        st, sb1, ps1 = scope()
        with st:
            xs = sb1("xs", [P, NCH, H])
            hs = sb1("hs", [P, NCH, H])
            w1raw = sb1("w1raw", [P, 2 * KC, H])
            w1h = sb1("w1h", [P, 2 * KC, H], F32R)
            w1l = sb1("w1l", [P, 2 * KC, H], F32R)
            w2raw = sb1("w2raw", [P, KC, H])
            wcraw = sb1("wcraw", [P, H])
            b1b = sb1("b1b", [P, H])
            b2raw = sb1("b2raw", [64, H])
            dsti = sb1("dsti", [NG, G], I32)
            dcoli = sb1("dcoli", [P, NG * SUB], I32)
            win = sb1("win", [NG, 2])
            mx = sb1("mx", [NG, 1])
            iota_i = sb1("iota_i", [P, WIN], I32)
            iop_i = sb1("iop_i", [P, 1], I32)
            stats = sb1("stats", [P, NCH, 6])
            mv = sb1("mv", [P, NCH, 2])
            var = sb1("var", [P, NCH])
            lnv = sb1("lnv", [P, NCH])
            rstd = sb1("rstd", [P, NCH])
            nmr = sb1("nmr", [P, NCH])
            tmp = sb1("tmp", [P, NCH])
            ta = [sb1(f"ta{i}", [P, H]) for i in range(2)]
            tb = [sb1(f"tb{i}", [P, H]) for i in range(2)]
            tbh = [sb1(f"tbh{i}", [P, H], F32R) for i in range(2)]
            tbl = [sb1(f"tbl{i}", [P, H], F32R) for i in range(2)]
            zero = sb1("zero", [P, NCH * H // 2])
            pT = [ps1(f"pT{i}") for i in range(2)]
            pA = [ps1(f"pA{i}") for i in range(2)]
            pB = [ps1(f"pB{i}") for i in range(2)]

            q_x = [sem(f"q_x{i}") for i in range(3)]
            q_dst = sem("q_dst")
            q_w1 = sem("q_w1")
            q_w2 = sem("q_w2")
            q_win = sem("q_win")
            q_winb = sem("q_winb")
            q_st = [sem(f"q_st{i}") for i in range(2)]
            q_h = sem("q_h")
            c_g = Line(sem("c_g"))
            c_v = Line(sem("c_v"))
            c_a = sem("c_a")
            c_hT = sem("c_hT")
            c_tr = sem("c_tr")
            c_hi = sem("c_hi")
            c_lo = sem("c_lo")
            c_A = sem("c_A")
            c_B = sem("c_B")
            c_ta = sem("c_ta")
            c_tb = sem("c_tb")
            c_pad = sem("c_pad")
            c_bz = sem("c_bz")
            v = {}

            with nc.Block() as blk:
                def store_b(e, c):
                    i = c % 2
                    e.wait_ge(c_B, c + 1)
                    if c >= 2:
                        e.wait_ge(q_st[i], 48 * (c // 2))
                    e.tensor_tensor(tb[i][:], pB[i][:, :], b1b[:], ALU.add).then_inc(c_tb, 1)
                    e.wait_ge(c_tb, 3 * c + 1)
                    e.tensor_copy(tbh[i][:], tb[i][:]).then_inc(c_tb, 1)
                    e.wait_ge(c_tb, 3 * c + 2)
                    e.tensor_tensor(tbl[i][:], tb[i][:], tbh[i][:], ALU.subtract).then_inc(c_tb, 1)

                def evac(e, c):
                    i = c % 2
                    e.wait_ge(c_tr, c + 1)
                    e.activation(nTh[:, :, c * P:(c + 1) * P], pT[i][:, :].rearrange("p (k n) -> p k n", k=KC),
                                 ACT.Copy).then_inc(c_hi, 1)
                    if c >= 1:
                        store_a(e, c - 1)

                def store_a(e, c):
                    i = c % 2
                    e.wait_ge(c_A, c + 1)
                    if c >= 2:
                        e.wait_ge(q_st[i], 48 * (c // 2))
                    e.activation(ta[i][:], pA[i][:, :], ACT.Copy).then_inc(c_ta, 1)

                @blk.vector
                def _(e):
                    def link(ins):
                        c_v.inc(ins)
                        e.wait_ge(c_v.sem, c_v.n)

                    c_pad_i = e.memset(xs[:, NCH - 1, :], 0.0)
                    c_pad_i.then_inc(c_pad, 1)
                    c_v.inc(e.memset(zero[:], 0.0))
                    v["zero"] = c_v.n
                    e.memset(b2raw[:], 0.0).then_inc(c_bz, 1)
                    e.wait_ge(q_dst, 32)
                    c_v.inc(e.tensor_reduce(win[:, 0:1], dsti[:, :], AX.X, ALU.min))
                    link(e.tensor_reduce(mx[:], dsti[:, :], AX.X, ALU.max))
                    link(e.tensor_scalar(win[:, 0:1], win[:, 0:1], float(NP - WIN), None, ALU.min))
                    link(e.tensor_tensor(win[:, 1:2], mx[:], win[:, 0:1], ALU.subtract))
                    v["win"] = c_v.n
                    c_v.inc(e.tensor_copy(dcol[:], dcoli[:]))
                    e.wait_ge(c_g.sem, 3)
                    c_v.inc(e.tensor_copy(iota_w[:], iota_i[:]))
                    c_v.inc(e.tensor_scalar(iop_i[:], iop_i[:], WIN - 1, None, ALU.bitwise_and))
                    e.wait_ge(c_v.sem, c_v.n)
                    c_v.inc(e.tensor_copy(iota_p[:], iop_i[:]))
                    for c in range(NCH):
                        if c in (0, 1, 5):
                            e.wait_ge(q_x[(0, 1, 5).index(c)], (16, 16, 32)[(0, 1, 5).index(c)])
                        c_v.inc(e.bn_stats(stats[:, c, :], xs[:, c, :]))
                    e.wait_ge(c_v.sem, c_v.n)
                    for c in range(NCH):
                        c_v.inc(e.bn_aggr(mv[:, c, :], stats[:, c, :]))
                    e.wait_ge(c_v.sem, c_v.n)
                    link(e.tensor_scalar(var[:], mv[:, :, 1], LN_EPS, None, ALU.add))
                    v["var"] = c_v.n
                    e.wait_ge(c_a, 2)
                    newton(e, link, var[:], rstd[:], tmp[:])
                    link(e.scalar_tensor_tensor(nmr[:], mv[:, :, 0], -1.0, rstd[:], ALU.mult, ALU.mult))
                    v["rstd"] = c_v.n
                    e.wait_ge(q_w1, 16)
                    link(e.tensor_copy(w1h[:], w1raw[:]))
                    link(e.tensor_tensor(w1l[:], w1raw[:], w1h[:], ALU.subtract))
                    v["w1"] = c_v.n
                    e.wait_ge(q_w2, 6 * 16)
                    e.wait_ge(c_g.sem, 5)
                    link(e.tensor_scalar(w2raw[:], w2raw[:], -1.0, None, ALU.mult))
                    c_v.inc(e.tensor_copy(W2h[:], w2raw[:]))
                    c_v.inc(e.tensor_copy(eaW2[:], wcraw[:]))
                    for i in range(2):
                        c_v.inc(e.tensor_copy(eaW1[i][64:128, :], wcraw[64:128, :]))
                    c_v.inc(e.tensor_copy(b2r[:], b2raw[:]))
                    e.wait_ge(c_v.sem, c_v.n)
                    c_v.inc(e.tensor_tensor(W2l[:], w2raw[:], W2h[:], ALU.subtract))
                    c_v.inc(e.tensor_tensor(eaW2[64:128, :], wcraw[64:128, :], eaW2[64:128, :], ALU.subtract))
                    link(e.tensor_tensor(b2r[32:64, :], b2raw[32:64, :], b2r[32:64, :], ALU.subtract))
                    v["w2"] = c_v.n
                    e.wait_ge(q_winb, 16)
                    c_v.inc(e.tensor_copy(base_i[0:1, :], base_b[0:1, :, 0]))
                    c_v.inc(e.tensor_reduce(wide_i[0:1, :], base_b[0:1, :, 1], AX.X, ALU.max))
                    for c in range(NCH):
                        i = c % 2
                        e.wait_ge(c_hi, c + 1)
                        e.tensor_tensor(nTl[:, :, c * P:(c + 1) * P], pT[i][:, :].rearrange("p (k n) -> p k n", k=KC),
                                        nTh[:, :, c * P:(c + 1) * P], ALU.subtract).then_inc(c_lo, 1)
                        if c >= 1:
                            store_b(e, c - 1)
                    store_b(e, NCH - 1)

                @blk.gpsimd
                def _(e):
                    c_g.inc(e.memset(ident[:], 0.0))
                    c_g.inc(e.iota(iota_i[:], pattern=[[1, WIN]], base=0, channel_multiplier=0))
                    c_g.inc(e.iota(iop_i[:], pattern=[[0, 1]], base=0, channel_multiplier=1))
                    e.wait_ge(c_g.sem, 1)
                    c_g.inc(e.affine_select(out=ident[:], in_=ident[:], compare_op=ALU.not_equal, fill=1.0,
                                            base=0, pattern=[[-1, P]], channel_multiplier=1))
                    c_g.inc(e.memset(ones[:].bitcast(F32), 1.0))

                @blk.scalar
                def _(e):
                    e.preload_act_table_set("natural_log_exp_and_others")
                    e.wait_ge(c_v.sem, v["var"])
                    e.activation(lnv[:], var[:], ACT.Ln).then_inc(c_a, 1)
                    e.wait_ge(c_a, 1)
                    e.activation(rstd[:], lnv[:], ACT.Exp, scale=-0.5).then_inc(c_a, 1)
                    e.wait_ge(c_v.sem, v["rstd"])
                    for c in range(NCH):
                        e.activation(hs[:, c, :], xs[:, c, :], ACT.Relu, bias=nmr[:, c:c + 1],
                                     scale=rstd[:, c:c + 1]).then_inc(c_hT, 1)
                        if c >= 1:
                            evac(e, c - 1)
                    evac(e, NCH - 1)
                    store_a(e, NCH - 1)

                @blk.tensor
                def _(e):
                    e.wait_ge(c_g.sem, 4)

                    def tables(c):
                        i = c % 2
                        if c == 0:
                            e.wait_ge(c_v.sem, v["w1"])
                        e.wait_ge(c_lo, c + 1)
                        if c >= 2:
                            e.wait_ge(c_ta, c - 1)
                            e.wait_ge(c_tb, 3 * (c - 2) + 1)
                        for half, bank, done in ((0, pA[i], c_A), (1, pB[i], c_B)):
                            n = 0
                            for k in range(KC):
                                for a, w in ((nTh, w1h), (nTl, w1h), (nTh, w1l)):
                                    last = e.matmul(bank[:, :], a[:, k, c * P:(c + 1) * P], w[:, half * KC + k, :],
                                                    start=n == 0, stop=n == 3 * KC - 1)
                                    n += 1
                            last.then_inc(done, 1)

                    for c in range(NCH):
                        e.wait_ge(c_hT, c + 1)
                        if c >= 2:
                            e.wait_ge(c_lo, c - 1)
                        for k in range(KC):
                            last = e.transpose(pT[c % 2][:, k * P:(k + 1) * P], hs[:, c, k * P:(k + 1) * P], ident[:])
                        last.then_inc(c_tr, 1)
                        if c >= 1:
                            tables(c - 1)
                    tables(NCH - 1)

                @blk.sync
                def _(e):
                    xv = x[0:(NCH - 1) * P, :].rearrange("(c p) n -> p c n", p=P)
                    e.dma_start(xs[:, 0:1, :], xv[:, 0:1, :]).then_inc(q_x[0], 16)
                    e.dma_start(xs[:, 1:5, :], xv[:, 1:5, :]).then_inc(q_x[1], 16)
                    e.dma_start(xs[:, 5:NCH - 1, :], xv[:, 5:NCH - 1, :]).then_inc(q_x[2], 16)
                    e.wait_ge(c_pad, 1)
                    e.dma_start(xs[0:NTAIL, NCH - 1, :], x[(NCH - 1) * P:N, :]).then_inc(q_x[2], 16)
                    e.dma_start(dsti[:], dst_rows).then_inc(q_dst, 16)
                    e.dma_start(dcoli[:], dst_cols).then_inc(q_dst, 16)
                    e.dma_start(w1raw[:], W1[0:2 * H, :].rearrange("(c p) n -> p c n", p=P)).then_inc(q_w1, 16)
                    e.dma_start(w2raw[:], W2.rearrange("(c p) n -> p c n", p=P)).then_inc(q_w2, 16)
                    for a, b in HALF:
                        e.dma_start(wcraw[a:b, :], W1[2 * H:2 * H + ED, :]).then_inc(q_w2, 16)
                    e.wait_ge(c_bz, 1)
                    for p in (0, 32):
                        e.dma_start(b2raw[p:p + 1, :], b2.rearrange("(a n) -> a n", a=1)).then_inc(q_w2, 16)
                    e.dma_start(b1b[:], row_bcast(b1, H, P)).then_inc(q_w2, 16)
                    e.wait_ge(c_v.sem, v["win"])
                    e.dma_start(win_d, win[:]).then_inc(q_win, 16)
                    e.wait_ge(q_win, 16)
                    e.dma_start(base_b[:].rearrange("p g a -> p (g a)"),
                                row_bcast(win_d.rearrange("g a -> (g a)"), 2 * NG, P)).then_inc(q_winb, 16)
                    e.wait_ge(c_v.sem, v["zero"])
                    for i in range(2):
                        e.dma_start(agg_d[i * NP // 2:(i + 1) * NP // 2, :].rearrange("(p c) n -> p (c n)", p=P),
                                    zero[:]).then_inc(q_h, 16)
                    for c in range(NCH):
                        i = c % 2
                        rows = slice(c * P, (c + 1) * P)
                        e.wait_ge(c_ta, c + 1)
                        e.dma_start(A_d[rows, :], ta[i][:]).then_inc(q_st[i], 16)
                        e.wait_ge(c_tb, 3 * c + 3)
                        e.dma_start(Bh_d[rows, :], tbh[i][:].bitcast(F32)).then_inc(q_st[i], 16)
                        e.dma_start(Bl_d[rows, :], tbl[i][:].bitcast(F32)).then_inc(q_st[i], 16)
                    e.wait_ge(c_hT, NCH)
                    e.dma_start(h_d.rearrange("(c p) n -> p c n", p=P), hs[:]).then_inc(q_h, 16)
                    e.wait_ge(q_st[0], 48 * (NCH // 2))
                    e.wait_ge(q_st[1], 48 * (NCH // 2))
                    e.wait_ge(q_h, 48)

        with est:
            edge_phase(nc, scope, sem, locals())

        xst, sb, _ = scope()
        with xst:
            x1 = sb("x1", [P, NCH, H])
            node_phase(nc, scope, sem, locals())
            conv_phase(nc, scope, sem, locals())


def edge_phase(nc, scope, sem, k):
    ident, iota_w, iota_p, base_b, base_i, dcol = (k[n] for n in ("ident", "iota_w", "iota_p", "base_b", "base_i", "dcol"))
    W2h, W2l, b2r, ones, eaW2, eaW1 = (k[n] for n in ("W2h", "W2l", "b2r", "ones", "eaW2", "eaW1"))
    A_d, Bh_d, Bl_d, agg_d, eaT, src_idx, dst_rows = (k[n] for n in ("A_d", "Bh_d", "Bl_d", "agg_d", "eaT", "src_idx", "dst_rows"))
    row_bcast = k["row_bcast"]

    PRE_AHEAD = 5
    ACT_MSG = 1
    DVE_PRE = 4
    DVE_MSG = 2
    SEG_LAG = 3
    PREP_AHEAD = 8
    BANK = (0, 1, 2, 0, 1, 2, 0, 1)
    BACK = (2, 2, 3, 3, 3, 3, 3, 3)
    FIRST, LOOP0 = -PREP_AHEAD, 16
    LOOP1 = 4 * FULL - 8
    LAST = 4 * NG + SEG_LAG + 2
    PRES = 4 * NG
    MSGS = 4 * FULL + 1
    assert (LOOP1 - LOOP0) % 8 == 0 and G * FULL + ETAIL == E and 0 < ETAIL <= P

    st, sb, ps = scope()
    with st:
        xg = [sb(f"xg{i}", [P, SUB, H]) for i in range(2)]
        idx = [sb(f"idx{i}", [P, SUB], I32) for i in range(2)]
        ea = [sb(f"ea{i}", [P, G]) for i in range(2)]
        db = [sb(f"db{i}", [64, G], I32) for i in range(2)]
        M1 = [sb(f"M1_{i}", [P, G], F32R) for i in range(2)]
        M2 = [sb(f"M2_{i}", [P, G], F32R) for i in range(2)]
        hTh = [sb(f"hTh{i}", [P, KC, G], F32R) for i in range(2)]
        hTl = [sb(f"hTl{i}", [P, KC, G], F32R) for i in range(2)]
        rp = [sb(f"rp{i}", [P, G]) for i in range(2)]
        rm = [sb(f"rm{i}", [P, H]) for i in range(2)]
        tp = [sb(f"tp{i}", [P, G]) for i in range(2)]
        tm = [sb(f"tm{i}", [P, H]) for i in range(2)]
        mh = [sb(f"mh{i}", [P, H], F32R) for i in range(4)]
        ml = [sb(f"ml{i}", [P, H], F32R) for i in range(4)]
        oh = [sb(f"oh{i}", [P, SUB, P], F32R) for i in range(2)]
        ev = [sb(f"ev{i}", [WIN, H]) for i in range(2)]
        bp = [ps(f"bp{i}") for i in range(3)]
        bm = [ps(f"bm{i}") for i in range(4)]
        bs = ps("bs")

        q_in = [sem(f"e_in{i}") for i in range(2)]
        q_win = [sem(f"e_win{i}") for i in range(2)]
        q_ix = [sem(f"e_ix{i}") for i in range(2)]
        q_ga = [sem(f"e_ga{i}") for i in range(2)]
        q_acc = sem("e_acc")
        s_zero = sem("e_zero")
        s_go = sem("e_go")
        s_prep = sem("e_prep")
        s_oh = sem("e_oh")
        s_pre = sem("e_pre")
        s_msg = sem("e_msg")
        s_seg = sem("e_seg")
        a_pre = sem("a_pre")
        a_msg = sem("a_msg")
        v_pre = sem("v_pre")
        v_msg = sem("v_msg")
        s_ev = sem("e_ev")

        def tail(u):
            return u.reg is None and u.const >= 4 * FULL

        def wait(e, s, val):
            if not (isinstance(val, int) and val < 1):
                e.wait_ge(s, val)

        with nc.Block() as blk:
            @blk.sync
            def _(e):
                def loads(u):
                    p, n = u.par, ETAIL if tail(u) else G
                    wait(e, s_prep, u.group(4, -4))
                    for a, b in HALF:
                        e.dma_start(ea[p][a:b, 0:n], eaT[:, bass.ds(u.group(G), n)]).then_inc(q_in[p], 16)
                    e.dma_start(db[p][:, 0:n], dst_rows[bass.ds(u.group(), 1), 0:n].to_broadcast([64, n]))\
                     .then_inc(q_in[p], 16)
                    wait(e, q_ga[p], u.pair(64, 0))
                    e.dma_start(idx[p][:], src_idx[bass.ds(u.group(), 1), :, :].rearrange("a p s -> (a p) s"))\
                     .then_inc(q_ix[p], 16)
                    b = e.value_load(base_i[0:1, bass.ds(u.group(), 1)], min_val=0, max_val=NP - WIN)
                    wait(e, s_pre, u.val(1, -4))
                    e.dma_start(eaW1[p][0:32, :].bitcast(F32), Bh_d[bass.ds(b, WIN), :]).then_inc(q_win[p], 16)
                    e.dma_start(eaW1[p][32:64, :].bitcast(F32), Bl_d[bass.ds(b, WIN), :]).then_inc(q_win[p], 16)

                loads(At(None, 0))
                loads(At(None, 4))
                with e.Fori(1, FULL // 2) as i:
                    loads(At(i, 0))
                    loads(At(i, 4))
                loads(At(None, 4 * FULL))
                e.wait_ge(q_acc, 16 * NG)

            @blk.gpsimd
            def _(e):
                def gather(u):
                    p, n, r = u.par, 1 if tail(u) else SUB, ETAIL if tail(u) else P
                    e.wait_ge(q_ix[p], u.pair(16, 16))
                    wait(e, s_pre, u.val(1, -4))
                    e.sem_inc(s_go, 1)
                    for t in range(n):
                        e.indirect_dma_start(out=xg[p][0:r, t, :], out_offset=None, in_=A_d,
                                             in_offset=bass.IndirectOffsetOnAxis(ap=idx[p][0:r, t:t + 1], axis=0))\
                         .then_inc(q_ga[p], 16)

                def accumulate(u):
                    b = e.value_load(base_i[0:1, bass.ds(u.group(), 1)], min_val=0, max_val=NP - WIN)
                    e.wait_ge(s_ev, u.group(1, 1))
                    wait(e, q_acc, u.group(16))
                    e.dma_start(agg_d[bass.ds(b, WIN), :], ev[u.par][:], accum_op=ALU.add).then_inc(q_acc, 16)

                for i in range(2):
                    e.memset(oh[i][:].bitcast(F32), 0.0).then_inc(s_zero, 1)
                for g in range(6):
                    if g >= 4:
                        accumulate(At(None, 4 * g - 16))
                    gather(At(None, 4 * g))
                with e.Fori(3, FULL // 2) as i:
                    for k in (0, 4):
                        accumulate(At(i, k - 16))
                        gather(At(i, k))
                accumulate(At(None, 4 * (FULL - 4)))
                gather(At(None, 4 * FULL))
                for g in range(FULL - 3, NG):
                    accumulate(At(None, 4 * g))

            @blk.tensor
            def _(e):
                def pre(u):
                    j, p, w, bank = u.j, u.par, ETAIL if tail(u) else G, bp[BANK[u.const % 8]]
                    wait(e, v_pre, u.val(3, 1 - 3 * BACK[u.const % 8]))
                    if j == 0:
                        n = 16 if tail(u) else 64
                        e.wait_ge(q_ga[p], u.pair(64, n))
                        e.wait_ge(q_win[p], u.pair(32, 32))
                        e.wait_ge(s_prep, u.group(4, 4))
                    for t in range(SUB if w == G else 1):
                        r = min(P, w)
                        e.matmul(bank[:, t * P:t * P + r], xg[p][0:r, t, j * P:(j + 1) * P], ident[0:r, 0:r],
                                 start=t == 0, stop=False, is_transpose=True, skip_group_check=True)
                    e.matmul(bank[:, 0:w], eaW1[p][:, j * P:(j + 1) * P], M1[p][:, 0:w], start=False, stop=False,
                             skip_group_check=True)
                    e.matmul(bank[:, 0:w], eaW2[:, j * P:(j + 1) * P], M2[p][:, 0:w], start=False, stop=True,
                             skip_group_check=True).then_inc(s_pre, 1)

                def msg(u):
                    j, p, r = u.j, u.par, ETAIL if tail(u) else P
                    wait(e, v_msg, u.val(3, 1 - 12))
                    bank = bm[j]
                    e.matmul(bank[0:r, :], ones[:, 0:r], b2r[:], start=True, stop=False)
                    for c in range(KC):
                        if j == 0:
                            e.wait_ge(v_pre, u.val(3, 3 * c + 3))
                        for a, w in ((hTh, W2h), (hTl, W2h), (hTh, W2l)):
                            last = e.matmul(bank[0:r, :], a[p][:, c, j * P:j * P + r], w[:, c, :], start=False,
                                            stop=c == KC - 1 and w is W2l)
                    last.then_inc(s_msg, 1)

                def seg(u):
                    j, p, r = u.j, u.par, ETAIL if tail(u) else P
                    e.wait_ge(v_msg, u.val(3, 3))
                    if j == 0:
                        e.wait_ge(s_oh, u.group(SUB, 1 if tail(u) else SUB))
                        wait(e, s_ev, u.group())
                    end = j == SUB - 1 or r < P
                    e.matmul(bs[:, :], oh[p][0:r, j, :], mh[j][0:r, :], start=j == 0, stop=False)
                    e.matmul(bs[:, :], oh[p][0:r, j, :], ml[j][0:r, :], start=False, stop=end).then_inc(s_seg, 1)

                def step(s):
                    if (s + PRE_AHEAD).has(PRES):
                        pre(s + PRE_AHEAD)
                    if s.has(MSGS):
                        msg(s)
                    if (s + -SEG_LAG).has(MSGS):
                        seg(s + -SEG_LAG)

                slots(e, FIRST, LOOP0, LOOP1, LAST, step)

            @blk.scalar
            def _(e):
                def chain(u, k, src, dst, sa, n):
                    if k == 0:
                        e.activation(dst, src, ACT.Exp).then_inc(sa, 1)
                        return
                    e.wait_ge(sa, u.val(4, k))
                    if k == 1:
                        e.activation(dst, dst, ACT.Square, bias=SQ, scale=SQ).then_inc(sa, 1)
                    elif k == 2:
                        e.activation(dst, dst, ACT.Ln, bias=0.5, scale=0.5 / (SQ * SQ)).then_inc(sa, 1)
                    else:
                        e.activation(dst, dst, ACT.Exp, scale=-1.0).then_inc(sa, 1)

                def step(s):
                    u, m = s + PRE_AHEAD, s + -ACT_MSG
                    for k in range(4):
                        if u.has(PRES):
                            w = ETAIL if tail(u) else G
                            if k == 0:
                                wait(e, v_pre, u.val(3, 1 - 6))
                                e.wait_ge(s_pre, u.val(1, 1))
                            chain(u, k, bp[BANK[u.const % 8]][:, 0:w], rp[u.const % 2][:, 0:w], a_pre, w)
                        if m.has(MSGS):
                            r = ETAIL if tail(m) else P
                            if k == 0:
                                wait(e, v_msg, m.val(3, 1 - 6))
                                e.wait_ge(s_msg, m.val(1, 1))
                            chain(m, k, bm[m.j][0:r, :], rm[m.const % 2][0:r, :], a_msg, r)

                slots(e, FIRST, LOOP0, LOOP1, LAST, step)

            @blk.vector
            def _(e):
                def prep(u):
                    p, n, gs = u.par, ETAIL if tail(u) else G, bass.ds(u.group(), 1)
                    e.wait_ge(q_in[p], u.pair(48, 48))
                    wait(e, s_pre, u.val(1, -4))
                    e.tensor_copy(M2[p][:, 0:n], ea[p][:, 0:n]).then_inc(s_prep, 1)
                    e.tensor_copy(M1[p][64:128, 0:n], ea[p][64:128, 0:n]).then_inc(s_prep, 1)
                    e.tensor_scalar(M1[p][0:64, 0:n], db[p][:, 0:n], base_b[0:64, gs, 0], iota_p[0:64, :],
                                    ALU.subtract, ALU.is_equal).then_inc(s_prep, 1)
                    e.wait_ge(s_prep, u.group(4, 3))
                    e.tensor_tensor(M2[p][0:64, 0:n], ea[p][0:64, 0:n], M2[p][0:64, 0:n], ALU.subtract).then_inc(s_prep, 1)

                def onehots(u):
                    wait(e, s_seg, u.val(1, -4))
                    for j in range(1 if tail(u) else SUB):
                        col = bass.ds(u.val(1, j), 1)
                        e.tensor_scalar(oh[u.par][:, j, 0:WIN], iota_w[:], base_b[:, bass.ds(u.group(), 1), 0], dcol[:, col],
                                        ALU.add, ALU.is_equal).then_inc(s_oh, 1)

                def half(u, k, bank, rho, t, hi, lo, sa, sv):
                    if k == 0:
                        e.wait_ge(sa, u.val(4, 4))
                        e.scalar_tensor_tensor(t, rho, 1.0, bank, ALU.subtract, ALU.mult).then_inc(sv, 1)
                        return
                    e.wait_ge(sv, u.val(3, k))
                    if k == 1:
                        e.tensor_copy(hi, t).then_inc(sv, 1)
                    else:
                        e.tensor_tensor(lo, t, hi, ALU.subtract).then_inc(sv, 1)

                def step(s):
                    u, m = s + DVE_PRE, s + -DVE_MSG
                    for k in range(3):
                        if u.has(PRES):
                            w, p, j = ETAIL if tail(u) else G, u.par, u.j
                            if k == 1 and j == 0:
                                wait(e, s_msg, u.val(1, -4))
                            half(u, k, bp[BANK[u.const % 8]][:, 0:w], rp[u.const % 2][:, 0:w], tp[u.const % 2][:, 0:w],
                                 hTh[p][:, j, 0:w], hTl[p][:, j, 0:w], a_pre, v_pre)
                        if m.has(MSGS):
                            r, j = ETAIL if tail(m) else P, m.j
                            if k == 1:
                                wait(e, s_seg, m.val(1, 1 - 4))
                            half(m, k, bm[j][0:r, :], rm[m.const % 2][0:r, :], tm[m.const % 2][0:r, :],
                                 mh[j][0:r, :], ml[j][0:r, :], a_msg, v_msg)
                    g = s + PREP_AHEAD
                    if s.j == 0 and g.has(4 * NG):
                        prep(g)
                    if s.j == 0 and s.has(4 * NG):
                        if s.reg is None and s.const == 0:
                            e.wait_ge(s_zero, 2)
                        onehots(s)
                    q = s + -(SEG_LAG + 1)
                    if (q.j == SUB - 1 and q.has(MSGS)) or (q.reg is None and q.const == MSGS - 1):
                        e.wait_ge(s_seg, q.val(1, 1))
                        wait(e, q_acc, q.group(16, -16))
                        e.tensor_copy(ev[q.par][:], bs[0:WIN, :]).then_inc(s_ev, 1)

                slots(e, FIRST, LOOP0, LOOP1, LAST, step)


def node_phase(nc, scope, sem, k):
    ident, nTh, nTl, x1 = (k[n] for n in ("ident", "nTh", "nTl", "x1"))
    x, h_d, agg_d, W3, b3, W4, b4 = (k[n] for n in ("x", "h_d", "agg_d", "W3", "b3", "W4", "b4"))
    gamma, beta, U, sv, Sh_d, Sl_d, row_bcast, newton = (
        k[n] for n in ("gamma", "beta", "U", "sv", "Sh_d", "Sl_d", "row_bcast", "newton"))
    BLK = [range(0, 4), range(4, 8), range(8, NCH)]
    NB = len(BLK)

    st, sb, ps = scope()
    with st:
        raw = sb("raw", [P, KC, H])
        W3h = sb("W3h", [P, 2 * KC, H], F32R)
        W3l = sb("W3l", [P, 2 * KC, H], F32R)
        W4h = sb("W4h", [P, KC, H], F32R)
        W4l = sb("W4l", [P, KC, H], F32R)
        Us = sb("Us", [P, KC, R])
        b3c = sb("b3c", [P, KC])
        b4b = sb("b4b", [P, H])
        gab = sb("gab", [P, H])
        beb = sb("beb", [P, H])
        svb = sb("svb", [P, R])
        ag = sb("ag", [P, 4, H])
        aTh = sb("aTh", [P, KC, 4 * P], F32R)
        aTl = sb("aTl", [P, KC, 4 * P], F32R)
        uTh = sb("uTh", [P, KC, 4 * P], F32R)
        uTl = sb("uTl", [P, KC, 4 * P], F32R)
        hb = sb("hb", [P, 4, H])
        xb = sb("xb", [P, 4, H])
        xf = [sb(f"xf{i}", [P, H]) for i in range(2)]
        rho = [sb(f"rho{i}", [P, H]) for i in range(2)]
        um = [sb(f"um{i}", [P, H]) for i in range(2)]
        h2T = [sb(f"h2T{i}", [P, KC, P]) for i in range(2)]
        Ss = [sb(f"Ss{i}", [P, R]) for i in range(2)]
        Sh = [sb(f"Sh{i}", [P, R], F32R) for i in range(2)]
        Sl = [sb(f"Sl{i}", [P, R], F32R) for i in range(2)]
        stats = sb("stats3", [P, 4, 6])
        mv = sb("mv3", [P, 4, 2])
        var = sb("var3", [P, 4])
        lnv = sb("lnv3", [P, 4])
        rstd = sb("rstd3", [P, 4])
        nmr = sb("nmr3", [P, 4])
        tmp = sb("tmp3", [P, 4])
        pt = [ps(f"pt{i}") for i in range(2)]
        pu = [ps(f"pu{i}") for i in range(2)]
        po = [ps(f"po{i}") for i in range(2)]
        psS = [ps(f"psS{i}") for i in range(2)]

        q_w = [sem(f"n_w{i}") for i in range(3)]
        q_c = sem("n_c")
        q_ag = [sem(f"n_ag{b}") for b in range(NB)]
        q_hx = [sem(f"n_hx{b}") for b in range(NB)]
        q_S = [sem(f"n_S{i}") for i in range(2)]
        s_raw = sem("n_raw")
        s_tr = sem("n_tr")
        s_ah = sem("n_ah")
        s_al = sem("n_al")
        s_u = sem("n_u")
        s_xf = sem("n_xf")
        s_rho = sem("n_rho")
        s_o = sem("n_o")
        s_hb = sem("n_hb")
        s_ln = sem("n_ln")
        s_var = sem("n_var")
        s_r = sem("n_r")
        s_nm = sem("n_nm")
        s_x1 = sem("n_x1")
        s_h2 = sem("n_h2")
        s_t2 = sem("n_t2")
        s_e2 = sem("n_e2")
        s_S = sem("n_Sm")
        s_Sv = sem("n_Sv")

        def first(b):
            return BLK[b][0]

        with nc.Block() as blk:
            @blk.sync
            def _(e):
                def block_loads(b):
                    n, r0 = len(BLK[b]), first(b) * P
                    if b >= 1:
                        e.wait_ge(s_tr, first(b))
                    e.dma_start(ag[:, 0:n, :], agg_d[r0:r0 + n * P, :].rearrange("(c p) n -> p c n", p=P))\
                     .then_inc(q_ag[b], 16)
                    if b >= 1:
                        e.wait_ge(s_ln, first(b))
                        e.wait_ge(s_t2, first(b))
                    e.dma_start(hb[:, 0:n, :], h_d[r0:r0 + n * P, :].rearrange("(c p) n -> p c n", p=P))\
                     .then_inc(q_hx[b], 16)
                    full = n if b < NB - 1 else n - 1
                    e.dma_start(xb[:, 0:full, :], x[r0:r0 + full * P, :].rearrange("(c p) n -> p c n", p=P))\
                     .then_inc(q_hx[b], 16)
                    if b == NB - 1:
                        e.dma_start(xb[0:NTAIL, full, :], x[r0 + full * P:N, :]).then_inc(q_hx[b], 16)

                for i, src in enumerate((W3[0:H, :], W3[H:2 * H, :], W4)):
                    if i:
                        e.wait_ge(s_raw, i)
                    e.dma_start(raw[:], src.rearrange("(c p) n -> p c n", p=P)).then_inc(q_w[i], 16)
                    if i == 0:
                        e.dma_start(ag[:, 0:4, :], agg_d[0:4 * P, :].rearrange("(c p) n -> p c n", p=P))\
                         .then_inc(q_ag[0], 16)
                        e.dma_start(Us[:], U.rearrange("(c p) n -> p c n", p=P)).then_inc(q_c, 16)
                        with nc.allow_non_contiguous_dma(reason="512 values, once"):
                            e.dma_start(b3c[:], b3.rearrange("(c p) -> p c", p=P)).then_inc(q_c, 16)
                        e.dma_start(b4b[:], row_bcast(b4, H, P)).then_inc(q_c, 16)
                        e.dma_start(gab[:], row_bcast(gamma, H, P)).then_inc(q_c, 16)
                        e.dma_start(beb[:], row_bcast(beta, H, P)).then_inc(q_c, 16)
                        e.dma_start(svb[:], row_bcast(sv, R, P)).then_inc(q_c, 16)
                        e.dma_start(hb[:], h_d[0:4 * P, :].rearrange("(c p) n -> p c n", p=P)).then_inc(q_hx[0], 16)
                        e.dma_start(xb[:], x[0:4 * P, :].rearrange("(c p) n -> p c n", p=P)).then_inc(q_hx[0], 16)
                for b in range(NB):
                    if b >= 1:
                        block_loads(b)
                    for c in BLK[b]:
                        e.wait_ge(s_Sv, 3 * c + 3)
                        rows = slice(c * P, (c + 1) * P)
                        e.dma_start(Sh_d[rows, :], Sh[c % 2][:].bitcast(F32)).then_inc(q_S[c % 2], 16)
                        e.dma_start(Sl_d[rows, :], Sl[c % 2][:].bitcast(F32)).then_inc(q_S[c % 2], 16)
                for i in range(2):
                    e.wait_ge(q_S[i], 32 * (NCH // 2))

            @blk.gpsimd
            def _(e):
                e.wait_ge(q_c, 6 * 16)
                for b in range(NB):
                    n = len(BLK[b])
                    e.wait_ge(q_hx[b], 32 if b < NB - 1 else 48)
                    for c in range(n):
                        r = NTAIL if first(b) + c == NCH - 1 else P
                        e.tensor_tensor(hb[:, c, :], hb[:, c, :], b4b[:], ALU.add).then_inc(s_hb, 1)
                        e.tensor_tensor(xb[0:r, c, :], xb[0:r, c, :], beb[0:r, :], ALU.add).then_inc(s_hb, 1)

            @blk.scalar
            def _(e):
                def stats_chain(i):
                    e.wait_ge(s_var, i + 1)
                    n = len(BLK[i // 2])
                    e.activation(lnv[:, 0:n], var[:, 0:n], ACT.Ln).then_inc(s_r, 1)
                    e.wait_ge(s_r, 2 * i + 1)
                    e.activation(rstd[:, 0:n], lnv[:, 0:n], ACT.Exp, scale=-0.5).then_inc(s_r, 1)

                def evac_agg(b):
                    for i, c in enumerate(BLK[b]):
                        e.wait_ge(s_tr, c + 1)
                        if i == 0 and b:
                            e.wait_ge(s_u, KC * b)
                        e.activation(aTh[:, :, i * P:(i + 1) * P], pt[c % 2][:, :].rearrange("p (k n) -> p k n", k=KC),
                                     ACT.Copy).then_inc(s_ah, 1)

                def chain(b):
                    w = len(BLK[b]) * P
                    for f in range(KC):
                        i = KC * b + f
                        t = rho[i % 2][:, 0:w]
                        e.wait_ge(s_xf, 5 * i + 1)
                        e.activation(t, t, ACT.Exp).then_inc(s_rho, 1)
                        e.wait_ge(s_rho, 4 * i + 1)
                        e.activation(t, t, ACT.Square, bias=SQ, scale=SQ).then_inc(s_rho, 1)
                        e.wait_ge(s_rho, 4 * i + 2)
                        e.activation(t, t, ACT.Ln, bias=0.5, scale=0.5 / (SQ * SQ)).then_inc(s_rho, 1)
                        e.wait_ge(s_rho, 4 * i + 3)
                        e.activation(t, t, ACT.Exp, scale=-1.0).then_inc(s_rho, 1)

                def h2(b):
                    e.wait_ge(s_nm, b + 1)
                    for i, c in enumerate(BLK[b]):
                        e.activation(xb[:, i, :], x1[:, c, :], ACT.Relu, bias=nmr[:, i:i + 1], scale=rstd[:, i:i + 1])\
                         .then_inc(s_h2, 1)
                    for c in BLK[b]:
                        e.wait_ge(s_t2, c + 1)
                        if c >= 2:
                            e.wait_ge(s_S, c - 1)
                        e.activation(h2T[c % 2][:], pt[c % 2][:, :].rearrange("p (k n) -> p k n", k=KC), ACT.Copy)\
                         .then_inc(s_e2, 1)

                for b in range(NB):
                    evac_agg(b)
                    chain(b)
                    stats_chain(2 * b)
                    stats_chain(2 * b + 1)
                    h2(b)

            @blk.vector
            def _(e):
                s_v = sem("n_v")
                cnt = [0]

                def link(ins):
                    cnt[0] += 1
                    ins.then_inc(s_v, 1)
                    e.wait_ge(s_v, cnt[0])

                def split(i, hi, lo, sign):
                    e.wait_ge(q_w[i], 16)
                    if sign < 0:
                        link(e.tensor_scalar(raw[:], raw[:], -1.0, None, ALU.mult))
                    link(e.tensor_copy(hi, raw[:]))
                    e.tensor_tensor(lo, raw[:], hi, ALU.subtract).then_inc(s_raw, 1)

                def lo_agg(b):
                    for i, c in enumerate(BLK[b]):
                        e.wait_ge(s_ah, c + 1)
                        e.tensor_tensor(aTl[:, :, i * P:(i + 1) * P], pt[c % 2][:, :].rearrange("p (k n) -> p k n", k=KC),
                                        aTh[:, :, i * P:(i + 1) * P], ALU.subtract).then_inc(s_al, 1)

                def units(b):
                    w = len(BLK[b]) * P

                    def load_x(i):
                        e.wait_ge(s_u, i + 1)
                        f = i % KC
                        e.tensor_scalar(rho[i % 2][:, 0:w], pu[i % 2][:, 0:w], b3c[:, f:f + 1], XMAX, ALU.add, ALU.min)\
                         .then_inc(s_xf, 1)
                        e.tensor_scalar(xf[i % 2][:, 0:w], pu[i % 2][:, 0:w], b3c[:, f:f + 1], None, ALU.add)\
                         .then_inc(s_xf, 1)

                    for f in range(KC):
                        i = KC * b + f
                        t = um[i % 2][:, 0:w]
                        load_x(i)
                        e.wait_ge(s_xf, 5 * i + 2)
                        e.wait_ge(s_rho, 4 * i + 4)
                        e.scalar_tensor_tensor(t, rho[i % 2][:, 0:w], 1.0, xf[i % 2][:, 0:w], ALU.subtract, ALU.mult)\
                         .then_inc(s_xf, 1)
                        e.wait_ge(s_xf, 5 * i + 3)
                        if f == 0 and b:
                            e.wait_ge(s_o, first(b))
                        e.tensor_copy(uTh[:, f, 0:w], t).then_inc(s_xf, 1)
                        e.wait_ge(s_xf, 5 * i + 4)
                        e.tensor_tensor(uTl[:, f, 0:w], t, uTh[:, f, 0:w], ALU.subtract).then_inc(s_xf, 1)

                def norm(i, n):
                    for j in range(n):
                        (link if j == n - 1 else lambda ins: None)(e.bn_aggr(mv[:, j, :], stats[:, j, :]))
                    e.tensor_scalar(var[:, 0:n], mv[:, 0:n, 1], LN_EPS, None, ALU.add).then_inc(s_var, 1)
                    e.wait_ge(s_r, 2 * i + 2)
                    newton(e, link, var[:, 0:n], rstd[:, 0:n], tmp[:, 0:n])

                def residual(b):
                    n, c0 = len(BLK[b]), first(b)
                    for j, c in enumerate(BLK[b]):
                        e.wait_ge(s_o, c + 1)
                        e.wait_ge(s_hb, 2 * (c + 1))
                        e.tensor_tensor(x1[:, c, :], po[c % 2][:, :], hb[:, j, :], ALU.add).then_inc(s_ln, 1)
                        e.wait_ge(s_ln, c + 1)
                        (link if j == n - 1 else lambda ins: None)(e.bn_stats(stats[:, j, :], x1[:, c, :]))
                    norm(2 * b, n)
                    for j, c in enumerate(BLK[b]):
                        link(e.scalar_tensor_tensor(x1[:, c, :], x1[:, c, :], mv[:, j, 0:1], gab[:], ALU.subtract, ALU.mult))
                    for j, c in enumerate(BLK[b]):
                        r = NTAIL if c == NCH - 1 else P
                        link(e.scalar_tensor_tensor(x1[0:r, c, :], x1[0:r, c, :], rstd[0:r, j:j + 1], xb[0:r, j, :],
                                                    ALU.mult, ALU.add))
                        (link if j == n - 1 else lambda ins: None)(e.bn_stats(stats[:, j, :], x1[:, c, :]))
                    norm(2 * b + 1, n)
                    e.scalar_tensor_tensor(nmr[:, 0:n], mv[:, 0:n, 0], -1.0, rstd[:, 0:n], ALU.mult, ALU.mult)\
                     .then_inc(s_nm, 1)

                def store_S(b):
                    for c in BLK[b]:
                        i = c % 2
                        e.wait_ge(s_S, c + 1)
                        if c >= 2:
                            e.wait_ge(q_S[i], 32 * (c // 2))
                        e.tensor_tensor(Ss[i][:], psS[i][:, 0:R], svb[:], ALU.mult).then_inc(s_Sv, 1)
                        e.wait_ge(s_Sv, 3 * c + 1)
                        e.tensor_copy(Sh[i][:], Ss[i][:]).then_inc(s_Sv, 1)
                        e.wait_ge(s_Sv, 3 * c + 2)
                        e.tensor_tensor(Sl[i][:], Ss[i][:], Sh[i][:], ALU.subtract).then_inc(s_Sv, 1)

                split(0, W3h[:, 0:KC, :], W3l[:, 0:KC, :], 1)
                split(1, W3h[:, KC:2 * KC, :], W3l[:, KC:2 * KC, :], -1)
                split(2, W4h[:], W4l[:], -1)
                e.wait_ge(q_c, 6 * 16)
                for b in range(NB):
                    lo_agg(b)
                    units(b)
                    residual(b)
                    store_S(b)

            @blk.tensor
            def _(e):
                def agg_T(b):
                    e.wait_ge(q_ag[b], 16)
                    for i, c in enumerate(BLK[b]):
                        if c >= 2:
                            e.wait_ge(s_al, c - 1)
                        if i == 0 and b:
                            e.wait_ge(s_e2, first(b))
                        for f in range(KC):
                            last = e.transpose(pt[c % 2][:, f * P:(f + 1) * P], ag[:, i, f * P:(f + 1) * P], ident[:])
                        last.then_inc(s_tr, 1)

                def u_units(b):
                    n0, w = first(b) * P, len(BLK[b]) * P
                    if b == 0:
                        e.wait_ge(s_raw, 2)
                    for f in range(KC):
                        i = KC * b + f
                        if i >= 2:
                            e.wait_ge(s_xf, 5 * (i - 2) + 2)
                        m = 0
                        for c in range(2 * KC):
                            if f == 0 and c == KC:
                                e.wait_ge(s_al, BLK[b][-1] + 1)
                            ah, al = ((nTh[:, c, n0:n0 + w], nTl[:, c, n0:n0 + w]) if c < KC else
                                      (aTh[:, c - KC, 0:w], aTl[:, c - KC, 0:w]))
                            for wt, a in ((W3h, ah), (W3h, al), (W3l, ah)):
                                last = e.matmul(pu[i % 2][:, 0:w], wt[:, c, f * P:(f + 1) * P], a,
                                                start=m == 0, stop=m == 6 * KC - 1)
                                m += 1
                        last.then_inc(s_u, 1)

                def out_chunks(b):
                    if b == 0:
                        e.wait_ge(s_raw, 3)
                    for i, c in enumerate(BLK[b]):
                        if c >= 2:
                            e.wait_ge(s_ln, c - 1)
                        m = 0
                        for f in range(KC):
                            if i == 0:
                                e.wait_ge(s_xf, 5 * (KC * b + f) + 5)
                            for a, w in ((uTh, W4h), (uTl, W4h), (uTh, W4l)):
                                last = e.matmul(po[c % 2][:, :], a[:, f, i * P:(i + 1) * P], w[:, f, :],
                                                start=m == 0, stop=m == 3 * KC - 1)
                                m += 1
                        last.then_inc(s_o, 1)

                def S_chunks(b):
                    for i, c in enumerate(BLK[b]):
                        e.wait_ge(s_h2, c + 1)
                        if i == 0:
                            e.wait_ge(s_al, BLK[b][-1] + 1)
                        if c >= 2:
                            e.wait_ge(s_e2, c - 1)
                        for f in range(KC):
                            last = e.transpose(pt[c % 2][:, f * P:(f + 1) * P], xb[:, i, f * P:(f + 1) * P], ident[:])
                        last.then_inc(s_t2, 1)
                        if c >= 2:
                            e.wait_ge(s_Sv, 3 * (c - 2) + 1)
                        e.wait_ge(s_e2, c + 1)
                        for f in range(KC):
                            last = e.matmul(psS[c % 2][:, 0:R], h2T[c % 2][:, f, :], Us[:, f, :], start=f == 0, stop=f == KC - 1)
                        last.then_inc(s_S, 1)

                e.wait_ge(q_c, 6 * 16)
                for b in range(NB):
                    agg_T(b)
                    u_units(b)
                    out_chunks(b)
                    S_chunks(b)


def conv_phase(nc, scope, sem, k):
    iota_p, base_b, base_i, x1, row_bcast = (k[n] for n in ("iota_p", "base_b", "base_i", "x1", "row_bcast"))
    Sh_d, Sl_d, dst_rows, src_cols, ew_cols, Vt, bias, out = (
        k[n] for n in ("Sh_d", "Sl_d", "dst_rows", "src_cols", "ew_cols", "Vt", "bias", "out"))
    NBUF = 4
    st, sb, ps = scope()
    with st:
        iota_ni = sb("iota_ni", [P, NP], I32)
        iota_n = sb("iota_n", [P, NP])
        scoli = sb("scoli", [P, NG * SUB], I32)
        scol = sb("scol", [P, NG * SUB])
        ewc = sb("ewc", [P, NG * SUB])
        VV = sb("VV", [P, H])
        bib = sb("bib", [P, H])
        db = [sb(f"c_db{i}", [64, G], I32) for i in range(2)]
        oT = [sb(f"c_oT{i}", [64, G], F32R) for i in range(2)]
        Sw = [sb(f"c_Sw{i}", [64, R], F32R) for i in range(2)]
        gw = [sb(f"c_gw{i}", [P, SUB, R]) for i in range(2)]
        ghl = [sb(f"c_ghl{i}", [P, SUB, 2 * R], F32R) for i in range(2)]
        so = [sb(f"c_so{i}", [P, N], F32R) for i in range(NBUF)]
        sums = sb("sums", [P, NP])
        res = [sb(f"res{i}", [P, H]) for i in range(2)]
        pg = [ps(f"pg{i}") for i in range(2)]
        pc = [ps(f"pc{i}") for i in range(3)]
        pf = [ps(f"pf{i}") for i in range(2)]

        q_k = sem("k_k")
        q_in = [sem(f"k_in{i}") for i in range(2)]
        q_w = [sem(f"k_w{i}") for i in range(2)]
        q_o = [sem(f"k_o{i}") for i in range(2)]
        s_c = sem("k_c")
        s_oT = sem("k_oT")
        s_g = sem("k_g")
        s_gw = sem("k_gw")
        s_so = sem("k_so")
        s_sc = sem("k_sc")
        s_sum = sem("k_sum")
        s_f = sem("k_f")
        s_r = sem("k_r")

        def tail(u):
            return u.reg is None and u.const >= 4 * FULL

        def wait(e, s, val):
            if not (isinstance(val, int) and val < 1):
                e.wait_ge(s, val)

        def groups(e, step):
            step(At(None, 0))
            step(At(None, 4))
            with e.Fori(1, FULL // 2) as i:
                step(At(i, 0))
                step(At(i, 4))
            step(At(None, 4 * FULL))

        with nc.Block() as blk:
            @blk.sync
            def _(e):
                e.dma_start(scoli[:], src_cols).then_inc(q_k, 16)
                e.dma_start(ewc[:], ew_cols).then_inc(q_k, 16)
                for a, b in HALF:
                    e.dma_start(VV[a:b, :], Vt).then_inc(q_k, 16)
                e.dma_start(bib[:], row_bcast(bias, H, P)).then_inc(q_k, 16)

                def loads(u):
                    p, n = u.par, ETAIL if tail(u) else G
                    wait(e, s_oT, u.group(1, -1))
                    e.dma_start(db[p][:, 0:n], dst_rows[bass.ds(u.group(), 1), 0:n].to_broadcast([64, n]))\
                     .then_inc(q_in[p], 16)
                    b = e.value_load(base_i[0:1, bass.ds(u.group(), 1)], min_val=0, max_val=NP - WIN)
                    wait(e, s_g, u.group(1, -1))
                    e.dma_start(Sw[p][0:32, :].bitcast(F32), Sh_d[bass.ds(b, WIN), :]).then_inc(q_w[p], 16)
                    e.dma_start(Sw[p][32:64, :].bitcast(F32), Sl_d[bass.ds(b, WIN), :]).then_inc(q_w[p], 16)

                groups(e, loads)
                for c in range(NCH):
                    r = min(P, N - c * P)
                    e.wait_ge(s_r, 3 * c + 3)
                    e.dma_start(out[c * P:c * P + r, :], res[c % 2][0:r, :]).then_inc(q_o[c % 2], 16)
                for i in range(2):
                    e.wait_ge(q_o[i], 16 * (NCH // 2))

            @blk.gpsimd
            def _(e):
                e.iota(iota_ni[:], pattern=[[1, NP]], base=0, channel_multiplier=0).then_inc(s_c, 1)

            @blk.scalar
            def _(e):
                e.wait_ge(s_sc, 4 * FULL + 1)
                e.activation(sums[:, 0:512], pc[0][:, :], ACT.Copy).then_inc(s_sum, 1)

            @blk.vector
            def _(e):
                e.wait_ge(s_c, 1)
                e.tensor_copy(iota_n[:], iota_ni[:]).then_inc(s_c, 1)
                e.wait_ge(q_k, 5 * 16)
                e.tensor_copy(scol[:], scoli[:]).then_inc(s_c, 1)
                e.wait_ge(s_c, 3)

                def oneT(u):
                    p, n = u.par, ETAIL if tail(u) else G
                    e.wait_ge(q_in[p], u.pair(16, 16))
                    wait(e, s_g, u.group(1, -1))
                    e.tensor_scalar(oT[p][:, 0:n], db[p][:, 0:n], base_b[0:64, bass.ds(u.group(), 1), 0], iota_p[0:64, :],
                                    ALU.subtract, ALU.is_equal).then_inc(s_oT, 1)

                def step(u):
                    p, last = u.par, tail(u)
                    for j in range(1 if last else SUB):
                        r = ETAIL if last else P
                        if j == 1 or last:
                            weigh(u)
                        wait(e, s_sc, u.val(1, j + 1 - NBUF))
                        e.tensor_scalar(so[j][0:r, :], iota_n[0:r, 0:N], scol[0:r, bass.ds(u.val(1, j), 1)], None,
                                        ALU.is_equal).then_inc(s_so, 1)
                    if not last:
                        oneT(u + 4)

                def weigh(u):
                    p, n, r = u.par, 1 if tail(u) else SUB, ETAIL if tail(u) else P
                    e.wait_ge(s_g, u.group(1, 1))
                    w = ewc[0:r, bass.ds(u.val(), n)].rearrange("p (s a) -> p s a", a=1).to_broadcast([r, n, R])
                    e.tensor_tensor(gw[p][0:r, 0:n, :], pg[p][0:r, 0:n * R].rearrange("p (s a) -> p s a", s=n), w, ALU.mult)\
                     .then_inc(s_gw, 1)
                    e.wait_ge(s_gw, u.group(3, 1))
                    wait(e, s_sc, u.val(1, -4))
                    e.tensor_copy(ghl[p][0:r, 0:n, 0:R], gw[p][0:r, 0:n, :]).then_inc(s_gw, 1)
                    e.wait_ge(s_gw, u.group(3, 2))
                    e.tensor_tensor(ghl[p][0:r, 0:n, R:2 * R], gw[p][0:r, 0:n, :], ghl[p][0:r, 0:n, 0:R], ALU.subtract)\
                     .then_inc(s_gw, 1)

                oneT(At(None, 0))
                groups(e, step)
                e.wait_ge(s_sc, 4 * FULL + 1)
                e.tensor_copy(sums[:, 512:1024], pc[1][:, :]).then_inc(s_sum, 1)
                e.tensor_copy(sums[:, 1024:N], pc[2][:, 0:N - 1024]).then_inc(s_sum, 1)
                for c in range(NCH):
                    r, t = min(P, N - c * P), res[c % 2]
                    e.wait_ge(s_f, c + 1)
                    if c >= 2:
                        e.wait_ge(q_o[c % 2], 16 * (c // 2))
                    e.tensor_tensor(t[0:r, :], pf[c % 2][0:r, :], bib[0:r, :], ALU.add).then_inc(s_r, 1)
                    e.wait_ge(s_r, 3 * c + 1)
                    e.scalar_tensor_tensor(t[0:r, :], t[0:r, :], 0.0, x1[0:r, c, :], ALU.max, ALU.add).then_inc(s_r, 2)

            @blk.tensor
            def _(e):
                def rows_of(u):
                    p, n, r = u.par, 1 if tail(u) else SUB, ETAIL if tail(u) else P
                    e.wait_ge(q_w[p], u.pair(32, 32))
                    e.wait_ge(s_oT, u.group(1, 1))
                    wait(e, s_gw, u.group(3, 1 - 6))
                    for j in range(n):
                        m = e.matmul(pg[p][0:r, j * R:(j + 1) * R], oT[p][:, j * P:j * P + r], Sw[p][:], start=j == 0,
                                     stop=j == n - 1, skip_group_check=True)
                    m.then_inc(s_g, 1)

                def scatter(u):
                    p, last = u.par, tail(u)
                    r = ETAIL if last else P
                    for j in range(1 if last else SUB):
                        if j == 0:
                            e.wait_ge(s_gw, u.group(3, 3))
                        e.wait_ge(s_so, u.val(1, j + 1))
                        first = u.reg is None and u.const + j == 0
                        for i, (c0, w) in enumerate(SBLK):
                            m = e.matmul(pc[i][:, 0:w], ghl[p][0:r, j, :], so[j][0:r, c0:c0 + w], start=first, stop=last,
                                         skip_group_check=True)
                        m.then_inc(s_sc, 1)

                def step(u):
                    if not tail(u):
                        rows_of(u + 4)
                    scatter(u)

                rows_of(At(None, 0))
                groups(e, step)
                e.wait_ge(s_sum, 3)
                for c in range(NCH):
                    r = min(P, N - c * P)
                    if c >= 2:
                        e.wait_ge(s_r, 3 * (c - 2) + 1)
                    e.matmul(pf[c % 2][0:r, :], sums[:, c * P:c * P + r], VV[:], start=True, stop=True).then_inc(s_f, 1)


def kernel(x, src, dst, edge_attr_64, edge_weight, L0_gnn_W1, L0_gnn_b1, L0_gnn_W2, L0_gnn_b2, L0_gnn_W3,
           L0_gnn_b3, L0_gnn_W4, L0_gnn_b4, L0_gnn_gamma, L0_gnn_beta, L1_gnn_U, L1_gnn_s, L1_gnn_Vt, L1_gnn_bias):
    import numpy as np
    import concourse.bacc as bacc
    from concourse.bass_utils import run_bass_kernel_spmd

    def groups(a):
        a = np.asarray(a)
        return np.concatenate([a, np.repeat(a[-1:], NG * G - E)]).reshape(NG, SUB, P)

    w = np.asarray(edge_weight)
    arrays = {
        "x": x,
        "src_idx": groups(src).transpose(0, 2, 1),
        "dst_rows": groups(dst).reshape(NG, G),
        "src_cols": groups(src).reshape(NG * SUB, P).T,
        "dst_cols": groups(dst).reshape(NG * SUB, P).T,
        "eaT": np.asarray(edge_attr_64).T,
        "ew_cols": groups(w).reshape(NG * SUB, P).T,
        "W1": L0_gnn_W1, "b1": L0_gnn_b1, "W2": L0_gnn_W2, "b2": L0_gnn_b2, "W3": L0_gnn_W3, "b3": L0_gnn_b3,
        "W4": L0_gnn_W4, "b4": L0_gnn_b4, "gamma": L0_gnn_gamma, "beta": L0_gnn_beta,
        "U": L1_gnn_U, "sv": L1_gnn_s, "Vt": L1_gnn_Vt, "bias": L1_gnn_bias,
    }
    arrays = {n: np.ascontiguousarray(a) for n, a in arrays.items()}
    nc = bacc.Bacc("TRN2", target_bir_lowering=False, num_devices=1)
    args = {n: nc.dram_tensor(f"in_{n}", a.shape, mybir.dt.from_np(a.dtype), kind="ExternalInput").ap()
            for n, a in arrays.items()}
    out = nc.dram_tensor("out_0", (N, H), F32, kind="ExternalOutput").ap()
    gnn_two_layers(nc, out=out, **args)
    r = run_bass_kernel_spmd(nc, [{f"in_{n}": a for n, a in arrays.items()}], core_ids=[0])
    return r.results[0]["out_0"]
```

```python
import concourse.bass as bass
from concourse import mybir
from concourse.alu_op_type import AluOpType as ALU
from contextlib import ExitStack

F32 = mybir.dt.float32
F32R = mybir.dt.float32r
I32 = mybir.dt.int32
ACT = mybir.ActivationFunctionType
AX = mybir.AxisListType

P = 128
H = 512
KC = H // P
N = 1250
NCH = -(-N // P)
NP = NCH * P
NTAIL = N - (NCH - 1) * P
E = 40000
SUB = 4
G = SUB * P
NG = -(-E // G)
FULL = E // G
ETAIL = E - FULL * G
ED = 64
R = 64
WIN = 32
LN_EPS = 1e-5
XMAX = 20.0
SQ = 2.0 ** 32
LNSQ = 32 * 0.6931471805599453
HALF = [(0, 64), (64, 128)]
NBLK = [(0, 512), (512, 512), (1024, 256)]
NPAIR = N // 2 + 1
SBLK = [(0, 314), (314, NPAIR - 314)]


class At:

    def __init__(self, reg, const):
        self.reg, self.const = reg, const

    def __add__(self, n):
        return At(self.reg, self.const + n)

    def val(self, mult=1, add=0):
        c = self.const * mult + add
        return c if self.reg is None else self.reg * (2 * SUB * mult) + c

    def group(self, mult=1, add=0):
        c = self.const // SUB * mult + add
        return c if self.reg is None else self.reg * (2 * mult) + c

    def pair(self, mult, add=0):
        c = self.const // (2 * SUB) * mult + add
        return c if self.reg is None else self.reg * mult + c

    @property
    def j(self):
        return self.const % SUB

    @property
    def par(self):
        return self.const // SUB % 2

    def has(self, n):
        return self.reg is not None or 0 <= self.const < n


def slots(eng, first, head, tail, last, step):
    for s in range(first, head):
        step(At(None, s))
    with eng.Fori(head // (2 * SUB), tail // (2 * SUB)) as i:
        for k in range(2 * SUB):
            step(At(i, k))
    for s in range(tail, last):
        step(At(None, s))


class Work:

    def __init__(self):
        self.of = {}

    def on(self, engine):
        def keep(program):
            self.of[engine] = program
        return keep


def phase(nc, wide_i, narrow, general):
    def both(engine, e):
        span = e.value_load(wide_i[0:1, 0:1], min_val=0, max_val=NP)
        with e.If(span < WIN):
            narrow.of[engine](e)
        with e.Else():
            general.of[engine](e)

    with nc.Block() as blk:
        @blk.sync
        def _(e):
            both("sync", e)

        @blk.gpsimd
        def _(e):
            both("gpsimd", e)

        @blk.scalar
        def _(e):
            both("scalar", e)

        @blk.vector
        def _(e):
            both("vector", e)

        @blk.tensor
        def _(e):
            both("tensor", e)


class Chain:

    def __init__(self, s, s_gather, s_go):
        self.s, self.s_gather, self.s_go = s, s_gather, s_go
        self.n = self.g = 0

    def run(self, engine, e, steps, t=0):
        total_n = sum(by for who, by, _ in steps if who != "gather")
        total_g = sum(by for who, by, _ in steps if who == "gather")
        n, g, after_gather = self.n, self.g, False
        for who, by, step in steps:
            gather = who == "gather"
            if who == engine or (gather and engine == "gpsimd"):
                if after_gather:
                    e.wait_ge(self.s_gather, t * total_g + g)
                elif not (isinstance(t, int) and t * total_n + n == 0):
                    e.wait_ge(self.s, t * total_n + n)
                if gather:
                    e.sem_inc(self.s_go, 1)
                step(e, self.s_gather if gather else self.s)
            if gather:
                g += by
            else:
                n += by
            after_gather = gather

    def done(self, steps, times=1):
        self.n += times * sum(by for who, by, _ in steps if who != "gather")
        self.g += times * sum(by for who, by, _ in steps if who == "gather")


class Line:

    def __init__(self, sem):
        self.sem, self.n = sem, 0

    def inc(self, ins, by=1):
        ins.then_inc(self.sem, by)
        self.n += by
        return self.n


def gnn_two_layers(nc, x, src_idx, dst_rows, src_cols, dst_cols, eaT, ew_cols, W1, b1, W2, b2, W3, b3, W4, b4,
                   gamma, beta, U, sv, Vt, bias, out):
    ctx = ExitStack()
    names = set()

    def sem(name):
        assert name not in names
        names.add(name)
        return ctx.enter_context(nc.semaphore(name))

    def scope():
        st = ExitStack()
        return (st, lambda n, s, d=F32: st.enter_context(nc.sbuf_tensor(n, s, d)),
                lambda n, s=(P, 512): st.enter_context(nc.psum_tensor(n, list(s), F32)))

    def dram(name, shape, dt=F32):
        return nc.dram_tensor(name, shape, dt, kind="Internal").ap()

    def row_bcast(ap, n, parts):
        return ap.rearrange("(a n) -> a n", a=1).to_broadcast([parts, n])

    A_d = dram("A_tab", (NP, H))
    Bh_d = dram("Bh_tab", (NP, H))
    Bl_d = dram("Bl_tab", (NP, H))
    h_d = dram("h_tab", (NP, H))
    agg_d = dram("agg_tab", (NP, H))
    Sh_d = dram("Sh_tab", (NP, R))
    Sl_d = dram("Sl_tab", (NP, R))
    win_d = dram("win_tab", (NG, 2))

    with ctx:
        pst, sb, _ = scope()
        ctx.enter_context(pst)
        ident = sb("ident", [P, P])
        iota_w = sb("iota_w", [P, WIN])
        iota_p = sb("iota_p", [P, 1])
        base_b = sb("base_b", [P, NG, 2])
        base_i = sb("base_i", [1, NG], I32)
        wide_i = sb("wide_i", [1, 1], I32)
        dcol = sb("dcol", [P, NG * SUB])
        nTh = sb("nTh", [P, KC, NP], F32R)
        nTl = sb("nTl", [P, KC, NP], F32R)
        est, sb, _ = scope()
        W2h = sb("W2h", [P, KC, H], F32R)
        W2l = sb("W2l", [P, KC, H], F32R)
        b2r = sb("b2r", [64, H], F32R)
        ones = sb("ones", [64, P], F32R)
        eaW2 = sb("eaW2", [P, H], F32R)
        eaW1 = [sb(f"eaW1_{i}", [P, H], F32R) for i in range(2)]

        def newton(e, link, var, r, t):
            link(e.tensor_tensor(t, r, r, ALU.mult))
            link(e.tensor_tensor(t, t, var, ALU.mult))
            link(e.tensor_scalar(t, t, -0.5, 1.5, ALU.mult, ALU.add))
            link(e.tensor_tensor(r, r, t, ALU.mult))

        st, sb1, ps1 = scope()
        with st:
            xs = sb1("xs", [P, NCH, H])
            hs = sb1("hs", [P, NCH, H])
            w1raw = sb1("w1raw", [P, 2 * KC, H])
            w1h = sb1("w1h", [P, 2 * KC, H], F32R)
            w1l = sb1("w1l", [P, 2 * KC, H], F32R)
            w2raw = sb1("w2raw", [P, KC, H])
            wcraw = sb1("wcraw", [P, H])
            b1b = sb1("b1b", [P, H])
            b2raw = sb1("b2raw", [64, H])
            dsti = sb1("dsti", [NG, G], I32)
            dcoli = sb1("dcoli", [P, NG * SUB], I32)
            win = sb1("win", [NG, 2])
            mx = sb1("mx", [NG, 1])
            iota_i = sb1("iota_i", [P, WIN], I32)
            iop_i = sb1("iop_i", [P, 1], I32)
            stats = sb1("stats", [P, NCH, 6])
            mv = sb1("mv", [P, NCH, 2])
            var = sb1("var", [P, NCH])
            lnv = sb1("lnv", [P, NCH])
            rstd = sb1("rstd", [P, NCH])
            nmr = sb1("nmr", [P, NCH])
            tmp = sb1("tmp", [P, NCH])
            ta = [sb1(f"ta{i}", [P, H]) for i in range(2)]
            tb = [sb1(f"tb{i}", [P, H]) for i in range(2)]
            tbh = [sb1(f"tbh{i}", [P, H], F32R) for i in range(2)]
            tbl = [sb1(f"tbl{i}", [P, H], F32R) for i in range(2)]
            zero = sb1("zero", [P, NCH * H // 2])
            pT = [ps1(f"pT{i}") for i in range(2)]
            pA = [ps1(f"pA{i}") for i in range(2)]
            pB = [ps1(f"pB{i}") for i in range(2)]

            q_x = [sem(f"q_x{i}") for i in range(3)]
            q_dst = sem("q_dst")
            q_w1 = sem("q_w1")
            q_w2 = sem("q_w2")
            q_win = sem("q_win")
            q_winb = sem("q_winb")
            q_st = [sem(f"q_st{i}") for i in range(2)]
            q_h = sem("q_h")
            c_g = Line(sem("c_g"))
            c_v = Line(sem("c_v"))
            c_a = sem("c_a")
            c_hT = sem("c_hT")
            c_tr = sem("c_tr")
            c_hi = sem("c_hi")
            c_lo = sem("c_lo")
            c_A = sem("c_A")
            c_B = sem("c_B")
            c_ta = sem("c_ta")
            c_tb = sem("c_tb")
            c_pad = sem("c_pad")
            c_bz = sem("c_bz")
            v = {}

            with nc.Block() as blk:
                def store_b(e, c):
                    i = c % 2
                    e.wait_ge(c_B, c + 1)
                    if c >= 2:
                        e.wait_ge(q_st[i], 48 * (c // 2))
                    e.tensor_tensor(tb[i][:], pB[i][:, :], b1b[:], ALU.add).then_inc(c_tb, 1)
                    e.wait_ge(c_tb, 3 * c + 1)
                    e.tensor_copy(tbh[i][:], tb[i][:]).then_inc(c_tb, 1)
                    e.wait_ge(c_tb, 3 * c + 2)
                    e.tensor_tensor(tbl[i][:], tb[i][:], tbh[i][:], ALU.subtract).then_inc(c_tb, 1)

                def evac(e, c):
                    i = c % 2
                    e.wait_ge(c_tr, c + 1)
                    e.activation(nTh[:, :, c * P:(c + 1) * P], pT[i][:, :].rearrange("p (k n) -> p k n", k=KC),
                                 ACT.Copy).then_inc(c_hi, 1)
                    if c >= 1:
                        store_a(e, c - 1)

                def store_a(e, c):
                    i = c % 2
                    e.wait_ge(c_A, c + 1)
                    if c >= 2:
                        e.wait_ge(q_st[i], 48 * (c // 2))
                    e.activation(ta[i][:], pA[i][:, :], ACT.Copy).then_inc(c_ta, 1)

                @blk.vector
                def _(e):
                    def link(ins):
                        c_v.inc(ins)
                        e.wait_ge(c_v.sem, c_v.n)

                    c_pad_i = e.memset(xs[:, NCH - 1, :], 0.0)
                    c_pad_i.then_inc(c_pad, 1)
                    c_v.inc(e.memset(zero[:], 0.0))
                    v["zero"] = c_v.n
                    e.memset(b2raw[:], 0.0).then_inc(c_bz, 1)
                    e.wait_ge(q_dst, 32)
                    c_v.inc(e.tensor_reduce(win[:, 0:1], dsti[:, :], AX.X, ALU.min))
                    link(e.tensor_reduce(mx[:], dsti[:, :], AX.X, ALU.max))
                    link(e.tensor_scalar(win[:, 0:1], win[:, 0:1], float(NP - WIN), None, ALU.min))
                    link(e.tensor_tensor(win[:, 1:2], mx[:], win[:, 0:1], ALU.subtract))
                    v["win"] = c_v.n
                    c_v.inc(e.tensor_copy(dcol[:], dcoli[:]))
                    e.wait_ge(c_g.sem, 3)
                    c_v.inc(e.tensor_copy(iota_w[:], iota_i[:]))
                    c_v.inc(e.tensor_scalar(iop_i[:], iop_i[:], WIN - 1, None, ALU.bitwise_and))
                    e.wait_ge(c_v.sem, c_v.n)
                    c_v.inc(e.tensor_copy(iota_p[:], iop_i[:]))
                    for c in range(NCH):
                        if c in (0, 1, 5):
                            e.wait_ge(q_x[(0, 1, 5).index(c)], (16, 16, 32)[(0, 1, 5).index(c)])
                        c_v.inc(e.bn_stats(stats[:, c, :], xs[:, c, :]))
                    e.wait_ge(c_v.sem, c_v.n)
                    for c in range(NCH):
                        c_v.inc(e.bn_aggr(mv[:, c, :], stats[:, c, :]))
                    e.wait_ge(c_v.sem, c_v.n)
                    link(e.tensor_scalar(var[:], mv[:, :, 1], LN_EPS, None, ALU.add))
                    v["var"] = c_v.n
                    e.wait_ge(c_a, 2)
                    newton(e, link, var[:], rstd[:], tmp[:])
                    link(e.scalar_tensor_tensor(nmr[:], mv[:, :, 0], -1.0, rstd[:], ALU.mult, ALU.mult))
                    v["rstd"] = c_v.n
                    e.wait_ge(q_w1, 16)
                    link(e.tensor_copy(w1h[:], w1raw[:]))
                    link(e.tensor_tensor(w1l[:], w1raw[:], w1h[:], ALU.subtract))
                    v["w1"] = c_v.n
                    e.wait_ge(q_w2, 6 * 16)
                    e.wait_ge(c_g.sem, 5)
                    link(e.tensor_scalar(w2raw[:], w2raw[:], -1.0, None, ALU.mult))
                    c_v.inc(e.tensor_copy(W2h[:], w2raw[:]))
                    c_v.inc(e.tensor_copy(eaW2[:], wcraw[:]))
                    for i in range(2):
                        c_v.inc(e.tensor_copy(eaW1[i][64:128, :], wcraw[64:128, :]))
                    c_v.inc(e.tensor_copy(b2r[:], b2raw[:]))
                    e.wait_ge(c_v.sem, c_v.n)
                    c_v.inc(e.tensor_tensor(W2l[:], w2raw[:], W2h[:], ALU.subtract))
                    c_v.inc(e.tensor_tensor(eaW2[64:128, :], wcraw[64:128, :], eaW2[64:128, :], ALU.subtract))
                    link(e.tensor_tensor(b2r[32:64, :], b2raw[32:64, :], b2r[32:64, :], ALU.subtract))
                    v["w2"] = c_v.n
                    e.wait_ge(q_winb, 16)
                    c_v.inc(e.tensor_copy(base_i[0:1, :], base_b[0:1, :, 0]))
                    c_v.inc(e.tensor_reduce(wide_i[0:1, :], base_b[0:1, :, 1], AX.X, ALU.max))
                    for c in range(NCH):
                        i = c % 2
                        e.wait_ge(c_hi, c + 1)
                        e.tensor_tensor(nTl[:, :, c * P:(c + 1) * P], pT[i][:, :].rearrange("p (k n) -> p k n", k=KC),
                                        nTh[:, :, c * P:(c + 1) * P], ALU.subtract).then_inc(c_lo, 1)
                        if c >= 1:
                            store_b(e, c - 1)
                    store_b(e, NCH - 1)

                @blk.gpsimd
                def _(e):
                    c_g.inc(e.memset(ident[:], 0.0))
                    c_g.inc(e.iota(iota_i[:], pattern=[[1, WIN]], base=0, channel_multiplier=0))
                    c_g.inc(e.iota(iop_i[:], pattern=[[0, 1]], base=0, channel_multiplier=1))
                    e.wait_ge(c_g.sem, 1)
                    c_g.inc(e.affine_select(out=ident[:], in_=ident[:], compare_op=ALU.not_equal, fill=1.0,
                                            base=0, pattern=[[-1, P]], channel_multiplier=1))
                    c_g.inc(e.memset(ones[:].bitcast(F32), 1.0))

                @blk.scalar
                def _(e):
                    e.preload_act_table_set("natural_log_exp_and_others")
                    e.wait_ge(c_v.sem, v["var"])
                    e.activation(lnv[:], var[:], ACT.Ln).then_inc(c_a, 1)
                    e.wait_ge(c_a, 1)
                    e.activation(rstd[:], lnv[:], ACT.Exp, scale=-0.5).then_inc(c_a, 1)
                    e.wait_ge(c_v.sem, v["rstd"])
                    for c in range(NCH):
                        e.activation(hs[:, c, :], xs[:, c, :], ACT.Relu, bias=nmr[:, c:c + 1],
                                     scale=rstd[:, c:c + 1]).then_inc(c_hT, 1)
                        if c >= 1:
                            evac(e, c - 1)
                    evac(e, NCH - 1)
                    store_a(e, NCH - 1)

                @blk.tensor
                def _(e):
                    e.wait_ge(c_g.sem, 4)

                    def tables(c):
                        i = c % 2
                        if c == 0:
                            e.wait_ge(c_v.sem, v["w1"])
                        e.wait_ge(c_lo, c + 1)
                        if c >= 2:
                            e.wait_ge(c_ta, c - 1)
                            e.wait_ge(c_tb, 3 * (c - 2) + 1)
                        for half, bank, done in ((0, pA[i], c_A), (1, pB[i], c_B)):
                            n = 0
                            for k in range(KC):
                                for a, w in ((nTh, w1h), (nTl, w1h), (nTh, w1l)):
                                    last = e.matmul(bank[:, :], a[:, k, c * P:(c + 1) * P], w[:, half * KC + k, :],
                                                    start=n == 0, stop=n == 3 * KC - 1)
                                    n += 1
                            last.then_inc(done, 1)

                    for c in range(NCH):
                        e.wait_ge(c_hT, c + 1)
                        if c >= 2:
                            e.wait_ge(c_lo, c - 1)
                        for k in range(KC):
                            last = e.transpose(pT[c % 2][:, k * P:(k + 1) * P], hs[:, c, k * P:(k + 1) * P], ident[:])
                        last.then_inc(c_tr, 1)
                        if c >= 1:
                            tables(c - 1)
                    tables(NCH - 1)

                @blk.sync
                def _(e):
                    xv = x[0:(NCH - 1) * P, :].rearrange("(c p) n -> p c n", p=P)
                    e.dma_start(xs[:, 0:1, :], xv[:, 0:1, :]).then_inc(q_x[0], 16)
                    e.dma_start(xs[:, 1:5, :], xv[:, 1:5, :]).then_inc(q_x[1], 16)
                    e.dma_start(xs[:, 5:NCH - 1, :], xv[:, 5:NCH - 1, :]).then_inc(q_x[2], 16)
                    e.wait_ge(c_pad, 1)
                    e.dma_start(xs[0:NTAIL, NCH - 1, :], x[(NCH - 1) * P:N, :]).then_inc(q_x[2], 16)
                    e.dma_start(dsti[:], dst_rows).then_inc(q_dst, 16)
                    e.dma_start(dcoli[:], dst_cols).then_inc(q_dst, 16)
                    e.dma_start(w1raw[:], W1[0:2 * H, :].rearrange("(c p) n -> p c n", p=P)).then_inc(q_w1, 16)
                    e.dma_start(w2raw[:], W2.rearrange("(c p) n -> p c n", p=P)).then_inc(q_w2, 16)
                    for a, b in HALF:
                        e.dma_start(wcraw[a:b, :], W1[2 * H:2 * H + ED, :]).then_inc(q_w2, 16)
                    e.wait_ge(c_bz, 1)
                    for p in (0, 32):
                        e.dma_start(b2raw[p:p + 1, :], b2.rearrange("(a n) -> a n", a=1)).then_inc(q_w2, 16)
                    e.dma_start(b1b[:], row_bcast(b1, H, P)).then_inc(q_w2, 16)
                    e.wait_ge(c_v.sem, v["win"])
                    e.dma_start(win_d, win[:]).then_inc(q_win, 16)
                    e.wait_ge(q_win, 16)
                    e.dma_start(base_b[:].rearrange("p g a -> p (g a)"),
                                row_bcast(win_d.rearrange("g a -> (g a)"), 2 * NG, P)).then_inc(q_winb, 16)
                    e.wait_ge(c_v.sem, v["zero"])
                    for i in range(2):
                        e.dma_start(agg_d[i * NP // 2:(i + 1) * NP // 2, :].rearrange("(p c) n -> p (c n)", p=P),
                                    zero[:]).then_inc(q_h, 16)
                    for c in range(NCH):
                        i = c % 2
                        rows = slice(c * P, (c + 1) * P)
                        e.wait_ge(c_ta, c + 1)
                        e.dma_start(A_d[rows, :], ta[i][:]).then_inc(q_st[i], 16)
                        e.wait_ge(c_tb, 3 * c + 3)
                        e.dma_start(Bh_d[rows, :], tbh[i][:].bitcast(F32)).then_inc(q_st[i], 16)
                        e.dma_start(Bl_d[rows, :], tbl[i][:].bitcast(F32)).then_inc(q_st[i], 16)
                    e.wait_ge(c_hT, NCH)
                    e.dma_start(h_d.rearrange("(c p) n -> p c n", p=P), hs[:]).then_inc(q_h, 16)
                    e.wait_ge(q_st[0], 48 * (NCH // 2))
                    e.wait_ge(q_st[1], 48 * (NCH // 2))
                    e.wait_ge(q_h, 48)

        with est:
            narrow, general = Work(), Work()
            edge_narrow(narrow, scope, sem, locals())
            edge_general(general, scope, sem, locals())
            phase(nc, wide_i, narrow, general)

        xst, sb, _ = scope()
        with xst:
            x1 = sb("x1", [P, NCH, H])
            node_phase(nc, scope, sem, locals())
            conv_phase(nc, scope, sem, locals())


def edge_narrow(work, scope, sem, k):
    ident, iota_w, iota_p, base_b, base_i, dcol = (k[n] for n in ("ident", "iota_w", "iota_p", "base_b", "base_i", "dcol"))
    W2h, W2l, b2r, ones, eaW2, eaW1 = (k[n] for n in ("W2h", "W2l", "b2r", "ones", "eaW2", "eaW1"))
    A_d, Bh_d, Bl_d, agg_d, eaT, src_idx, dst_rows = (k[n] for n in ("A_d", "Bh_d", "Bl_d", "agg_d", "eaT", "src_idx", "dst_rows"))

    PRE_AHEAD = 5
    ACT_MSG = 1
    DVE_PRE = 4
    DVE_MSG = 2
    SEG_LAG = 3
    PREP_AHEAD = (9, 8, 8, 7)
    POOL_MSG = 2
    GATHER_AHEAD = 8
    ACC_LAG = 9
    BANK = (0, 1, 2, 0, 1, 2, 0, 1)
    BACK = (2, 2, 3, 3, 3, 3, 3, 3)
    FIRST, LOOP0 = -PREP_AHEAD[0], 16
    LOOP1 = 4 * FULL - 16
    LAST = 4 * NG + SEG_LAG + 2
    PRES = 4 * NG
    MSGS = 4 * FULL + 1
    assert (LOOP1 - LOOP0) % 8 == 0 and G * FULL + ETAIL == E and 0 < ETAIL <= P

    st, sb, ps = scope()
    with st:
        xg = [sb(f"xg{i}", [P, SUB, H]) for i in range(2)]
        idx = [sb(f"idx{i}", [P, SUB], I32) for i in range(2)]
        ea = [sb(f"ea{i}", [P, G]) for i in range(2)]
        db = [sb(f"db{i}", [64, G], I32) for i in range(2)]
        M1 = [sb(f"M1_{i}", [P, G], F32R) for i in range(2)]
        M2 = [sb(f"M2_{i}", [P, G], F32R) for i in range(2)]
        hTh = [sb(f"hTh{i}", [P, KC, G], F32R) for i in range(2)]
        hTl = [sb(f"hTl{i}", [P, KC, G], F32R) for i in range(2)]
        rp = [sb(f"rp{i}", [P, G]) for i in range(2)]
        rm = [sb(f"rm{i}", [P, H]) for i in range(2)]
        tp = [sb(f"tp{i}", [P, G]) for i in range(2)]
        tm = [sb(f"tm{i}", [P, H]) for i in range(2)]
        mh = [sb(f"mh{i}", [P, H], F32R) for i in range(4)]
        ml = [sb(f"ml{i}", [P, H], F32R) for i in range(4)]
        oh = [sb(f"oh{i}", [P, SUB, P], F32R) for i in range(2)]
        ev = [sb(f"ev{i}", [WIN, H]) for i in range(2)]
        bp = [ps(f"bp{i}") for i in range(3)]
        bm = [ps(f"bm{i}") for i in range(4)]
        bs = ps("bs")

        q_in = [sem(f"e_in{i}") for i in range(2)]
        q_win = [sem(f"e_win{i}") for i in range(2)]
        q_ix = [sem(f"e_ix{i}") for i in range(2)]
        q_ga = [sem(f"e_ga{i}") for i in range(2)]
        q_acc = sem("e_acc")
        s_zero = sem("e_zero")
        s_go = sem("e_go")
        s_prep = sem("e_prep")
        s_oh = sem("e_oh")
        s_pre = sem("e_pre")
        s_msg = sem("e_msg")
        s_seg = sem("e_seg")
        a_pre = sem("a_pre")
        v_sq = sem("v_sq")
        a_msg = sem("a_msg")
        v_pre = sem("v_pre")
        v_msg = sem("v_msg")
        p_msg = sem("p_msg")
        s_ev = sem("e_ev")

        def tail(u):
            return u.reg is None and u.const >= 4 * FULL

        def wait(e, s, val):
            if not (isinstance(val, int) and val < 1):
                e.wait_ge(s, val)

        @work.on("sync")
        def _(e):
            def loads(u):
                p, n = u.par, ETAIL if tail(u) else G
                wait(e, s_prep, u.group(4, -4))
                for a, b in HALF:
                    e.dma_start(ea[p][a:b, 0:n], eaT[:, bass.ds(u.group(G), n)]).then_inc(q_in[p], 16)
                e.dma_start(db[p][:, 0:n], dst_rows[bass.ds(u.group(), 1), 0:n].to_broadcast([64, n]))\
                 .then_inc(q_in[p], 16)
                wait(e, q_ga[p], u.pair(64, 0))
                e.dma_start(idx[p][:], src_idx[bass.ds(u.group(), 1), :, :].rearrange("a p s -> (a p) s"))\
                 .then_inc(q_ix[p], 16)
                b = e.value_load(base_i[0:1, bass.ds(u.group(), 1)], min_val=0, max_val=NP - WIN)
                wait(e, s_pre, u.val(1, -4))
                e.dma_start(eaW1[p][0:32, :].bitcast(F32), Bh_d[bass.ds(b, WIN), :]).then_inc(q_win[p], 16)
                e.dma_start(eaW1[p][32:64, :].bitcast(F32), Bl_d[bass.ds(b, WIN), :]).then_inc(q_win[p], 16)

            loads(At(None, 0))
            loads(At(None, 4))
            with e.Fori(1, FULL // 2) as i:
                loads(At(i, 0))
                loads(At(i, 4))
            loads(At(None, 4 * FULL))
            e.wait_ge(q_acc, 16 * NG)

        @work.on("gpsimd")
        def _(e):
            def gather(u):
                p, n, r = u.par, 1 if tail(u) else SUB, ETAIL if tail(u) else P
                e.wait_ge(q_ix[p], u.pair(16, 16))
                wait(e, s_pre, u.val(1, -4))
                e.sem_inc(s_go, 1)
                for t in range(n):
                    e.indirect_dma_start(out=xg[p][0:r, t, :], out_offset=None, in_=A_d,
                                         in_offset=bass.IndirectOffsetOnAxis(ap=idx[p][0:r, t:t + 1], axis=0))\
                     .then_inc(q_ga[p], 16)

            def accumulate(u):
                b = e.value_load(base_i[0:1, bass.ds(u.group(), 1)], min_val=0, max_val=NP - WIN)
                e.wait_ge(s_ev, u.group(1, 1))
                wait(e, q_acc, u.group(16))
                e.dma_start(agg_d[bass.ds(b, WIN), :], ev[u.par][:], accum_op=ALU.add).then_inc(q_acc, 16)

            def lo(m):
                r, j = ETAIL if tail(m) else P, m.j
                e.wait_ge(v_msg, m.val(2, 2))
                e.tensor_tensor(ml[j][0:r, :], tm[m.const % 2][0:r, :], mh[j][0:r, :], ALU.subtract).then_inc(p_msg, 1)

            def step(s):
                if (s + -POOL_MSG).has(MSGS):
                    lo(s + -POOL_MSG)
                if s.j == 0 and (s + GATHER_AHEAD).has(4 * NG):
                    gather(s + GATHER_AHEAD)
                if s.j == ACC_LAG % SUB and (s + -ACC_LAG).has(4 * FULL):
                    accumulate(s + -ACC_LAG)

            for i in range(2):
                e.memset(oh[i][:].bitcast(F32), 0.0).then_inc(s_zero, 1)
            slots(e, FIRST, LOOP0, LOOP1, LAST, step)
            accumulate(At(None, 4 * FULL))

        @work.on("tensor")
        def _(e):
            def pre(u):
                j, p, w, bank = u.j, u.par, ETAIL if tail(u) else G, bp[BANK[u.const % 8]]
                wait(e, v_pre, u.val(3, 1 - 3 * BACK[u.const % 8]))
                if j == 0:
                    n = 16 if tail(u) else 64
                    e.wait_ge(q_ga[p], u.pair(64, n))
                    e.wait_ge(q_win[p], u.pair(32, 32))
                    e.wait_ge(s_prep, u.group(4, 4))
                for t in range(SUB if w == G else 1):
                    r = min(P, w)
                    e.matmul(bank[:, t * P:t * P + r], xg[p][0:r, t, j * P:(j + 1) * P], ident[0:r, 0:r],
                             start=t == 0, stop=False, is_transpose=True, skip_group_check=True)
                e.matmul(bank[:, 0:w], eaW1[p][:, j * P:(j + 1) * P], M1[p][:, 0:w], start=False, stop=False,
                         skip_group_check=True)
                e.matmul(bank[:, 0:w], eaW2[:, j * P:(j + 1) * P], M2[p][:, 0:w], start=False, stop=True,
                         skip_group_check=True).then_inc(s_pre, 1)

            def msg(u):
                j, p, r = u.j, u.par, ETAIL if tail(u) else P
                wait(e, v_msg, u.val(2, 1 - 8))
                bank = bm[j]
                e.matmul(bank[0:r, :], ones[:, 0:r], b2r[:], start=True, stop=False)
                for c in range(KC):
                    if j == 0:
                        e.wait_ge(v_pre, u.val(3, 3 * c + 3))
                    for a, w in ((hTh, W2h), (hTl, W2h), (hTh, W2l)):
                        last = e.matmul(bank[0:r, :], a[p][:, c, j * P:j * P + r], w[:, c, :], start=False,
                                        stop=c == KC - 1 and w is W2l)
                last.then_inc(s_msg, 1)

            def seg(u):
                j, p, r = u.j, u.par, ETAIL if tail(u) else P
                e.wait_ge(v_msg, u.val(2, 2))
                e.wait_ge(p_msg, u.val(1, 1))
                e.wait_ge(s_oh, u.val(1, 1))
                if j == 0:
                    wait(e, s_ev, u.group())
                end = j == SUB - 1 or r < P
                e.matmul(bs[:, :], oh[p][0:r, j, :], mh[j][0:r, :], start=j == 0, stop=False)
                e.matmul(bs[:, :], oh[p][0:r, j, :], ml[j][0:r, :], start=False, stop=end).then_inc(s_seg, 1)

            def step(s):
                if (s + PRE_AHEAD).has(PRES):
                    pre(s + PRE_AHEAD)
                if s.has(MSGS):
                    msg(s)
                if (s + -SEG_LAG).has(MSGS):
                    seg(s + -SEG_LAG)

            slots(e, FIRST, LOOP0, LOOP1, LAST, step)

        @work.on("scalar")
        def _(e):
            def pre_chain(u, k):
                w = ETAIL if tail(u) else G
                t = rp[u.const % 2][:, 0:w]
                if k == 0:
                    wait(e, v_pre, u.val(3, 1 - 6))
                    e.wait_ge(s_pre, u.val(1, 1))
                    e.activation(t, bp[BANK[u.const % 8]][:, 0:w], ACT.Exp, bias=LNSQ).then_inc(a_pre, 1)
                elif k == 2:
                    e.wait_ge(v_sq, u.val(1, 1))
                    e.activation(t, t, ACT.Ln, bias=1.0, scale=0.5 / (SQ * SQ)).then_inc(a_pre, 1)
                elif k == 3:
                    e.wait_ge(a_pre, u.val(3, 2))
                    e.activation(t, t, ACT.Exp, scale=-1.0).then_inc(a_pre, 1)

            def msg_chain(m, k):
                r = ETAIL if tail(m) else P
                t = rm[m.const % 2][0:r, :]
                if k == 0:
                    wait(e, v_msg, m.val(2, 1 - 4))
                    e.wait_ge(s_msg, m.val(1, 1))
                    e.activation(t, bm[m.j][0:r, :], ACT.Exp).then_inc(a_msg, 1)
                    return
                e.wait_ge(a_msg, m.val(4, k))
                if k == 1:
                    e.activation(t, t, ACT.Square, bias=SQ, scale=SQ).then_inc(a_msg, 1)
                elif k == 2:
                    e.activation(t, t, ACT.Ln, bias=0.5, scale=0.5 / (SQ * SQ)).then_inc(a_msg, 1)
                else:
                    e.activation(t, t, ACT.Exp, scale=-1.0).then_inc(a_msg, 1)

            def step(s):
                u, m = s + PRE_AHEAD, s + -ACT_MSG
                for pre, k in ((1, 0), (0, 0), (0, 1), (1, 2), (0, 2), (1, 3), (0, 3)):
                    if pre and u.has(PRES):
                        pre_chain(u, k)
                    if not pre and m.has(MSGS):
                        msg_chain(m, k)

            slots(e, FIRST, LOOP0, LOOP1, LAST, step)

        @work.on("vector")
        def _(e):
            def prep(u, k):
                p, n, gs = u.par, ETAIL if tail(u) else G, bass.ds(u.group(), 1)
                if k == 0:
                    e.wait_ge(q_in[p], u.pair(48, 48))
                    wait(e, s_pre, u.val(1, -4))
                    e.tensor_copy(M2[p][:, 0:n], ea[p][:, 0:n]).then_inc(s_prep, 1)
                elif k == 1:
                    e.tensor_copy(M1[p][64:128, 0:n], ea[p][64:128, 0:n]).then_inc(s_prep, 1)
                elif k == 2:
                    e.tensor_scalar(M1[p][0:64, 0:n], db[p][:, 0:n], base_b[0:64, gs, 0], iota_p[0:64, :],
                                    ALU.subtract, ALU.is_equal).then_inc(s_prep, 1)
                else:
                    e.wait_ge(s_prep, u.group(4, 1))
                    e.tensor_tensor(M2[p][0:64, 0:n], ea[p][0:64, 0:n], M2[p][0:64, 0:n], ALU.subtract)\
                     .then_inc(s_prep, 1)

            def onehot(u):
                wait(e, s_seg, u.val(1, 1 - 8))
                e.tensor_scalar(oh[u.par][:, u.j, 0:WIN], iota_w[:], base_b[:, bass.ds(u.group(), 1), 0],
                                dcol[:, bass.ds(u.val(), 1)], ALU.add, ALU.is_equal).then_inc(s_oh, 1)

            def square(u):
                w = ETAIL if tail(u) else G
                t = rp[u.const % 2][:, 0:w]
                e.wait_ge(a_pre, u.val(3, 1))
                e.scalar_tensor_tensor(t, t, 2.0 * SQ, t, ALU.add, ALU.mult).then_inc(v_sq, 1)

            def pre(u, k):
                w, p, j = ETAIL if tail(u) else G, u.par, u.j
                t = tp[u.const % 2][:, 0:w]
                if k == 0:
                    e.wait_ge(a_pre, u.val(3, 3))
                    e.scalar_tensor_tensor(t, rp[u.const % 2][:, 0:w], 1.0, bp[BANK[u.const % 8]][:, 0:w],
                                           ALU.subtract, ALU.mult).then_inc(v_pre, 1)
                    return
                e.wait_ge(v_pre, u.val(3, k))
                if k == 1:
                    if j == 0:
                        wait(e, s_msg, u.val(1, -4))
                    e.tensor_copy(hTh[p][:, j, 0:w], t).then_inc(v_pre, 1)
                else:
                    e.tensor_tensor(hTl[p][:, j, 0:w], t, hTh[p][:, j, 0:w], ALU.subtract).then_inc(v_pre, 1)

            def msg(m, k):
                r, j = ETAIL if tail(m) else P, m.j
                t = tm[m.const % 2][0:r, :]
                if k == 0:
                    wait(e, p_msg, m.val(1, -1))
                    e.wait_ge(a_msg, m.val(4, 4))
                    e.scalar_tensor_tensor(t, rm[m.const % 2][0:r, :], 1.0, bm[j][0:r, :], ALU.subtract, ALU.mult)\
                     .then_inc(v_msg, 1)
                else:
                    e.wait_ge(v_msg, m.val(2, 1))
                    wait(e, s_seg, m.val(1, 1 - 4))
                    e.tensor_copy(mh[j][0:r, :], t).then_inc(v_msg, 1)

            def step(s):
                u, m, v = s + DVE_PRE, s + -DVE_MSG, s + PRE_AHEAD
                if u.has(PRES):
                    pre(u, 0)
                if v.has(PRES):
                    square(v)
                if u.has(PRES):
                    pre(u, 1)
                q = s + -(SEG_LAG + 1)
                if (q.j == SUB - 1 and q.has(MSGS)) or (q.reg is None and q.const == MSGS - 1):
                    e.wait_ge(s_seg, q.val(1, 1))
                    wait(e, q_acc, q.group(16, -16))
                    e.tensor_copy(ev[q.par][:], bs[0:WIN, :]).then_inc(s_ev, 1)
                if m.has(MSGS):
                    msg(m, 0)
                if u.has(PRES):
                    pre(u, 2)
                if m.has(MSGS):
                    msg(m, 1)
                for k in range(4):
                    g = s + PREP_AHEAD[k]
                    if g.j == 0 and g.has(4 * NG):
                        prep(g, k)
                if s.has(MSGS):
                    if s.reg is None and s.const == 0:
                        e.wait_ge(s_zero, 2)
                    onehot(s)

            slots(e, FIRST, LOOP0, LOOP1, LAST, step)


def edge_general(work, scope, sem, k):
    A_d, Bh_d, Bl_d, agg_d, eaT, src_cols, dst_cols, W1, W2, b2, dcol, ident, row_bcast = (
        k[n] for n in ("A_d", "Bh_d", "Bl_d", "agg_d", "eaT", "src_cols", "dst_cols", "W1", "W2", "b2", "dcol",
                       "ident", "row_bcast"))
    st, sb, ps = scope()
    with st:
        idx_all = sb("g_idx_all", [P, 2, NG * SUB], I32)
        idx = sb("g_idx", [P, 2], I32)
        xa = sb("g_xa", [P, H])
        xb = sb("g_xb", [P, 2, H])
        ea = sb("g_ea", [ED, P])
        we = sb("g_we", [ED, H])
        w2 = sb("g_w2", [P, KC, H])
        b2b = sb("g_b2b", [P, H])
        rho = sb("g_rho", [P, H])
        t = sb("g_t", [P, H])
        tT = sb("g_tT", [P, KC, P])
        iota_i = sb("g_iota_i", [P, NP], I32)
        iota_n = sb("g_iota_n", [P, NP])
        oh = sb("g_oh", [P, NP])
        agg = sb("g_agg", [P, NCH, H])
        px, pT = ps("g_px"), ps("g_pT")
        pa = [ps(f"g_pa{i}") for i in range(NCH // 2)]

        q_k = sem("g_k")
        q_agg = sem("g_out")
        chain = Chain(sem("g_s"), sem("g_ga"), sem("g_go"))

        def one(op, *args, **kw):
            return lambda e, s: op(e)(*args, **kw).then_inc(s, 1)

        def mish():
            act = lambda e: e.activation
            return [("scalar", 1, one(act, rho[:], xa[:], ACT.Exp)),
                    ("scalar", 1, one(act, rho[:], rho[:], ACT.Square, bias=SQ, scale=SQ)),
                    ("scalar", 1, one(act, rho[:], rho[:], ACT.Ln, bias=0.5, scale=0.5 / (SQ * SQ))),
                    ("scalar", 1, one(act, rho[:], rho[:], ACT.Exp, scale=-1.0)),
                    ("vector", 1, one(lambda e: e.scalar_tensor_tensor, t[:], rho[:], 1.0, xa[:], ALU.subtract, ALU.mult))]

        def setup(e, s):
            e.wait_ge(q_k, 5 * 16)
            e.tensor_copy(iota_n[:], iota_i[:]).then_inc(s, 1)
            e.tensor_scalar(w2[:], w2[:], -1.0, None, ALU.mult).then_inc(s, 1)
            e.memset(agg[:], 0.0).then_inc(s, 1)
            e.memset(xa[:], 0.0).then_inc(s, 1)

        start = [("gpsimd", 1, one(lambda e: e.iota, iota_i[:], pattern=[[1, NP]], base=0, channel_multiplier=0)),
                 ("vector", 4, setup)]

        def subtile(i, r):
            def copy_idx(e, s):
                e.tensor_copy(idx[:], idx_all[:, :, bass.ds(i, 1)].rearrange("p a b -> p (a b)")).then_inc(s, 1)

            def gather(e, s):
                for dst, tab, col in ((xa[0:r, :], A_d, 0), (xb[0:r, 0, :], Bh_d, 1), (xb[0:r, 1, :], Bl_d, 1)):
                    e.indirect_dma_start(out=dst, out_offset=None, in_=tab, in_offset=bass.IndirectOffsetOnAxis(
                        ap=idx[0:r, col:col + 1], axis=0)).then_inc(s, 16)

            def load_ea(e, s):
                e.dma_start(ea[:, 0:r], eaT[:, bass.ds(i * P, r)]).then_inc(s, 16)

            def transposes(e, s):
                for c in range(KC):
                    last = e.transpose(pT[:, c * P:(c + 1) * P], t[:, c * P:(c + 1) * P], ident[:])
                last.then_inc(s, 1)

            def messages(e, s):
                for c in range(KC):
                    last = e.matmul(px[:, :], tT[:, c, :], w2[:, c, :], start=c == 0, stop=c == KC - 1)
                last.then_inc(s, 1)

            def products(half):
                def step(e, s):
                    for n in range(NCH // 2):
                        c = half * (NCH // 2) + n
                        last = e.matmul(pa[n][:, :], oh[0:r, c * P:(c + 1) * P], t[0:r, :], start=True, stop=True)
                    last.then_inc(s, 1)
                return step

            def adds(half):
                def step(e, s):
                    for n in range(NCH // 2):
                        c = half * (NCH // 2) + n
                        e.tensor_tensor(agg[:, c, :], agg[:, c, :], pa[n][:, :], ALU.add).then_inc(s, 1)
                return step

            tt = lambda e: e.tensor_tensor
            return [("vector", 1, copy_idx),
                    ("gather", 48, gather),
                    ("sync", 16, load_ea),
                    ("tensor", 1, one(lambda e: e.matmul, px[0:r, :], ea[:, 0:r], we[:], start=True, stop=True)),
                    ("vector", 1, one(tt, xa[0:r, :], xa[0:r, :], xb[0:r, 0, :], ALU.add)),
                    ("vector", 1, one(tt, xa[0:r, :], xa[0:r, :], xb[0:r, 1, :], ALU.add)),
                    ("vector", 1, one(tt, xa[0:r, :], xa[0:r, :], px[0:r, :], ALU.add)),
                    *mish(),
                    ("tensor", 1, transposes),
                    ("scalar", 1, one(lambda e: e.activation, tT[:].rearrange("p k n -> p (k n)"), pT[:, :], ACT.Copy)),
                    ("tensor", 1, messages),
                    ("vector", 1, one(tt, xa[:], px[:, :], b2b[:], ALU.add)),
                    *mish(),
                    ("vector", 1, one(lambda e: e.tensor_scalar, oh[:], iota_n[:], dcol[:, bass.ds(i, 1)], None, ALU.is_equal)),
                    ("tensor", 1, products(0)), ("vector", NCH // 2, adds(0)),
                    ("tensor", 1, products(1)), ("vector", NCH // 2, adds(1))]

        def program(engine, e):
            chain.n = chain.g = 0
            chain.run(engine, e, start)
            chain.done(start)
            with e.Fori(0, SUB * FULL) as i:
                chain.run(engine, e, subtile(i, P), i)
            chain.done(subtile(0, P), SUB * FULL)
            chain.run(engine, e, subtile(SUB * FULL, ETAIL))
            chain.done(subtile(0, P))

        @work.on("sync")
        def _(e):
            e.dma_start(idx_all[:, 0, :], src_cols).then_inc(q_k, 16)
            e.dma_start(idx_all[:, 1, :], dst_cols).then_inc(q_k, 16)
            e.dma_start(we[:], W1[2 * H:2 * H + ED, :]).then_inc(q_k, 16)
            e.dma_start(w2[:], W2.rearrange("(c p) n -> p c n", p=P)).then_inc(q_k, 16)
            e.dma_start(b2b[:], row_bcast(b2, H, P)).then_inc(q_k, 16)
            program("sync", e)
            e.wait_ge(chain.s, chain.n)
            e.dma_start(agg_d.rearrange("(c p) n -> p c n", p=P), agg[:]).then_inc(q_agg, 16)
            e.wait_ge(q_agg, 16)

        @work.on("gpsimd")
        def _(e):
            program("gpsimd", e)

        @work.on("scalar")
        def _(e):
            program("scalar", e)

        @work.on("vector")
        def _(e):
            program("vector", e)

        @work.on("tensor")
        def _(e):
            program("tensor", e)


def node_phase(nc, scope, sem, k):
    ident, nTh, nTl, x1 = (k[n] for n in ("ident", "nTh", "nTl", "x1"))
    x, h_d, agg_d, W3, b3, W4, b4 = (k[n] for n in ("x", "h_d", "agg_d", "W3", "b3", "W4", "b4"))
    gamma, beta, U, sv, Sh_d, Sl_d, row_bcast, newton = (
        k[n] for n in ("gamma", "beta", "U", "sv", "Sh_d", "Sl_d", "row_bcast", "newton"))
    BLK = [range(0, 4), range(4, 8), range(8, NCH)]
    NB = len(BLK)

    st, sb, ps = scope()
    with st:
        raw = sb("raw", [P, KC, H])
        W3h = sb("W3h", [P, 2 * KC, H], F32R)
        W3l = sb("W3l", [P, 2 * KC, H], F32R)
        W4h = sb("W4h", [P, KC, H], F32R)
        W4l = sb("W4l", [P, KC, H], F32R)
        Us = sb("Us", [P, KC, R])
        b3c = sb("b3c", [P, KC])
        b4b = sb("b4b", [P, H])
        gab = sb("gab", [P, H])
        beb = sb("beb", [P, H])
        svb = sb("svb", [P, R])
        ag = sb("ag", [P, 4, H])
        aTh = sb("aTh", [P, KC, 4 * P], F32R)
        aTl = sb("aTl", [P, KC, 4 * P], F32R)
        uTh = sb("uTh", [P, KC, 4 * P], F32R)
        uTl = sb("uTl", [P, KC, 4 * P], F32R)
        hb = sb("hb", [P, 4, H])
        xb = sb("xb", [P, 4, H])
        xf = [sb(f"xf{i}", [P, H]) for i in range(2)]
        rho = [sb(f"rho{i}", [P, H]) for i in range(2)]
        um = [sb(f"um{i}", [P, H]) for i in range(2)]
        h2T = [sb(f"h2T{i}", [P, KC, P]) for i in range(2)]
        Ss = [sb(f"Ss{i}", [P, R]) for i in range(2)]
        Sh = [sb(f"Sh{i}", [P, R], F32R) for i in range(2)]
        Sl = [sb(f"Sl{i}", [P, R], F32R) for i in range(2)]
        stats = sb("stats3", [P, 4, 6])
        mv = sb("mv3", [P, 4, 2])
        var = sb("var3", [P, 4])
        lnv = sb("lnv3", [P, 4])
        rstd = sb("rstd3", [P, 4])
        nmr = sb("nmr3", [P, 4])
        tmp = sb("tmp3", [P, 4])
        pt = [ps(f"pt{i}") for i in range(2)]
        pu = [ps(f"pu{i}") for i in range(2)]
        po = [ps(f"po{i}") for i in range(2)]
        psS = [ps(f"psS{i}") for i in range(2)]

        q_w = [sem(f"n_w{i}") for i in range(3)]
        q_c = sem("n_c")
        q_ag = [sem(f"n_ag{b}") for b in range(NB)]
        q_hx = [sem(f"n_hx{b}") for b in range(NB)]
        q_S = [sem(f"n_S{i}") for i in range(2)]
        s_raw = sem("n_raw")
        s_tr = sem("n_tr")
        s_ah = sem("n_ah")
        s_al = sem("n_al")
        s_u = sem("n_u")
        s_xf = sem("n_xf")
        s_rho = sem("n_rho")
        s_o = sem("n_o")
        s_hb = sem("n_hb")
        s_ln = sem("n_ln")
        s_var = sem("n_var")
        s_r = sem("n_r")
        s_nm = sem("n_nm")
        s_x1 = sem("n_x1")
        s_h2 = sem("n_h2")
        s_t2 = sem("n_t2")
        s_e2 = sem("n_e2")
        s_S = sem("n_Sm")
        s_Sv = sem("n_Sv")

        def first(b):
            return BLK[b][0]

        with nc.Block() as blk:
            @blk.sync
            def _(e):
                def block_loads(b):
                    n, r0 = len(BLK[b]), first(b) * P
                    if b >= 1:
                        e.wait_ge(s_tr, first(b))
                    e.dma_start(ag[:, 0:n, :], agg_d[r0:r0 + n * P, :].rearrange("(c p) n -> p c n", p=P))\
                     .then_inc(q_ag[b], 16)
                    if b >= 1:
                        e.wait_ge(s_ln, first(b))
                        e.wait_ge(s_t2, first(b))
                    e.dma_start(hb[:, 0:n, :], h_d[r0:r0 + n * P, :].rearrange("(c p) n -> p c n", p=P))\
                     .then_inc(q_hx[b], 16)
                    full = n if b < NB - 1 else n - 1
                    e.dma_start(xb[:, 0:full, :], x[r0:r0 + full * P, :].rearrange("(c p) n -> p c n", p=P))\
                     .then_inc(q_hx[b], 16)
                    if b == NB - 1:
                        e.dma_start(xb[0:NTAIL, full, :], x[r0 + full * P:N, :]).then_inc(q_hx[b], 16)

                for i, src in enumerate((W3[0:H, :], W3[H:2 * H, :], W4)):
                    if i:
                        e.wait_ge(s_raw, i)
                    e.dma_start(raw[:], src.rearrange("(c p) n -> p c n", p=P)).then_inc(q_w[i], 16)
                    if i == 0:
                        e.dma_start(ag[:, 0:4, :], agg_d[0:4 * P, :].rearrange("(c p) n -> p c n", p=P))\
                         .then_inc(q_ag[0], 16)
                        e.dma_start(Us[:], U.rearrange("(c p) n -> p c n", p=P)).then_inc(q_c, 16)
                        with nc.allow_non_contiguous_dma(reason="512 values, once"):
                            e.dma_start(b3c[:], b3.rearrange("(c p) -> p c", p=P)).then_inc(q_c, 16)
                        e.dma_start(b4b[:], row_bcast(b4, H, P)).then_inc(q_c, 16)
                        e.dma_start(gab[:], row_bcast(gamma, H, P)).then_inc(q_c, 16)
                        e.dma_start(beb[:], row_bcast(beta, H, P)).then_inc(q_c, 16)
                        e.dma_start(svb[:], row_bcast(sv, R, P)).then_inc(q_c, 16)
                        e.dma_start(hb[:], h_d[0:4 * P, :].rearrange("(c p) n -> p c n", p=P)).then_inc(q_hx[0], 16)
                        e.dma_start(xb[:], x[0:4 * P, :].rearrange("(c p) n -> p c n", p=P)).then_inc(q_hx[0], 16)
                for b in range(NB):
                    if b >= 1:
                        block_loads(b)
                    for c in BLK[b]:
                        e.wait_ge(s_Sv, 3 * c + 3)
                        rows = slice(c * P, (c + 1) * P)
                        e.dma_start(Sh_d[rows, :], Sh[c % 2][:].bitcast(F32)).then_inc(q_S[c % 2], 16)
                        e.dma_start(Sl_d[rows, :], Sl[c % 2][:].bitcast(F32)).then_inc(q_S[c % 2], 16)
                for i in range(2):
                    e.wait_ge(q_S[i], 32 * (NCH // 2))

            @blk.gpsimd
            def _(e):
                e.wait_ge(q_c, 6 * 16)
                for b in range(NB):
                    n = len(BLK[b])
                    e.wait_ge(q_hx[b], 32 if b < NB - 1 else 48)
                    for c in range(n):
                        r = NTAIL if first(b) + c == NCH - 1 else P
                        e.tensor_tensor(hb[:, c, :], hb[:, c, :], b4b[:], ALU.add).then_inc(s_hb, 1)
                        e.tensor_tensor(xb[0:r, c, :], xb[0:r, c, :], beb[0:r, :], ALU.add).then_inc(s_hb, 1)

            @blk.scalar
            def _(e):
                def stats_chain(i):
                    e.wait_ge(s_var, i + 1)
                    n = len(BLK[i // 2])
                    e.activation(lnv[:, 0:n], var[:, 0:n], ACT.Ln).then_inc(s_r, 1)
                    e.wait_ge(s_r, 2 * i + 1)
                    e.activation(rstd[:, 0:n], lnv[:, 0:n], ACT.Exp, scale=-0.5).then_inc(s_r, 1)

                def evac_agg(b):
                    for i, c in enumerate(BLK[b]):
                        e.wait_ge(s_tr, c + 1)
                        if i == 0 and b:
                            e.wait_ge(s_u, KC * b)
                        e.activation(aTh[:, :, i * P:(i + 1) * P], pt[c % 2][:, :].rearrange("p (k n) -> p k n", k=KC),
                                     ACT.Copy).then_inc(s_ah, 1)

                def chain(b):
                    w = len(BLK[b]) * P
                    for f in range(KC):
                        i = KC * b + f
                        t = rho[i % 2][:, 0:w]
                        e.wait_ge(s_xf, 5 * i + 1)
                        e.activation(t, t, ACT.Exp).then_inc(s_rho, 1)
                        e.wait_ge(s_rho, 4 * i + 1)
                        e.activation(t, t, ACT.Square, bias=SQ, scale=SQ).then_inc(s_rho, 1)
                        e.wait_ge(s_rho, 4 * i + 2)
                        e.activation(t, t, ACT.Ln, bias=0.5, scale=0.5 / (SQ * SQ)).then_inc(s_rho, 1)
                        e.wait_ge(s_rho, 4 * i + 3)
                        e.activation(t, t, ACT.Exp, scale=-1.0).then_inc(s_rho, 1)

                def h2(b):
                    e.wait_ge(s_nm, b + 1)
                    for i, c in enumerate(BLK[b]):
                        e.activation(xb[:, i, :], x1[:, c, :], ACT.Relu, bias=nmr[:, i:i + 1], scale=rstd[:, i:i + 1])\
                         .then_inc(s_h2, 1)
                    for c in BLK[b]:
                        e.wait_ge(s_t2, c + 1)
                        if c >= 2:
                            e.wait_ge(s_S, c - 1)
                        e.activation(h2T[c % 2][:], pt[c % 2][:, :].rearrange("p (k n) -> p k n", k=KC), ACT.Copy)\
                         .then_inc(s_e2, 1)

                for b in range(NB):
                    evac_agg(b)
                    chain(b)
                    stats_chain(2 * b)
                    stats_chain(2 * b + 1)
                    h2(b)

            @blk.vector
            def _(e):
                s_v = sem("n_v")
                cnt = [0]

                def link(ins):
                    cnt[0] += 1
                    ins.then_inc(s_v, 1)
                    e.wait_ge(s_v, cnt[0])

                def split(i, hi, lo, sign):
                    e.wait_ge(q_w[i], 16)
                    if sign < 0:
                        link(e.tensor_scalar(raw[:], raw[:], -1.0, None, ALU.mult))
                    link(e.tensor_copy(hi, raw[:]))
                    e.tensor_tensor(lo, raw[:], hi, ALU.subtract).then_inc(s_raw, 1)

                def lo_agg(b):
                    for i, c in enumerate(BLK[b]):
                        e.wait_ge(s_ah, c + 1)
                        e.tensor_tensor(aTl[:, :, i * P:(i + 1) * P], pt[c % 2][:, :].rearrange("p (k n) -> p k n", k=KC),
                                        aTh[:, :, i * P:(i + 1) * P], ALU.subtract).then_inc(s_al, 1)

                def units(b):
                    w = len(BLK[b]) * P

                    def load_x(i):
                        e.wait_ge(s_u, i + 1)
                        f = i % KC
                        e.tensor_scalar(rho[i % 2][:, 0:w], pu[i % 2][:, 0:w], b3c[:, f:f + 1], XMAX, ALU.add, ALU.min)\
                         .then_inc(s_xf, 1)
                        e.tensor_scalar(xf[i % 2][:, 0:w], pu[i % 2][:, 0:w], b3c[:, f:f + 1], None, ALU.add)\
                         .then_inc(s_xf, 1)

                    for f in range(KC):
                        i = KC * b + f
                        t = um[i % 2][:, 0:w]
                        load_x(i)
                        e.wait_ge(s_xf, 5 * i + 2)
                        e.wait_ge(s_rho, 4 * i + 4)
                        e.scalar_tensor_tensor(t, rho[i % 2][:, 0:w], 1.0, xf[i % 2][:, 0:w], ALU.subtract, ALU.mult)\
                         .then_inc(s_xf, 1)
                        e.wait_ge(s_xf, 5 * i + 3)
                        if f == 0 and b:
                            e.wait_ge(s_o, first(b))
                        e.tensor_copy(uTh[:, f, 0:w], t).then_inc(s_xf, 1)
                        e.wait_ge(s_xf, 5 * i + 4)
                        e.tensor_tensor(uTl[:, f, 0:w], t, uTh[:, f, 0:w], ALU.subtract).then_inc(s_xf, 1)

                def norm(i, n):
                    for j in range(n):
                        (link if j == n - 1 else lambda ins: None)(e.bn_aggr(mv[:, j, :], stats[:, j, :]))
                    e.tensor_scalar(var[:, 0:n], mv[:, 0:n, 1], LN_EPS, None, ALU.add).then_inc(s_var, 1)
                    e.wait_ge(s_r, 2 * i + 2)
                    newton(e, link, var[:, 0:n], rstd[:, 0:n], tmp[:, 0:n])

                def residual(b):
                    n, c0 = len(BLK[b]), first(b)
                    for j, c in enumerate(BLK[b]):
                        e.wait_ge(s_o, c + 1)
                        e.wait_ge(s_hb, 2 * (c + 1))
                        e.tensor_tensor(x1[:, c, :], po[c % 2][:, :], hb[:, j, :], ALU.add).then_inc(s_ln, 1)
                        e.wait_ge(s_ln, c + 1)
                        (link if j == n - 1 else lambda ins: None)(e.bn_stats(stats[:, j, :], x1[:, c, :]))
                    norm(2 * b, n)
                    for j, c in enumerate(BLK[b]):
                        link(e.scalar_tensor_tensor(x1[:, c, :], x1[:, c, :], mv[:, j, 0:1], gab[:], ALU.subtract, ALU.mult))
                    for j, c in enumerate(BLK[b]):
                        r = NTAIL if c == NCH - 1 else P
                        link(e.scalar_tensor_tensor(x1[0:r, c, :], x1[0:r, c, :], rstd[0:r, j:j + 1], xb[0:r, j, :],
                                                    ALU.mult, ALU.add))
                        (link if j == n - 1 else lambda ins: None)(e.bn_stats(stats[:, j, :], x1[:, c, :]))
                    norm(2 * b + 1, n)
                    e.scalar_tensor_tensor(nmr[:, 0:n], mv[:, 0:n, 0], -1.0, rstd[:, 0:n], ALU.mult, ALU.mult)\
                     .then_inc(s_nm, 1)

                def store_S(b):
                    for c in BLK[b]:
                        i = c % 2
                        e.wait_ge(s_S, c + 1)
                        if c >= 2:
                            e.wait_ge(q_S[i], 32 * (c // 2))
                        e.tensor_tensor(Ss[i][:], psS[i][:, 0:R], svb[:], ALU.mult).then_inc(s_Sv, 1)
                        e.wait_ge(s_Sv, 3 * c + 1)
                        e.tensor_copy(Sh[i][:], Ss[i][:]).then_inc(s_Sv, 1)
                        e.wait_ge(s_Sv, 3 * c + 2)
                        e.tensor_tensor(Sl[i][:], Ss[i][:], Sh[i][:], ALU.subtract).then_inc(s_Sv, 1)

                split(0, W3h[:, 0:KC, :], W3l[:, 0:KC, :], 1)
                split(1, W3h[:, KC:2 * KC, :], W3l[:, KC:2 * KC, :], -1)
                split(2, W4h[:], W4l[:], -1)
                e.wait_ge(q_c, 6 * 16)
                for b in range(NB):
                    lo_agg(b)
                    units(b)
                    residual(b)
                    store_S(b)

            @blk.tensor
            def _(e):
                def agg_T(b):
                    e.wait_ge(q_ag[b], 16)
                    for i, c in enumerate(BLK[b]):
                        if c >= 2:
                            e.wait_ge(s_al, c - 1)
                        if i == 0 and b:
                            e.wait_ge(s_e2, first(b))
                        for f in range(KC):
                            last = e.transpose(pt[c % 2][:, f * P:(f + 1) * P], ag[:, i, f * P:(f + 1) * P], ident[:])
                        last.then_inc(s_tr, 1)

                def u_units(b):
                    n0, w = first(b) * P, len(BLK[b]) * P
                    if b == 0:
                        e.wait_ge(s_raw, 2)
                    for f in range(KC):
                        i = KC * b + f
                        if i >= 2:
                            e.wait_ge(s_xf, 5 * (i - 2) + 2)
                        m = 0
                        for c in range(2 * KC):
                            if f == 0 and c == KC:
                                e.wait_ge(s_al, BLK[b][-1] + 1)
                            ah, al = ((nTh[:, c, n0:n0 + w], nTl[:, c, n0:n0 + w]) if c < KC else
                                      (aTh[:, c - KC, 0:w], aTl[:, c - KC, 0:w]))
                            for wt, a in ((W3h, ah), (W3h, al), (W3l, ah)):
                                last = e.matmul(pu[i % 2][:, 0:w], wt[:, c, f * P:(f + 1) * P], a,
                                                start=m == 0, stop=m == 6 * KC - 1)
                                m += 1
                        last.then_inc(s_u, 1)

                def out_chunks(b):
                    if b == 0:
                        e.wait_ge(s_raw, 3)
                    for i, c in enumerate(BLK[b]):
                        if c >= 2:
                            e.wait_ge(s_ln, c - 1)
                        m = 0
                        for f in range(KC):
                            if i == 0:
                                e.wait_ge(s_xf, 5 * (KC * b + f) + 5)
                            for a, w in ((uTh, W4h), (uTl, W4h), (uTh, W4l)):
                                last = e.matmul(po[c % 2][:, :], a[:, f, i * P:(i + 1) * P], w[:, f, :],
                                                start=m == 0, stop=m == 3 * KC - 1)
                                m += 1
                        last.then_inc(s_o, 1)

                def S_chunks(b):
                    for i, c in enumerate(BLK[b]):
                        e.wait_ge(s_h2, c + 1)
                        if i == 0:
                            e.wait_ge(s_al, BLK[b][-1] + 1)
                        if c >= 2:
                            e.wait_ge(s_e2, c - 1)
                        for f in range(KC):
                            last = e.transpose(pt[c % 2][:, f * P:(f + 1) * P], xb[:, i, f * P:(f + 1) * P], ident[:])
                        last.then_inc(s_t2, 1)
                        if c >= 2:
                            e.wait_ge(s_Sv, 3 * (c - 2) + 1)
                        e.wait_ge(s_e2, c + 1)
                        for f in range(KC):
                            last = e.matmul(psS[c % 2][:, 0:R], h2T[c % 2][:, f, :], Us[:, f, :], start=f == 0, stop=f == KC - 1)
                        last.then_inc(s_S, 1)

                e.wait_ge(q_c, 6 * 16)
                for b in range(NB):
                    agg_T(b)
                    u_units(b)
                    out_chunks(b)
                    S_chunks(b)


def conv_phase(nc, scope, sem, k):
    x1, row_bcast, wide_i = (k[n] for n in ("x1", "row_bcast", "wide_i"))
    src_cols, ew_cols, Vt, bias, out = (k[n] for n in ("src_cols", "ew_cols", "Vt", "bias", "out"))
    st, sb, ps = scope()
    with st:
        iota_ni = sb("iota_ni", [P, NP], I32)
        iota_n = sb("iota_n", [P, NP])
        scoli = sb("scoli", [P, NG * SUB], I32)
        paii = sb("paii", [P, NG * SUB], I32)
        scol = sb("scol", [P, NG * SUB])
        nscol = sb("nscol", [P, NG * SUB])
        odd = sb("odd", [P, NG * SUB])
        ewc = sb("ewc", [P, NG * SUB])
        ew2 = sb("ew2", [P, NG * SUB, 2])
        VV = sb("VV", [P, H])
        bib = sb("bib", [P, H])
        sums = sb("sums", [P, NP])
        res = [sb(f"res{i}", [P, H]) for i in range(2)]
        pc = [[ps(f"pc{odd}{i}") for i in range(2)] for odd in range(2)]
        pf = [ps(f"pf{i}") for i in range(2)]

        q_k = sem("k_k")
        q_v = sem("k_v")
        q_o = sem("k_o")
        s_c = sem("k_c")
        s_sum = sem("k_sum")
        s_f = sem("k_f")
        s_r = sem("k_r")

        def prelude(engine, e):
            if engine == "sync":
                e.dma_start(scoli[:], src_cols).then_inc(q_k, 16)
                e.dma_start(ewc[:], ew_cols).then_inc(q_k, 16)
                for a, b in HALF:
                    e.dma_start(VV[a:b, :], Vt).then_inc(q_v, 16)
                e.dma_start(bib[:], row_bcast(bias, H, P)).then_inc(q_v, 16)
            elif engine == "gpsimd":
                e.iota(iota_ni[:], pattern=[[1, NP]], base=0, channel_multiplier=0).then_inc(s_c, 1)
            elif engine == "vector":
                e.wait_ge(q_k, 2 * 16)
                e.tensor_scalar(paii[:], scoli[:], 1, None, ALU.arith_shift_right).then_inc(s_c, 1)
                e.tensor_scalar(scoli[:], scoli[:], 1, None, ALU.bitwise_and).then_inc(s_c, 1)
                e.wait_ge(s_c, 3)
                e.tensor_copy(scol[:], paii[:]).then_inc(s_c, 1)
                e.tensor_scalar(nscol[:], paii[:], -1.0, None, ALU.mult).then_inc(s_c, 1)
                e.tensor_copy(odd[:], scoli[:]).then_inc(s_c, 1)
                e.tensor_copy(iota_n[:], iota_ni[:]).then_inc(s_c, 1)
                e.wait_ge(s_c, 7)
                e.tensor_tensor(ew2[:, :, 1], ewc[:], odd[:], ALU.mult).then_inc(s_c, 1)
                e.wait_ge(s_c, 8)
                e.tensor_tensor(ew2[:, :, 0], ewc[:], ew2[:, :, 1], ALU.subtract).then_inc(s_c, 1)
                e.wait_ge(s_c, 9)

        narrow, general = Work(), Work()
        conv_narrow(narrow, scope, sem, k, locals())
        conv_general(general, scope, sem, k, locals())
        phase(nc, wide_i, narrow, general)

        with nc.Block() as blk:
            def evacuate(odd, i, copy):
                (c0, w) = SBLK[i]
                w = min(w, N // 2 - c0)
                nodes = sums[:].rearrange("p (n two) -> p n two", two=2)[:, c0:c0 + w, odd]
                copy(nodes, pc[odd][i][:, 0:w]).then_inc(s_sum, 1)

            @blk.scalar
            def _(e):
                for i in range(2):
                    evacuate(0, i, lambda out, src: e.activation(out, src, ACT.Copy))

            @blk.vector
            def _(e):
                for i in range(2):
                    evacuate(1, i, lambda out, src: e.tensor_copy(out, src))
                e.wait_ge(q_v, 3 * 16)
                for c in range(NCH):
                    r, t = min(P, N - c * P), res[c % 2]
                    e.wait_ge(s_f, c + 1)
                    e.tensor_tensor(t[0:r, :], pf[c % 2][0:r, :], bib[0:r, :], ALU.add).then_inc(s_r, 1)
                    e.wait_ge(s_r, 2 * c + 1)
                    e.scalar_tensor_tensor(x1[0:r, c, :], t[0:r, :], 0.0, x1[0:r, c, :], ALU.max, ALU.add).then_inc(s_r, 1)

            @blk.tensor
            def _(e):
                e.wait_ge(q_v, 3 * 16)
                e.wait_ge(s_sum, 4)
                for c in range(NCH):
                    r = min(P, N - c * P)
                    if c >= 2:
                        e.wait_ge(s_r, 2 * (c - 2) + 1)
                    e.matmul(pf[c % 2][0:r, :], sums[:, c * P:c * P + r], VV[:], start=True, stop=True).then_inc(s_f, 1)

            @blk.sync
            def _(e):
                for c in range(NCH):
                    r = min(P, N - c * P)
                    e.wait_ge(s_r, 2 * c + 2)
                    e.dma_start(out[c * P:c * P + r, :], x1[0:r, c, :]).then_inc(q_o, 16)
                e.wait_ge(q_o, 16 * NCH)


def conv_narrow(work, scope, sem, k, c):
    iota_p, base_b, base_i, Sh_d, Sl_d, dst_rows = (
        k[n] for n in ("iota_p", "base_b", "base_i", "Sh_d", "Sl_d", "dst_rows"))
    iota_n, scol, nscol, ew2, pc, prelude, s_c = (
        c[n] for n in ("iota_n", "scol", "nscol", "ew2", "pc", "prelude", "s_c"))
    BY_ACT = SUB // 2
    st, sb, ps = scope()
    with st:
        db = [sb(f"c_db{i}", [64, G], I32) for i in range(2)]
        oT = [sb(f"c_oT{i}", [64, G], F32R) for i in range(2)]
        Sw = [sb(f"c_Sw{i}", [64, R], F32R) for i in range(2)]
        gw = [sb(f"c_gw{i}", [P, SUB, 2, R]) for i in range(2)]
        ghl = [sb(f"c_ghl{i}", [P, SUB, 2, 2 * R], F32R) for i in range(2)]
        so = [sb(f"c_so{i}", [P, NPAIR], F32R) for i in range(SUB)]
        d2 = [sb(f"c_d2_{i}", [P, NPAIR]) for i in range(2 * (SUB - BY_ACT))]
        pg = [ps(f"pg{i}") for i in range(2)]

        q_in = [sem(f"k_in{i}") for i in range(2)]
        q_w = [sem(f"k_w{i}") for i in range(2)]
        s_oT = sem("k_oT")
        s_g = sem("k_g")
        s_gw = sem("k_gw")
        s_hi = sem("k_hi")
        s_lo = sem("k_lo")
        s_so = sem("k_so")
        s_sa = sem("k_sa")
        s_sc = sem("k_sc")

        def tail(u):
            return u.reg is None and u.const >= 4 * FULL

        def wait(e, s, val):
            if not (isinstance(val, int) and val < 1):
                e.wait_ge(s, val)

        def groups(e, step):
            for g in (0, 1):
                step(At(None, 4 * g))
            with e.Fori(1, FULL // 2 - 1) as i:
                for g in (0, 1):
                    step(At(i, 4 * g))
            for g in range(FULL - 2, NG):
                step(At(None, 4 * g))

        @work.on("sync")
        def _(e):
            prelude("sync", e)

            def loads(u):
                p, n = u.par, ETAIL if tail(u) else G
                wait(e, s_oT, u.group(1, -1))
                e.dma_start(db[p][:, 0:n], dst_rows[bass.ds(u.group(), 1), 0:n].to_broadcast([64, n]))\
                 .then_inc(q_in[p], 16)
                b = e.value_load(base_i[0:1, bass.ds(u.group(), 1)], min_val=0, max_val=NP - WIN)
                wait(e, s_g, u.group(1, -1))
                e.dma_start(Sw[p][0:32, :].bitcast(F32), Sh_d[bass.ds(b, WIN), :]).then_inc(q_w[p], 16)
                e.dma_start(Sw[p][32:64, :].bitcast(F32), Sl_d[bass.ds(b, WIN), :]).then_inc(q_w[p], 16)

            groups(e, loads)

        @work.on("gpsimd")
        def _(e):
            prelude("gpsimd", e)

        @work.on("scalar")
        def _(e):
            def step(u):
                if tail(u):
                    return
                for i, j in enumerate(range(BY_ACT, SUB)):
                    wait(e, s_sa, u.group(4, i - 5))
                    e.activation(d2[2 * u.par + i][:], iota_n[:, 0:NPAIR], ACT.Square, bias=nscol[:, bass.ds(u.val(1, j), 1)])\
                     .then_inc(s_sa, 1)
                for i, j in enumerate(range(BY_ACT, SUB)):
                    e.wait_ge(s_sa, u.group(4, i + 1))
                    wait(e, s_sc, u.val(1, j + 1 - SUB))
                    e.activation(so[j][:], d2[2 * u.par + i][:], ACT.Relu, bias=1.0, scale=-1.0).then_inc(s_sa, 1)

            e.wait_ge(s_c, 9)
            groups(e, step)

        @work.on("vector")
        def _(e):
            prelude("vector", e)

            def oneT(u):
                p, n = u.par, ETAIL if tail(u) else G
                e.wait_ge(q_in[p], u.pair(16, 16))
                wait(e, s_g, u.group(1, -1))
                e.tensor_scalar(oT[p][:, 0:n], db[p][:, 0:n], base_b[0:64, bass.ds(u.group(), 1), 0], iota_p[0:64, :],
                                ALU.subtract, ALU.is_equal).then_inc(s_oT, 1)

            def weigh(u):
                p, n, r = u.par, 1 if tail(u) else SUB, ETAIL if tail(u) else P
                e.wait_ge(s_g, u.group(1, 1))
                wait(e, s_lo, u.group(1, -1))
                rows = pg[p][0:r, 0:n * R].rearrange("p (s b a) -> p s b a", s=n, b=1).to_broadcast([r, n, 2, R])
                w = ew2[0:r, bass.ds(u.val(), n), :].rearrange("p s (b a) -> p s b a", a=1).to_broadcast([r, n, 2, R])
                e.tensor_tensor(gw[p][0:r, 0:n, :, :], rows, w, ALU.mult).then_inc(s_gw, 1)

            def hi(u):
                p, n, r = u.par, 1 if tail(u) else SUB, ETAIL if tail(u) else P
                e.wait_ge(s_gw, u.group(1, 1))
                wait(e, s_sc, u.val(1, -4))
                e.tensor_copy(ghl[p][0:r, 0:n, :, 0:R], gw[p][0:r, 0:n, :, :]).then_inc(s_hi, 1)

            def lo(u):
                p, n, r = u.par, 1 if tail(u) else SUB, ETAIL if tail(u) else P
                e.wait_ge(s_hi, u.group(1, 1))
                e.tensor_tensor(ghl[p][0:r, 0:n, :, R:2 * R], gw[p][0:r, 0:n, :, :], ghl[p][0:r, 0:n, :, 0:R], ALU.subtract)\
                 .then_inc(s_lo, 1)

            def onehot(u, j):
                r = ETAIL if tail(u) else P
                wait(e, s_sc, u.val(1, j + 1 - SUB))
                e.tensor_scalar(so[j][0:r, :], iota_n[0:r, 0:NPAIR], scol[0:r, bass.ds(u.val(1, j), 1)], None,
                                ALU.is_equal).then_inc(s_so, 1)

            def step(u):
                onehot(u, 0)
                if tail(u):
                    return
                weigh(u + 4)
                onehot(u, 1)
                if (u + 8).has(4 * NG):
                    oneT(u + 8)
                hi(u + 4)
                lo(u + 4)

            oneT(At(None, 0))
            oneT(At(None, 4))
            weigh(At(None, 0))
            hi(At(None, 0))
            lo(At(None, 0))
            groups(e, step)

        @work.on("tensor")
        def _(e):
            def rows_of(u):
                p, n, r = u.par, 1 if tail(u) else SUB, ETAIL if tail(u) else P
                e.wait_ge(q_w[p], u.pair(32, 32))
                e.wait_ge(s_oT, u.group(1, 1))
                wait(e, s_gw, u.group(1, -1))
                for j in range(n):
                    m = e.matmul(pg[p][0:r, j * R:(j + 1) * R], oT[p][:, j * P:j * P + r], Sw[p][:], start=j == 0,
                                 stop=j == n - 1, skip_group_check=True)
                m.then_inc(s_g, 1)

            def scatter(u):
                p, last = u.par, tail(u)
                r = ETAIL if last else P
                for j in range(1 if last else SUB):
                    if j == 0:
                        e.wait_ge(s_lo, u.group(1, 1))
                    if j == BY_ACT and (u + 8).has(4 * NG):
                        rows_of(u + 8)
                    if j >= BY_ACT:
                        e.wait_ge(s_sa, u.group(4, j + 1))
                    else:
                        e.wait_ge(s_so, u.group(BY_ACT, j + 1))
                    first = u.reg is None and u.const + j == 0
                    for odd in range(2):
                        for i, (c0, w) in enumerate(SBLK):
                            m = e.matmul(pc[odd][i][:, 0:w], ghl[p][0:r, j, odd, :], so[j][0:r, c0:c0 + w], start=first,
                                         stop=last, skip_group_check=True)
                    m.then_inc(s_sc, 1)

            rows_of(At(None, 0))
            rows_of(At(None, 4))
            groups(e, scatter)


def conv_general(work, scope, sem, k, c):
    Sh_d, Sl_d, dst_cols = (k[n] for n in ("Sh_d", "Sl_d", "dst_cols"))
    iota_n, scol, ew2, pc, prelude, s_c = (c[n] for n in ("iota_n", "scol", "ew2", "pc", "prelude", "s_c"))
    st, sb, ps = scope()
    with st:
        idx_all = sb("h_idx_all", [P, NG * SUB], I32)
        idx = sb("h_idx", [P, 1], I32)
        S = sb("h_S", [P, 2, R])
        g = sb("h_g", [P, 2, R])
        ghl = sb("h_ghl", [P, 2, 2 * R], F32R)
        so = sb("h_so", [P, NPAIR], F32R)
        q_k = sem("h_k")
        chain = Chain(sem("h_s"), sem("h_ga"), sem("h_go"))

        def subtile(i, r, first=False, last=False):
            def copy_idx(e, s):
                e.tensor_copy(idx[:], idx_all[:, bass.ds(i, 1)]).then_inc(s, 1)

            def gather(e, s):
                for n, tab in enumerate((Sh_d, Sl_d)):
                    e.indirect_dma_start(out=S[0:r, n, :], out_offset=None, in_=tab, in_offset=bass.IndirectOffsetOnAxis(
                        ap=idx[0:r, 0:1], axis=0)).then_inc(s, 16)

            def add(e, s):
                e.tensor_tensor(S[0:r, 0, :], S[0:r, 0, :], S[0:r, 1, :], ALU.add).then_inc(s, 1)

            def weigh(e, s):
                w = ew2[0:r, bass.ds(i, 1), :].rearrange("p a b -> p (a b)")
                for odd in range(2):
                    e.tensor_scalar(g[0:r, odd, :], S[0:r, 0, :], w[:, odd:odd + 1], None, ALU.mult).then_inc(s, 1)

            def hi(e, s):
                e.tensor_copy(ghl[0:r, :, 0:R], g[0:r, :, :]).then_inc(s, 1)

            def lo(e, s):
                e.tensor_tensor(ghl[0:r, :, R:2 * R], g[0:r, :, :], ghl[0:r, :, 0:R], ALU.subtract).then_inc(s, 1)

            def onehot(e, s):
                e.tensor_scalar(so[0:r, :], iota_n[0:r, 0:NPAIR], scol[0:r, bass.ds(i, 1)], None, ALU.is_equal)\
                 .then_inc(s, 1)

            def scatter(e, s):
                for odd in range(2):
                    for b, (c0, w) in enumerate(SBLK):
                        m = e.matmul(pc[odd][b][:, 0:w], ghl[0:r, odd, :], so[0:r, c0:c0 + w], start=first, stop=last,
                                     skip_group_check=True)
                m.then_inc(s, 1)

            return [("vector", 1, copy_idx), ("gather", 32, gather), ("vector", 1, add), ("vector", 2, weigh),
                    ("vector", 1, hi), ("vector", 1, lo), ("vector", 1, onehot), ("tensor", 1, scatter)]

        def program(engine, e):
            prelude(engine, e)
            if engine == "vector":
                e.wait_ge(q_k, 16)
            chain.n = chain.g = 0
            chain.run(engine, e, subtile(0, P, first=True))
            with e.Fori(1, SUB * FULL) as i:
                chain.run(engine, e, subtile(i, P), i)
            chain.done(subtile(0, P), SUB * FULL)
            chain.run(engine, e, subtile(SUB * FULL, ETAIL, last=True))

        @work.on("sync")
        def _(e):
            e.dma_start(idx_all[:], dst_cols).then_inc(q_k, 16)
            prelude("sync", e)

        @work.on("gpsimd")
        def _(e):
            program("gpsimd", e)

        @work.on("scalar")
        def _(e):
            e.wait_ge(s_c, 9)

        @work.on("vector")
        def _(e):
            program("vector", e)

        @work.on("tensor")
        def _(e):
            program("tensor", e)


def kernel(x, src, dst, edge_attr_64, edge_weight, L0_gnn_W1, L0_gnn_b1, L0_gnn_W2, L0_gnn_b2, L0_gnn_W3,
           L0_gnn_b3, L0_gnn_W4, L0_gnn_b4, L0_gnn_gamma, L0_gnn_beta, L1_gnn_U, L1_gnn_s, L1_gnn_Vt, L1_gnn_bias):
    import numpy as np
    import concourse.bacc as bacc
    from concourse.bass_utils import run_bass_kernel_spmd

    def groups(a):
        a = np.asarray(a)
        return np.concatenate([a, np.repeat(a[-1:], NG * G - E)]).reshape(NG, SUB, P)

    w = np.asarray(edge_weight)
    arrays = {
        "x": x,
        "src_idx": groups(src).transpose(0, 2, 1),
        "dst_rows": groups(dst).reshape(NG, G),
        "src_cols": groups(src).reshape(NG * SUB, P).T,
        "dst_cols": groups(dst).reshape(NG * SUB, P).T,
        "eaT": np.asarray(edge_attr_64).T,
        "ew_cols": groups(w).reshape(NG * SUB, P).T,
        "W1": L0_gnn_W1, "b1": L0_gnn_b1, "W2": L0_gnn_W2, "b2": L0_gnn_b2, "W3": L0_gnn_W3, "b3": L0_gnn_b3,
        "W4": L0_gnn_W4, "b4": L0_gnn_b4, "gamma": L0_gnn_gamma, "beta": L0_gnn_beta,
        "U": L1_gnn_U, "sv": L1_gnn_s, "Vt": L1_gnn_Vt, "bias": L1_gnn_bias,
    }
    arrays = {n: np.ascontiguousarray(a) for n, a in arrays.items()}
    nc = bacc.Bacc("TRN2", target_bir_lowering=False, num_devices=1)
    args = {n: nc.dram_tensor(f"in_{n}", a.shape, mybir.dt.from_np(a.dtype), kind="ExternalInput").ap()
            for n, a in arrays.items()}
    out = nc.dram_tensor("out_0", (N, H), F32, kind="ExternalOutput").ap()
    gnn_two_layers(nc, out=out, **args)
    r = run_bass_kernel_spmd(nc, [{f"in_{n}": a for n, a in arrays.items()}], core_ids=[0])
    return r.results[0]["out_0"]
```

```python
import concourse.bass as bass
from concourse import mybir
from concourse.alu_op_type import AluOpType as ALU
from contextlib import ExitStack

F32 = mybir.dt.float32
F32R = mybir.dt.float32r
I32 = mybir.dt.int32
ACT = mybir.ActivationFunctionType
AX = mybir.AxisListType

P = 128
H = 512
KC = H // P
N = 1250
NCH = -(-N // P)
NP = NCH * P
NTAIL = N - (NCH - 1) * P
E = 40000
SUB = 4
G = SUB * P
NG = -(-E // G)
FULL = E // G
ETAIL = E - FULL * G
ED = 64
R = 64
WIN = 32
LN_EPS = 1e-5
XMAX = 20.0
SQ = 2.0 ** 32
LNSQ = 32 * 0.6931471805599453
HALF = [(0, 64), (64, 128)]
ZERO_DMAS = 5
BATCH = [(0, 5), (5, NCH)]
NBLK = [(0, 512), (512, 512), (1024, 256)]
NPAIR = N // 2 + 1
SBLK = [(0, 314), (314, NPAIR - 314)]


class At:

    def __init__(self, reg, const):
        self.reg, self.const = reg, const

    def __add__(self, n):
        return At(self.reg, self.const + n)

    def val(self, mult=1, add=0):
        c = self.const * mult + add
        return c if self.reg is None else self.reg * (2 * SUB * mult) + c

    def group(self, mult=1, add=0):
        c = self.const // SUB * mult + add
        return c if self.reg is None else self.reg * (2 * mult) + c

    def pair(self, mult, add=0):
        c = self.const // (2 * SUB) * mult + add
        return c if self.reg is None else self.reg * mult + c

    @property
    def j(self):
        return self.const % SUB

    @property
    def par(self):
        return self.const // SUB % 2

    def has(self, n):
        return self.reg is not None or 0 <= self.const < n


def slots(eng, first, head, tail, last, step):
    for s in range(first, head):
        step(At(None, s))
    with eng.Fori(head // (2 * SUB), tail // (2 * SUB)) as i:
        for k in range(2 * SUB):
            step(At(i, k))
    for s in range(tail, last):
        step(At(None, s))


class Work:

    def __init__(self):
        self.of = {}

    def on(self, engine):
        def keep(program):
            self.of[engine] = program
        return keep


def phase(nc, wide_i, narrow, general):
    def both(engine, e):
        span = e.value_load(wide_i[0:1, 0:1], min_val=0, max_val=NP)
        with e.If(span < WIN):
            narrow.of[engine](e)
        with e.Else():
            general.of[engine](e)

    with nc.Block() as blk:
        @blk.sync
        def _(e):
            both("sync", e)

        @blk.gpsimd
        def _(e):
            both("gpsimd", e)

        @blk.scalar
        def _(e):
            both("scalar", e)

        @blk.vector
        def _(e):
            both("vector", e)

        @blk.tensor
        def _(e):
            both("tensor", e)


class Chain:

    def __init__(self, s, s_gather, s_go):
        self.s, self.s_gather, self.s_go = s, s_gather, s_go
        self.n = self.g = 0

    def run(self, engine, e, steps, t=0):
        total_n = sum(by for who, by, _ in steps if who != "gather")
        total_g = sum(by for who, by, _ in steps if who == "gather")
        n, g, after_gather = self.n, self.g, False
        for who, by, step in steps:
            gather = who == "gather"
            if who == engine or (gather and engine == "gpsimd"):
                if after_gather:
                    e.wait_ge(self.s_gather, t * total_g + g)
                elif not (isinstance(t, int) and t * total_n + n == 0):
                    e.wait_ge(self.s, t * total_n + n)
                if gather:
                    e.sem_inc(self.s_go, 1)
                step(e, self.s_gather if gather else self.s)
            if gather:
                g += by
            else:
                n += by
            after_gather = gather

    def done(self, steps, times=1):
        self.n += times * sum(by for who, by, _ in steps if who != "gather")
        self.g += times * sum(by for who, by, _ in steps if who == "gather")


class Line:

    def __init__(self, sem):
        self.sem, self.n = sem, 0

    def inc(self, ins, by=1):
        ins.then_inc(self.sem, by)
        self.n += by
        return self.n


def gnn_two_layers(nc, x, src_idx, dst_rows, src_cols, dst_cols, eaT, ew_cols, W1, b1, W2, b2, W3, b3, W4, b4,
                   gamma, beta, U, sv, Vt, bias, out):
    ctx = ExitStack()
    names = set()

    def sem(name):
        assert name not in names
        names.add(name)
        return ctx.enter_context(nc.semaphore(name))

    def scope():
        st = ExitStack()
        return (st, lambda n, s, d=F32: st.enter_context(nc.sbuf_tensor(n, s, d)),
                lambda n, s=(P, 512): st.enter_context(nc.psum_tensor(n, list(s), F32)))

    def twice(sb, name, shape):
        st, sb_raw, _ = scope()
        with st:
            raw = sb_raw(name + "_raw", shape)
        return raw, sb(name, shape, F32R)

    def dram(name, shape, dt=F32):
        return nc.dram_tensor(name, shape, dt, kind="Internal").ap()

    def row_bcast(ap, n, parts):
        return ap.rearrange("(a n) -> a n", a=1).to_broadcast([parts, n])

    A_d = dram("A_tab", (NP, H))
    Bh_d = dram("Bh_tab", (NP, H))
    Bl_d = dram("Bl_tab", (NP, H))
    h_d = dram("h_tab", (NP, H))
    agg_d = dram("agg_tab", (NP, H))
    Sh_d = dram("Sh_tab", (NP, R))
    Sl_d = dram("Sl_tab", (NP, R))
    win_d = dram("win_tab", (NG, 2))

    with ctx:
        pst, sb, _ = scope()
        ctx.enter_context(pst)
        ident = sb("ident", [P, P])
        iota_w = sb("iota_w", [P, WIN])
        iota_p = sb("iota_p", [P, 1])
        base_b = sb("base_b", [P, NG, 2])
        base_i = sb("base_i", [1, NG], I32)
        wide_i = sb("wide_i", [1, 1], I32)
        dcol = sb("dcol", [P, NG * SUB])
        nTh = sb("nTh", [P, KC, NP], F32R)
        nTl = sb("nTl", [P, KC, NP], F32R)
        W3raw, W3l = twice(sb, "W3l", [P, 2 * KC, H])
        W4raw, W4l = twice(sb, "W4l", [P, KC, H])
        q_w3 = [sem(f"q_w3_{i}") for i in range(3)]
        est, sb, _ = scope()
        W2h = sb("W2h", [P, KC, H], F32R)
        W2raw, W2l = twice(sb, "W2l", [P, KC, H])
        b2r = sb("b2r", [64, H], F32R)
        ones = sb("ones", [64, P], F32R)
        eaW2 = sb("eaW2", [P, H], F32R)
        eaW1 = [sb(f"eaW1_{i}", [P, H], F32R) for i in range(2)]

        def newton(e, link, var, r, t):
            link(e.tensor_tensor(t, r, r, ALU.mult))
            link(e.tensor_tensor(t, t, var, ALU.mult))
            link(e.tensor_scalar(t, t, -0.5, 1.5, ALU.mult, ALU.add))
            link(e.tensor_tensor(r, r, t, ALU.mult))

        st, sb1, ps1 = scope()
        with st:
            xs = sb1("xs", [P, NCH, H])
            hs = sb1("hs", [P, NCH, H])
            w1h = sb1("w1h", [P, 2 * KC, H], F32R)
            w1raw, w1l = twice(sb1, "w1l", [P, 2 * KC, H])
            wcraw = sb1("wcraw", [P, H])
            b1b = sb1("b1b", [P, H])
            b2raw = sb1("b2raw", [64, H])
            dsti = sb1("dsti", [NG, G], I32)
            dcoli = sb1("dcoli", [P, NG * SUB], I32)
            win = sb1("win", [NG, 2])
            mx = sb1("mx", [NG, 1])
            iota_i = sb1("iota_i", [P, WIN], I32)
            iop_i = sb1("iop_i", [P, 1], I32)
            stats = sb1("stats", [P, NCH, 6])
            mv = sb1("mv", [P, NCH, 2])
            var = sb1("var", [P, NCH])
            lnv = sb1("lnv", [P, NCH])
            rstd = sb1("rstd", [P, NCH])
            nmr = sb1("nmr", [P, NCH])
            tmp = sb1("tmp", [P, NCH])
            ta = [sb1(f"ta{i}", [P, H]) for i in range(2)]
            tb = [sb1(f"tb{i}", [P, H]) for i in range(2)]
            tbh = [sb1(f"tbh{i}", [P, H], F32R) for i in range(2)]
            tbl = [sb1(f"tbl{i}", [P, H], F32R) for i in range(2)]
            zero = sb1("zero", [P, NCH * H // ZERO_DMAS])
            pT = [ps1(f"pT{i}") for i in range(2)]
            pA = [ps1(f"pA{i}") for i in range(2)]
            pB = [ps1(f"pB{i}") for i in range(2)]

            q_x = [sem(f"q_x{i}") for i in range(2)]
            q_dst = sem("q_dst")
            q_w1 = [sem(f"q_w1_{i}") for i in range(2)]
            q_w2 = sem("q_w2")
            q_b1 = sem("q_b1")
            q_win = sem("q_win")
            q_winb = sem("q_winb")
            q_st = [sem(f"q_st{i}") for i in range(2)]
            q_h = sem("q_h")
            c_g = Line(sem("c_g"))
            c_v = Line(sem("c_v"))
            c_a = sem("c_a")
            c_hT = sem("c_hT")
            c_tr = sem("c_tr")
            c_hi = sem("c_hi")
            c_lo = sem("c_lo")
            c_A = sem("c_A")
            c_B = sem("c_B")
            c_ta = sem("c_ta")
            c_tb = sem("c_tb")
            c_pad = sem("c_pad")
            c_bz = sem("c_bz")
            v = {}

            with nc.Block() as blk:
                def store_b(e, c):
                    i = c % 2
                    if c == 0:
                        e.wait_ge(q_b1, 16)
                    e.wait_ge(c_B, c + 1)
                    if c >= 2:
                        e.wait_ge(q_st[i], 48 * (c // 2))
                    e.tensor_tensor(tb[i][:], pB[i][:, :], b1b[:], ALU.add).then_inc(c_tb, 1)
                    e.wait_ge(c_tb, 3 * c + 1)
                    e.tensor_copy(tbh[i][:], tb[i][:]).then_inc(c_tb, 1)
                    e.wait_ge(c_tb, 3 * c + 2)
                    e.tensor_tensor(tbl[i][:], tb[i][:], tbh[i][:], ALU.subtract).then_inc(c_tb, 1)

                def evac(e, c):
                    i = c % 2
                    e.wait_ge(c_tr, c + 1)
                    e.activation(nTh[:, :, c * P:(c + 1) * P], pT[i][:, :].rearrange("p (k n) -> p k n", k=KC),
                                 ACT.Copy).then_inc(c_hi, 1)
                    if c >= 1:
                        store_a(e, c - 1)

                def store_a(e, c):
                    i = c % 2
                    e.wait_ge(c_A, c + 1)
                    if c >= 2:
                        e.wait_ge(q_st[i], 48 * (c // 2))
                    e.activation(ta[i][:], pA[i][:, :], ACT.Copy).then_inc(c_ta, 1)

                @blk.vector
                def _(e):
                    def link(ins):
                        c_v.inc(ins)
                        e.wait_ge(c_v.sem, c_v.n)

                    def later():
                        e.wait_ge(c_v.sem, c_v.n)

                    def variances(i):
                        c0, c1 = BATCH[i]
                        e.wait_ge(q_x[i], (16, 32)[i])
                        for c in range(c0, c1):
                            c_v.inc(e.bn_stats(stats[:, c, :], xs[:, c, :]))
                        later()
                        for c in range(c0, c1):
                            c_v.inc(e.bn_aggr(mv[:, c, :], stats[:, c, :]))
                        later()
                        link(e.tensor_scalar(var[:, c0:c1], mv[:, c0:c1, 1], LN_EPS, None, ALU.add))
                        v["var", i] = c_v.n

                    def scales(i):
                        c0, c1 = BATCH[i]
                        e.wait_ge(c_a, 2 * i + 2)
                        newton(e, link, var[:, c0:c1], rstd[:, c0:c1], tmp[:, c0:c1])
                        link(e.scalar_tensor_tensor(nmr[:, c0:c1], mv[:, c0:c1, 0], -1.0, rstd[:, c0:c1],
                                                    ALU.mult, ALU.mult))
                        v["rstd", i] = c_v.n

                    def split_w1(i):
                        k = slice(i * KC, (i + 1) * KC)
                        e.wait_ge(q_w1[i], 16)
                        link(e.tensor_copy(w1h[:, k, :], w1raw[:, k, :]))
                        link(e.tensor_tensor(w1l[:, k, :], w1raw[:, k, :], w1h[:, k, :], ALU.subtract))
                        v["w1", i] = c_v.n

                    def windows():
                        e.wait_ge(q_dst, 32)
                        c_v.inc(e.tensor_reduce(win[:, 0:1], dsti[:, :], AX.X, ALU.min))
                        link(e.tensor_reduce(mx[:], dsti[:, :], AX.X, ALU.max))
                        link(e.tensor_scalar(win[:, 0:1], win[:, 0:1], float(NP - WIN), None, ALU.min))
                        link(e.tensor_tensor(win[:, 1:2], mx[:], win[:, 0:1], ALU.subtract))
                        v["win"] = c_v.n
                        c_v.inc(e.tensor_copy(dcol[:], dcoli[:]))

                    def iotas():
                        e.wait_ge(c_g.sem, 3)
                        c_v.inc(e.tensor_copy(iota_w[:], iota_i[:]))
                        link(e.tensor_scalar(iop_i[:], iop_i[:], WIN - 1, None, ALU.bitwise_and))
                        c_v.inc(e.tensor_copy(iota_p[:], iop_i[:]))

                    def w2_hi():
                        e.wait_ge(q_w2, 5 * 16)
                        c_v.inc(e.tensor_scalar(W2h[:], W2raw[:], -1.0, None, ALU.mult))
                        c_v.inc(e.tensor_copy(eaW2[:], wcraw[:]))
                        for i in range(2):
                            c_v.inc(e.tensor_copy(eaW1[i][64:128, :], wcraw[64:128, :]))
                        c_v.inc(e.tensor_copy(b2r[:], b2raw[:]))

                    def w2_lo():
                        later()
                        c_v.inc(e.scalar_tensor_tensor(W2l[:], W2raw[:], -1.0, W2h[:], ALU.mult, ALU.subtract))
                        c_v.inc(e.tensor_tensor(eaW2[64:128, :], wcraw[64:128, :], eaW2[64:128, :], ALU.subtract))
                        c_v.inc(e.tensor_tensor(b2r[32:64, :], b2raw[32:64, :], b2r[32:64, :], ALU.subtract))

                    def bases():
                        e.wait_ge(q_winb, 16)
                        c_v.inc(e.tensor_copy(base_i[0:1, :], base_b[0:1, :, 0]))
                        c_v.inc(e.tensor_reduce(wide_i[0:1, :], base_b[0:1, :, 1], AX.X, ALU.max))

                    between = {0: [lambda: split_w1(1)], 1: [lambda: variances(1)], 2: [windows],
                               3: [lambda: scales(1), iotas], 4: [w2_hi], 5: [w2_lo], 6: [bases]}

                    e.memset(xs[:, NCH - 1, :], 0.0).then_inc(c_pad, 1)
                    e.memset(b2raw[:], 0.0).then_inc(c_bz, 1)
                    c_v.inc(e.memset(zero[:], 0.0))
                    v["zero"] = c_v.n
                    variances(0)
                    scales(0)
                    split_w1(0)
                    for c in range(NCH):
                        i = c % 2
                        e.wait_ge(c_hi, c + 1)
                        e.tensor_tensor(nTl[:, :, c * P:(c + 1) * P], pT[i][:, :].rearrange("p (k n) -> p k n", k=KC),
                                        nTh[:, :, c * P:(c + 1) * P], ALU.subtract).then_inc(c_lo, 1)
                        if c >= 1:
                            store_b(e, c - 1)
                        for work in between.get(c, ()):
                            work()
                    store_b(e, NCH - 1)

                @blk.gpsimd
                def _(e):
                    c_g.inc(e.memset(ident[:], 0.0))
                    c_g.inc(e.iota(iota_i[:], pattern=[[1, WIN]], base=0, channel_multiplier=0))
                    c_g.inc(e.iota(iop_i[:], pattern=[[0, 1]], base=0, channel_multiplier=1))
                    e.wait_ge(c_g.sem, 1)
                    c_g.inc(e.affine_select(out=ident[:], in_=ident[:], compare_op=ALU.not_equal, fill=1.0,
                                            base=0, pattern=[[-1, P]], channel_multiplier=1))
                    c_g.inc(e.memset(ones[:].bitcast(F32), 1.0))

                @blk.scalar
                def _(e):
                    e.preload_act_table_set("natural_log_exp_and_others")
                    for c in range(NCH):
                        for i in range(2):
                            c0, c1 = BATCH[i]
                            if c == max(c0 - 1, 0):
                                e.wait_ge(c_v.sem, v["var", i])
                                e.activation(lnv[:, c0:c1], var[:, c0:c1], ACT.Ln).then_inc(c_a, 1)
                                e.wait_ge(c_a, 2 * i + 1)
                                e.activation(rstd[:, c0:c1], lnv[:, c0:c1], ACT.Exp, scale=-0.5).then_inc(c_a, 1)
                            if c == c0:
                                e.wait_ge(c_v.sem, v["rstd", i])
                        e.activation(hs[:, c, :], xs[:, c, :], ACT.Relu, bias=nmr[:, c:c + 1],
                                     scale=rstd[:, c:c + 1]).then_inc(c_hT, 1)
                        if c >= 1:
                            evac(e, c - 1)
                    evac(e, NCH - 1)
                    store_a(e, NCH - 1)

                @blk.tensor
                def _(e):
                    e.wait_ge(c_g.sem, 4)

                    def tables(c):
                        i = c % 2
                        e.wait_ge(c_lo, c + 1)
                        if c >= 2:
                            e.wait_ge(c_ta, c - 1)
                            e.wait_ge(c_tb, 3 * (c - 2) + 1)
                        for half, bank, done in ((0, pA[i], c_A), (1, pB[i], c_B)):
                            n = 0
                            if c == 0:
                                e.wait_ge(c_v.sem, v["w1", half])
                            for k in range(KC):
                                for a, w in ((nTh, w1h), (nTl, w1h), (nTh, w1l)):
                                    last = e.matmul(bank[:, :], a[:, k, c * P:(c + 1) * P], w[:, half * KC + k, :],
                                                    start=n == 0, stop=n == 3 * KC - 1)
                                    n += 1
                            last.then_inc(done, 1)

                    for c in range(NCH):
                        e.wait_ge(c_hT, c + 1)
                        if c >= 2:
                            e.wait_ge(c_lo, c - 1)
                        for k in range(KC):
                            last = e.transpose(pT[c % 2][:, k * P:(k + 1) * P], hs[:, c, k * P:(k + 1) * P], ident[:])
                        last.then_inc(c_tr, 1)
                        if c >= 1:
                            tables(c - 1)
                    tables(NCH - 1)

                @blk.sync
                def _(e):
                    def w1_half(i):
                        e.dma_start(w1raw[:, i * KC:(i + 1) * KC, :],
                                    W1[i * H:(i + 1) * H, :].rearrange("(c p) n -> p c n", p=P)).then_inc(q_w1[i], 16)

                    xv = x[0:(NCH - 1) * P, :].rearrange("(c p) n -> p c n", p=P)
                    half = BATCH[0][1]
                    e.dma_start(xs[:, 0:half, :], xv[:, 0:half, :]).then_inc(q_x[0], 16)
                    w1_half(0)
                    w1_half(1)
                    e.dma_start(b1b[:], row_bcast(b1, H, P)).then_inc(q_b1, 16)
                    e.dma_start(xs[:, half:NCH - 1, :], xv[:, half:NCH - 1, :]).then_inc(q_x[1], 16)
                    e.wait_ge(c_pad, 1)
                    e.dma_start(xs[0:NTAIL, NCH - 1, :], x[(NCH - 1) * P:N, :]).then_inc(q_x[1], 16)
                    for a, b in HALF:
                        e.dma_start(wcraw[a:b, :], W1[2 * H:2 * H + ED, :]).then_inc(q_w2, 16)
                    e.wait_ge(c_bz, 1)
                    for p in (0, 32):
                        e.dma_start(b2raw[p:p + 1, :], b2.rearrange("(a n) -> a n", a=1)).then_inc(q_w2, 16)
                    e.dma_start(W2raw[:], W2.rearrange("(c p) n -> p c n", p=P)).then_inc(q_w2, 16)
                    e.dma_start(dsti[:], dst_rows).then_inc(q_dst, 16)
                    e.dma_start(dcoli[:], dst_cols).then_inc(q_dst, 16)

                    def store_tables(c):
                        i = c % 2
                        rows = slice(c * P, (c + 1) * P)
                        e.wait_ge(c_ta, c + 1)
                        e.dma_start(A_d[rows, :], ta[i][:]).then_inc(q_st[i], 16)
                        e.wait_ge(c_tb, 3 * c + 3)
                        e.dma_start(Bh_d[rows, :], tbh[i][:].bitcast(F32)).then_inc(q_st[i], 16)
                        e.dma_start(Bl_d[rows, :], tbl[i][:].bitcast(F32)).then_inc(q_st[i], 16)

                    for c in range(NCH):
                        store_tables(c)
                        if c == 1:
                            e.wait_ge(c_v.sem, v["zero"])
                            for i in range(ZERO_DMAS):
                                e.dma_start(agg_d[i * NP // ZERO_DMAS:(i + 1) * NP // ZERO_DMAS, :]
                                            .rearrange("(p c) n -> p (c n)", p=P), zero[:]).then_inc(q_h, 16)
                        if c == 3:
                            e.wait_ge(c_v.sem, v["win"])
                            e.dma_start(win_d, win[:]).then_inc(q_win, 16)
                            e.wait_ge(q_win, 16)
                            e.dma_start(base_b[:].rearrange("p g a -> p (g a)"),
                                        row_bcast(win_d.rearrange("g a -> (g a)"), 2 * NG, P)).then_inc(q_winb, 16)
                        if c in (4, 5):
                            i = c - 4
                            e.dma_start(W3raw[:, i * KC:(i + 1) * KC, :],
                                        W3[i * H:(i + 1) * H, :].rearrange("(c p) n -> p c n", p=P)).then_inc(q_w3[i], 16)
                        if c == 6:
                            e.dma_start(W4raw[:], W4.rearrange("(c p) n -> p c n", p=P)).then_inc(q_w3[2], 16)
                        if c == 7:
                            e.wait_ge(c_hT, half)
                            e.dma_start(h_d[0:half * P, :].rearrange("(c p) n -> p c n", p=P), hs[:, 0:half, :])\
                             .then_inc(q_h, 16)
                        if c == 8:
                            e.wait_ge(c_hT, NCH)
                            e.dma_start(h_d[half * P:, :].rearrange("(c p) n -> p c n", p=P), hs[:, half:, :])\
                             .then_inc(q_h, 16)
                    e.wait_ge(q_st[0], 48 * (NCH // 2))
                    e.wait_ge(q_st[1], 48 * (NCH // 2))
                    e.wait_ge(q_h, 16 * (ZERO_DMAS + 2))

        with est:
            narrow, general = Work(), Work()
            edge_narrow(narrow, scope, sem, locals())
            edge_general(general, scope, sem, locals())
            phase(nc, wide_i, narrow, general)

        xst, sb, _ = scope()
        with xst:
            x1 = sb("x1", [P, NCH, H])
            node_phase(nc, scope, sem, locals())
            conv_phase(nc, scope, sem, locals())


def edge_narrow(work, scope, sem, k):
    ident, iota_w, iota_p, base_b, base_i, dcol = (k[n] for n in ("ident", "iota_w", "iota_p", "base_b", "base_i", "dcol"))
    W2h, W2l, b2r, ones, eaW2, eaW1 = (k[n] for n in ("W2h", "W2l", "b2r", "ones", "eaW2", "eaW1"))
    A_d, Bh_d, Bl_d, agg_d, eaT, src_idx, dst_rows = (k[n] for n in ("A_d", "Bh_d", "Bl_d", "agg_d", "eaT", "src_idx", "dst_rows"))

    PRE_AHEAD = 5
    ACT_MSG = 1
    DVE_PRE = 4
    DVE_MSG = 2
    SEG_LAG = 3
    PREP_AHEAD = (9, 8, 8, 7)
    POOL_MSG = 2
    GATHER_AHEAD = 8
    ACC_LAG = 9
    BANK = (0, 1, 2, 0, 1, 2, 0, 1)
    BACK = (2, 2, 3, 3, 3, 3, 3, 3)
    FIRST, LOOP0 = -PREP_AHEAD[0], 16
    LOOP1 = 4 * FULL - 16
    LAST = 4 * NG + SEG_LAG + 2
    PRES = 4 * NG
    MSGS = 4 * FULL + 1
    assert (LOOP1 - LOOP0) % 8 == 0 and G * FULL + ETAIL == E and 0 < ETAIL <= P

    st, sb, ps = scope()
    with st:
        xg = [sb(f"xg{i}", [P, SUB, H]) for i in range(2)]
        idx = [sb(f"idx{i}", [P, SUB], I32) for i in range(2)]
        ea = [sb(f"ea{i}", [P, G]) for i in range(2)]
        db = [sb(f"db{i}", [64, G], I32) for i in range(2)]
        M1 = [sb(f"M1_{i}", [P, G], F32R) for i in range(2)]
        M2 = [sb(f"M2_{i}", [P, G], F32R) for i in range(2)]
        hTh = [sb(f"hTh{i}", [P, KC, G], F32R) for i in range(2)]
        hTl = [sb(f"hTl{i}", [P, KC, G], F32R) for i in range(2)]
        rp = [sb(f"rp{i}", [P, G]) for i in range(2)]
        rm = [sb(f"rm{i}", [P, H]) for i in range(2)]
        tp = [sb(f"tp{i}", [P, G]) for i in range(2)]
        tm = [sb(f"tm{i}", [P, H]) for i in range(2)]
        mh = [sb(f"mh{i}", [P, H], F32R) for i in range(4)]
        ml = [sb(f"ml{i}", [P, H], F32R) for i in range(4)]
        oh = [sb(f"oh{i}", [P, SUB, P], F32R) for i in range(2)]
        ev = [sb(f"ev{i}", [WIN, H]) for i in range(2)]
        bp = [ps(f"bp{i}") for i in range(3)]
        bm = [ps(f"bm{i}") for i in range(4)]
        bs = ps("bs")

        q_in = [sem(f"e_in{i}") for i in range(2)]
        q_win = [sem(f"e_win{i}") for i in range(2)]
        q_ix = [sem(f"e_ix{i}") for i in range(2)]
        q_ga = [sem(f"e_ga{i}") for i in range(2)]
        q_acc = sem("e_acc")
        s_zero = sem("e_zero")
        s_go = sem("e_go")
        s_prep = sem("e_prep")
        s_oh = sem("e_oh")
        s_pre = sem("e_pre")
        s_msg = sem("e_msg")
        s_seg = sem("e_seg")
        a_pre = sem("a_pre")
        v_sq = sem("v_sq")
        a_msg = sem("a_msg")
        v_pre = sem("v_pre")
        v_msg = sem("v_msg")
        p_msg = sem("p_msg")
        s_ev = sem("e_ev")

        def tail(u):
            return u.reg is None and u.const >= 4 * FULL

        def wait(e, s, val):
            if not (isinstance(val, int) and val < 1):
                e.wait_ge(s, val)

        @work.on("sync")
        def _(e):
            def loads(u):
                p, n = u.par, ETAIL if tail(u) else G
                wait(e, q_ga[p], u.pair(64, 0))
                e.dma_start(idx[p][:], src_idx[bass.ds(u.group(), 1), :, :].rearrange("a p s -> (a p) s"))\
                 .then_inc(q_ix[p], 16)
                wait(e, s_prep, u.group(4, -4))
                for a, b in HALF:
                    e.dma_start(ea[p][a:b, 0:n], eaT[:, bass.ds(u.group(G), n)]).then_inc(q_in[p], 16)
                e.dma_start(db[p][:, 0:n], dst_rows[bass.ds(u.group(), 1), 0:n].to_broadcast([64, n]))\
                 .then_inc(q_in[p], 16)
                b = e.value_load(base_i[0:1, bass.ds(u.group(), 1)], min_val=0, max_val=NP - WIN)
                wait(e, s_pre, u.val(1, -4))
                e.dma_start(eaW1[p][0:32, :].bitcast(F32), Bh_d[bass.ds(b, WIN), :]).then_inc(q_win[p], 16)
                e.dma_start(eaW1[p][32:64, :].bitcast(F32), Bl_d[bass.ds(b, WIN), :]).then_inc(q_win[p], 16)

            loads(At(None, 0))
            loads(At(None, 4))
            with e.Fori(1, FULL // 2) as i:
                loads(At(i, 0))
                loads(At(i, 4))
            loads(At(None, 4 * FULL))
            e.wait_ge(q_acc, 16 * NG)

        @work.on("gpsimd")
        def _(e):
            def gather(u):
                p, n, r = u.par, 1 if tail(u) else SUB, ETAIL if tail(u) else P
                e.wait_ge(q_ix[p], u.pair(16, 16))
                wait(e, s_pre, u.val(1, -4))
                e.sem_inc(s_go, 1)
                for t in range(n):
                    e.indirect_dma_start(out=xg[p][0:r, t, :], out_offset=None, in_=A_d,
                                         in_offset=bass.IndirectOffsetOnAxis(ap=idx[p][0:r, t:t + 1], axis=0))\
                     .then_inc(q_ga[p], 16)

            def accumulate(u):
                b = e.value_load(base_i[0:1, bass.ds(u.group(), 1)], min_val=0, max_val=NP - WIN)
                e.wait_ge(s_ev, u.group(1, 1))
                wait(e, q_acc, u.group(16))
                e.dma_start(agg_d[bass.ds(b, WIN), :], ev[u.par][:], accum_op=ALU.add).then_inc(q_acc, 16)

            def lo(m):
                r, j = ETAIL if tail(m) else P, m.j
                e.wait_ge(v_msg, m.val(2, 2))
                e.tensor_tensor(ml[j][0:r, :], tm[m.const % 2][0:r, :], mh[j][0:r, :], ALU.subtract).then_inc(p_msg, 1)

            def step(s):
                if (s + -POOL_MSG).has(MSGS):
                    lo(s + -POOL_MSG)
                if s.j == 0 and (s + GATHER_AHEAD).has(4 * NG):
                    gather(s + GATHER_AHEAD)
                if s.j == ACC_LAG % SUB and (s + -ACC_LAG).has(4 * FULL):
                    accumulate(s + -ACC_LAG)

            for i in range(2):
                e.memset(oh[i][:].bitcast(F32), 0.0).then_inc(s_zero, 1)
            slots(e, FIRST, LOOP0, LOOP1, LAST, step)
            accumulate(At(None, 4 * FULL))

        @work.on("tensor")
        def _(e):
            def pre(u):
                j, p, w, bank = u.j, u.par, ETAIL if tail(u) else G, bp[BANK[u.const % 8]]
                wait(e, v_pre, u.val(3, 1 - 3 * BACK[u.const % 8]))
                if j == 0:
                    n = 16 if tail(u) else 64
                    e.wait_ge(q_ga[p], u.pair(64, n))
                    e.wait_ge(q_win[p], u.pair(32, 32))
                    e.wait_ge(s_prep, u.group(4, 4))
                for t in range(SUB if w == G else 1):
                    r = min(P, w)
                    e.matmul(bank[:, t * P:t * P + r], xg[p][0:r, t, j * P:(j + 1) * P], ident[0:r, 0:r],
                             start=t == 0, stop=False, is_transpose=True, skip_group_check=True)
                e.matmul(bank[:, 0:w], eaW1[p][:, j * P:(j + 1) * P], M1[p][:, 0:w], start=False, stop=False,
                         skip_group_check=True)
                e.matmul(bank[:, 0:w], eaW2[:, j * P:(j + 1) * P], M2[p][:, 0:w], start=False, stop=True,
                         skip_group_check=True).then_inc(s_pre, 1)

            def msg(u):
                j, p, r = u.j, u.par, ETAIL if tail(u) else P
                wait(e, v_msg, u.val(2, 1 - 8))
                bank = bm[j]
                e.matmul(bank[0:r, :], ones[:, 0:r], b2r[:], start=True, stop=False)
                for c in range(KC):
                    if j == 0:
                        e.wait_ge(v_pre, u.val(3, 3 * c + 3))
                    for a, w in ((hTh, W2h), (hTl, W2h), (hTh, W2l)):
                        last = e.matmul(bank[0:r, :], a[p][:, c, j * P:j * P + r], w[:, c, :], start=False,
                                        stop=c == KC - 1 and w is W2l)
                last.then_inc(s_msg, 1)

            def seg(u):
                j, p, r = u.j, u.par, ETAIL if tail(u) else P
                e.wait_ge(v_msg, u.val(2, 2))
                e.wait_ge(p_msg, u.val(1, 1))
                e.wait_ge(s_oh, u.val(1, 1))
                if j == 0:
                    wait(e, s_ev, u.group())
                end = j == SUB - 1 or r < P
                e.matmul(bs[:, :], oh[p][0:r, j, :], mh[j][0:r, :], start=j == 0, stop=False)
                e.matmul(bs[:, :], oh[p][0:r, j, :], ml[j][0:r, :], start=False, stop=end).then_inc(s_seg, 1)

            def step(s):
                if (s + PRE_AHEAD).has(PRES):
                    pre(s + PRE_AHEAD)
                if s.has(MSGS):
                    msg(s)
                if (s + -SEG_LAG).has(MSGS):
                    seg(s + -SEG_LAG)

            slots(e, FIRST, LOOP0, LOOP1, LAST, step)

        @work.on("scalar")
        def _(e):
            def pre_chain(u, k):
                w = ETAIL if tail(u) else G
                t = rp[u.const % 2][:, 0:w]
                if k == 0:
                    wait(e, v_pre, u.val(3, 1 - 6))
                    e.wait_ge(s_pre, u.val(1, 1))
                    e.activation(t, bp[BANK[u.const % 8]][:, 0:w], ACT.Exp, bias=LNSQ).then_inc(a_pre, 1)
                elif k == 2:
                    e.wait_ge(v_sq, u.val(1, 1))
                    e.activation(t, t, ACT.Ln, bias=1.0, scale=0.5 / (SQ * SQ)).then_inc(a_pre, 1)
                elif k == 3:
                    e.wait_ge(a_pre, u.val(3, 2))
                    e.activation(t, t, ACT.Exp, scale=-1.0).then_inc(a_pre, 1)

            def msg_chain(m, k):
                r = ETAIL if tail(m) else P
                t = rm[m.const % 2][0:r, :]
                if k == 0:
                    wait(e, v_msg, m.val(2, 1 - 4))
                    e.wait_ge(s_msg, m.val(1, 1))
                    e.activation(t, bm[m.j][0:r, :], ACT.Exp).then_inc(a_msg, 1)
                    return
                e.wait_ge(a_msg, m.val(4, k))
                if k == 1:
                    e.activation(t, t, ACT.Square, bias=SQ, scale=SQ).then_inc(a_msg, 1)
                elif k == 2:
                    e.activation(t, t, ACT.Ln, bias=0.5, scale=0.5 / (SQ * SQ)).then_inc(a_msg, 1)
                else:
                    e.activation(t, t, ACT.Exp, scale=-1.0).then_inc(a_msg, 1)

            def step(s):
                u, m = s + PRE_AHEAD, s + -ACT_MSG
                for pre, k in ((1, 0), (0, 0), (0, 1), (1, 2), (0, 2), (1, 3), (0, 3)):
                    if pre and u.has(PRES):
                        pre_chain(u, k)
                    if not pre and m.has(MSGS):
                        msg_chain(m, k)

            slots(e, FIRST, LOOP0, LOOP1, LAST, step)

        @work.on("vector")
        def _(e):
            def prep(u, k):
                p, n, gs = u.par, ETAIL if tail(u) else G, bass.ds(u.group(), 1)
                if k == 0:
                    e.wait_ge(q_in[p], u.pair(48, 48))
                    wait(e, s_pre, u.val(1, -4))
                    e.tensor_copy(M2[p][:, 0:n], ea[p][:, 0:n]).then_inc(s_prep, 1)
                elif k == 1:
                    e.tensor_copy(M1[p][64:128, 0:n], ea[p][64:128, 0:n]).then_inc(s_prep, 1)
                elif k == 2:
                    e.tensor_scalar(M1[p][0:64, 0:n], db[p][:, 0:n], base_b[0:64, gs, 0], iota_p[0:64, :],
                                    ALU.subtract, ALU.is_equal).then_inc(s_prep, 1)
                else:
                    e.wait_ge(s_prep, u.group(4, 1))
                    e.tensor_tensor(M2[p][0:64, 0:n], ea[p][0:64, 0:n], M2[p][0:64, 0:n], ALU.subtract)\
                     .then_inc(s_prep, 1)

            def onehot(u):
                wait(e, s_seg, u.val(1, 1 - 8))
                e.tensor_scalar(oh[u.par][:, u.j, 0:WIN], iota_w[:], base_b[:, bass.ds(u.group(), 1), 0],
                                dcol[:, bass.ds(u.val(), 1)], ALU.add, ALU.is_equal).then_inc(s_oh, 1)

            def square(u):
                w = ETAIL if tail(u) else G
                t = rp[u.const % 2][:, 0:w]
                e.wait_ge(a_pre, u.val(3, 1))
                e.scalar_tensor_tensor(t, t, 2.0 * SQ, t, ALU.add, ALU.mult).then_inc(v_sq, 1)

            def pre(u, k):
                w, p, j = ETAIL if tail(u) else G, u.par, u.j
                t = tp[u.const % 2][:, 0:w]
                if k == 0:
                    e.wait_ge(a_pre, u.val(3, 3))
                    e.scalar_tensor_tensor(t, rp[u.const % 2][:, 0:w], 1.0, bp[BANK[u.const % 8]][:, 0:w],
                                           ALU.subtract, ALU.mult).then_inc(v_pre, 1)
                    return
                e.wait_ge(v_pre, u.val(3, k))
                if k == 1:
                    if j == 0:
                        wait(e, s_msg, u.val(1, -4))
                    e.tensor_copy(hTh[p][:, j, 0:w], t).then_inc(v_pre, 1)
                else:
                    e.tensor_tensor(hTl[p][:, j, 0:w], t, hTh[p][:, j, 0:w], ALU.subtract).then_inc(v_pre, 1)

            def msg(m, k):
                r, j = ETAIL if tail(m) else P, m.j
                t = tm[m.const % 2][0:r, :]
                if k == 0:
                    wait(e, p_msg, m.val(1, -1))
                    e.wait_ge(a_msg, m.val(4, 4))
                    e.scalar_tensor_tensor(t, rm[m.const % 2][0:r, :], 1.0, bm[j][0:r, :], ALU.subtract, ALU.mult)\
                     .then_inc(v_msg, 1)
                else:
                    e.wait_ge(v_msg, m.val(2, 1))
                    wait(e, s_seg, m.val(1, 1 - 4))
                    e.tensor_copy(mh[j][0:r, :], t).then_inc(v_msg, 1)

            def step(s):
                u, m, v = s + DVE_PRE, s + -DVE_MSG, s + PRE_AHEAD
                if u.has(PRES):
                    pre(u, 0)
                if v.has(PRES):
                    square(v)
                if u.has(PRES):
                    pre(u, 1)
                q = s + -(SEG_LAG + 1)
                if (q.j == SUB - 1 and q.has(MSGS)) or (q.reg is None and q.const == MSGS - 1):
                    e.wait_ge(s_seg, q.val(1, 1))
                    wait(e, q_acc, q.group(16, -16))
                    e.tensor_copy(ev[q.par][:], bs[0:WIN, :]).then_inc(s_ev, 1)
                if m.has(MSGS):
                    msg(m, 0)
                if u.has(PRES):
                    pre(u, 2)
                if m.has(MSGS):
                    msg(m, 1)
                for k in range(4):
                    g = s + PREP_AHEAD[k]
                    if g.j == 0 and g.has(4 * NG):
                        prep(g, k)
                if s.has(MSGS):
                    if s.reg is None and s.const == 0:
                        e.wait_ge(s_zero, 2)
                    onehot(s)

            slots(e, FIRST, LOOP0, LOOP1, LAST, step)


def edge_general(work, scope, sem, k):
    A_d, Bh_d, Bl_d, agg_d, eaT, src_cols, dst_cols, W1, W2, b2, dcol, ident, row_bcast = (
        k[n] for n in ("A_d", "Bh_d", "Bl_d", "agg_d", "eaT", "src_cols", "dst_cols", "W1", "W2", "b2", "dcol",
                       "ident", "row_bcast"))
    st, sb, ps = scope()
    with st:
        idx_all = sb("g_idx_all", [P, 2, NG * SUB], I32)
        idx = sb("g_idx", [P, 2], I32)
        xa = sb("g_xa", [P, H])
        xb = sb("g_xb", [P, 2, H])
        ea = sb("g_ea", [ED, P])
        we = sb("g_we", [ED, H])
        w2 = sb("g_w2", [P, KC, H])
        b2b = sb("g_b2b", [P, H])
        rho = sb("g_rho", [P, H])
        t = sb("g_t", [P, H])
        tT = sb("g_tT", [P, KC, P])
        iota_i = sb("g_iota_i", [P, NP], I32)
        iota_n = sb("g_iota_n", [P, NP])
        oh = sb("g_oh", [P, NP])
        agg = sb("g_agg", [P, NCH, H])
        px, pT = ps("g_px"), ps("g_pT")
        pa = [ps(f"g_pa{i}") for i in range(NCH // 2)]

        q_k = sem("g_k")
        q_agg = sem("g_out")
        chain = Chain(sem("g_s"), sem("g_ga"), sem("g_go"))

        def one(op, *args, **kw):
            return lambda e, s: op(e)(*args, **kw).then_inc(s, 1)

        def mish():
            act = lambda e: e.activation
            return [("scalar", 1, one(act, rho[:], xa[:], ACT.Exp)),
                    ("scalar", 1, one(act, rho[:], rho[:], ACT.Square, bias=SQ, scale=SQ)),
                    ("scalar", 1, one(act, rho[:], rho[:], ACT.Ln, bias=0.5, scale=0.5 / (SQ * SQ))),
                    ("scalar", 1, one(act, rho[:], rho[:], ACT.Exp, scale=-1.0)),
                    ("vector", 1, one(lambda e: e.scalar_tensor_tensor, t[:], rho[:], 1.0, xa[:], ALU.subtract, ALU.mult))]

        def setup(e, s):
            e.wait_ge(q_k, 5 * 16)
            e.tensor_copy(iota_n[:], iota_i[:]).then_inc(s, 1)
            e.tensor_scalar(w2[:], w2[:], -1.0, None, ALU.mult).then_inc(s, 1)
            e.memset(agg[:], 0.0).then_inc(s, 1)
            e.memset(xa[:], 0.0).then_inc(s, 1)

        start = [("gpsimd", 1, one(lambda e: e.iota, iota_i[:], pattern=[[1, NP]], base=0, channel_multiplier=0)),
                 ("vector", 4, setup)]

        def subtile(i, r):
            def copy_idx(e, s):
                e.tensor_copy(idx[:], idx_all[:, :, bass.ds(i, 1)].rearrange("p a b -> p (a b)")).then_inc(s, 1)

            def gather(e, s):
                for dst, tab, col in ((xa[0:r, :], A_d, 0), (xb[0:r, 0, :], Bh_d, 1), (xb[0:r, 1, :], Bl_d, 1)):
                    e.indirect_dma_start(out=dst, out_offset=None, in_=tab, in_offset=bass.IndirectOffsetOnAxis(
                        ap=idx[0:r, col:col + 1], axis=0)).then_inc(s, 16)

            def load_ea(e, s):
                e.dma_start(ea[:, 0:r], eaT[:, bass.ds(i * P, r)]).then_inc(s, 16)

            def transposes(e, s):
                for c in range(KC):
                    last = e.transpose(pT[:, c * P:(c + 1) * P], t[:, c * P:(c + 1) * P], ident[:])
                last.then_inc(s, 1)

            def messages(e, s):
                for c in range(KC):
                    last = e.matmul(px[:, :], tT[:, c, :], w2[:, c, :], start=c == 0, stop=c == KC - 1)
                last.then_inc(s, 1)

            def products(half):
                def step(e, s):
                    for n in range(NCH // 2):
                        c = half * (NCH // 2) + n
                        last = e.matmul(pa[n][:, :], oh[0:r, c * P:(c + 1) * P], t[0:r, :], start=True, stop=True)
                    last.then_inc(s, 1)
                return step

            def adds(half):
                def step(e, s):
                    for n in range(NCH // 2):
                        c = half * (NCH // 2) + n
                        e.tensor_tensor(agg[:, c, :], agg[:, c, :], pa[n][:, :], ALU.add).then_inc(s, 1)
                return step

            tt = lambda e: e.tensor_tensor
            return [("vector", 1, copy_idx),
                    ("gather", 48, gather),
                    ("sync", 16, load_ea),
                    ("tensor", 1, one(lambda e: e.matmul, px[0:r, :], ea[:, 0:r], we[:], start=True, stop=True)),
                    ("vector", 1, one(tt, xa[0:r, :], xa[0:r, :], xb[0:r, 0, :], ALU.add)),
                    ("vector", 1, one(tt, xa[0:r, :], xa[0:r, :], xb[0:r, 1, :], ALU.add)),
                    ("vector", 1, one(tt, xa[0:r, :], xa[0:r, :], px[0:r, :], ALU.add)),
                    *mish(),
                    ("tensor", 1, transposes),
                    ("scalar", 1, one(lambda e: e.activation, tT[:].rearrange("p k n -> p (k n)"), pT[:, :], ACT.Copy)),
                    ("tensor", 1, messages),
                    ("vector", 1, one(tt, xa[:], px[:, :], b2b[:], ALU.add)),
                    *mish(),
                    ("vector", 1, one(lambda e: e.tensor_scalar, oh[:], iota_n[:], dcol[:, bass.ds(i, 1)], None, ALU.is_equal)),
                    ("tensor", 1, products(0)), ("vector", NCH // 2, adds(0)),
                    ("tensor", 1, products(1)), ("vector", NCH // 2, adds(1))]

        def program(engine, e):
            chain.n = chain.g = 0
            chain.run(engine, e, start)
            chain.done(start)
            with e.Fori(0, SUB * FULL) as i:
                chain.run(engine, e, subtile(i, P), i)
            chain.done(subtile(0, P), SUB * FULL)
            chain.run(engine, e, subtile(SUB * FULL, ETAIL))
            chain.done(subtile(0, P))

        @work.on("sync")
        def _(e):
            e.dma_start(idx_all[:, 0, :], src_cols).then_inc(q_k, 16)
            e.dma_start(idx_all[:, 1, :], dst_cols).then_inc(q_k, 16)
            e.dma_start(we[:], W1[2 * H:2 * H + ED, :]).then_inc(q_k, 16)
            e.dma_start(w2[:], W2.rearrange("(c p) n -> p c n", p=P)).then_inc(q_k, 16)
            e.dma_start(b2b[:], row_bcast(b2, H, P)).then_inc(q_k, 16)
            program("sync", e)
            e.wait_ge(chain.s, chain.n)
            e.dma_start(agg_d.rearrange("(c p) n -> p c n", p=P), agg[:]).then_inc(q_agg, 16)
            e.wait_ge(q_agg, 16)

        @work.on("gpsimd")
        def _(e):
            program("gpsimd", e)

        @work.on("scalar")
        def _(e):
            program("scalar", e)

        @work.on("vector")
        def _(e):
            program("vector", e)

        @work.on("tensor")
        def _(e):
            program("tensor", e)


def node_phase(nc, scope, sem, k):
    ident, nTh, nTl, x1, W3raw, W3l, W4raw, W4l, q_w3 = (
        k[n] for n in ("ident", "nTh", "nTl", "x1", "W3raw", "W3l", "W4raw", "W4l", "q_w3"))
    x, h_d, agg_d, b3, b4 = (k[n] for n in ("x", "h_d", "agg_d", "b3", "b4"))
    gamma, beta, U, sv, Sh_d, Sl_d, row_bcast, newton = (
        k[n] for n in ("gamma", "beta", "U", "sv", "Sh_d", "Sl_d", "row_bcast", "newton"))
    BLK = [range(0, 4), range(4, 8), range(8, NCH)]
    NB = len(BLK)

    st, sb, ps = scope()
    with st:
        W3h = sb("W3h", [P, 2 * KC, H], F32R)
        W4h = sb("W4h", [P, KC, H], F32R)
        Us = sb("Us", [P, KC, R])
        b3c = sb("b3c", [P, KC])
        b4b = sb("b4b", [P, H])
        gab = sb("gab", [P, H])
        beb = sb("beb", [P, H])
        svb = sb("svb", [P, R])
        ag = sb("ag", [P, 4, H])
        aTh = sb("aTh", [P, KC, 4 * P], F32R)
        aTl = sb("aTl", [P, KC, 4 * P], F32R)
        xb1, uTh = k["twice"](sb, "uTh", [P, KC, 4 * P])
        uTl = sb("uTl", [P, KC, 4 * P], F32R)
        hb = sb("hb", [P, 4, H])
        xb = sb("xb", [P, 4, H])
        xf = [sb(f"xf{i}", [P, H]) for i in range(2)]
        rho = [sb(f"rho{i}", [P, H]) for i in range(2)]
        um = [sb(f"um{i}", [P, H]) for i in range(2)]
        h2T = [sb(f"h2T{i}", [P, KC, P]) for i in range(2)]
        Ss = [sb(f"Ss{i}", [P, R]) for i in range(2)]
        Sh = [sb(f"Sh{i}", [P, R], F32R) for i in range(2)]
        Sl = [sb(f"Sl{i}", [P, R], F32R) for i in range(2)]
        stats = sb("stats3", [P, 4, 6])
        mv = sb("mv3", [P, 4, 2])
        var = sb("var3", [P, 4])
        lnv = sb("lnv3", [P, 4])
        rstd = sb("rstd3", [P, 4])
        nmr = sb("nmr3", [P, 4])
        tmp = sb("tmp3", [P, 4])
        pt = [ps(f"pt{i}") for i in range(2)]
        pu = [ps(f"pu{i}") for i in range(2)]
        po = [ps(f"po{i}") for i in range(2)]
        psS = [ps(f"psS{i}") for i in range(2)]

        q_c = sem("n_c")
        q_ag = [sem(f"n_ag{b}") for b in range(NB)]
        q_h = [sem(f"n_hl{b}") for b in range(NB)]
        q_x = [sem(f"n_xl{b}") for b in range(NB)]
        q_S = [sem(f"n_S{i}") for i in range(2)]
        s_wh = sem("n_wh")
        s_wl = sem("n_wl")
        s_tr = sem("n_tr")
        s_ah = sem("n_ah")
        s_al = sem("n_al")
        s_u = sem("n_u")
        s_xf = sem("n_xf")
        s_rho = sem("n_rho")
        s_o = sem("n_o")
        s_hb = sem("n_hb")
        s_xb = sem("n_xb")
        s_ln = sem("n_ln")
        s_var = sem("n_var")
        s_r = sem("n_r")
        s_nm = sem("n_nm")
        s_h2 = sem("n_h2")
        s_t2 = sem("n_t2")
        s_e2 = sem("n_e2")
        s_S = sem("n_Sm")
        s_Sv = sem("n_Sv")

        HB = [hb, hb, ag[:, 2:4, :]]
        XB = [xb, xb1, ag[:, 0:2, :]]

        def first(b):
            return BLK[b][0]

        def uT(b, f, cols):
            if b == 0:
                return uTh[:, f, cols], uTl[:, f, cols]
            o = first(b - 1) * P
            cols = slice(o + cols.start, o + cols.stop)
            return nTh[:, f, cols], nTl[:, f, cols]

        with nc.Block() as blk:
            @blk.sync
            def _(e):
                def rows(tab, b, n):
                    return tab[first(b) * P:(first(b) + n) * P, :].rearrange("(c p) n -> p c n", p=P)

                def load_ag(b):
                    n = len(BLK[b])
                    if b:
                        e.wait_ge(s_tr, first(b))
                    e.dma_start(ag[:, 0:n, :], rows(agg_d, b, n)).then_inc(q_ag[b], 16)

                def load_hb(b):
                    if b == 1:
                        e.wait_ge(s_ln, first(b))
                    if b == 2:
                        e.wait_ge(s_tr, first(b))
                    e.dma_start(HB[b][:, 0:len(BLK[b]), :], rows(h_d, b, len(BLK[b]))).then_inc(q_h[b], 16)

                def load_xb(b):
                    n = len(BLK[b]) - (b == NB - 1)
                    if b == 1:
                        e.wait_ge(s_o, first(b))
                    if b == 2:
                        e.wait_ge(s_tr, NCH)
                    e.dma_start(XB[b][:, 0:n, :], rows(x, b, n)).then_inc(q_x[b], 16)
                    if b == NB - 1:
                        e.dma_start(XB[b][0:NTAIL, n, :], x[(NCH - 1) * P:N, :]).then_inc(q_x[b], 16)

                def store_S(b):
                    for c in BLK[b]:
                        e.wait_ge(s_Sv, 3 * c + 3)
                        rows = slice(c * P, (c + 1) * P)
                        e.dma_start(Sh_d[rows, :], Sh[c % 2][:].bitcast(F32)).then_inc(q_S[c % 2], 16)
                        e.dma_start(Sl_d[rows, :], Sl[c % 2][:].bitcast(F32)).then_inc(q_S[c % 2], 16)

                load_ag(0)
                with nc.allow_non_contiguous_dma(reason="512 values, once"):
                    e.dma_start(b3c[:], b3.rearrange("(c p) -> p c", p=P)).then_inc(q_c, 16)
                e.dma_start(b4b[:], row_bcast(b4, H, P)).then_inc(q_c, 16)
                e.dma_start(gab[:], row_bcast(gamma, H, P)).then_inc(q_c, 16)
                e.dma_start(beb[:], row_bcast(beta, H, P)).then_inc(q_c, 16)
                e.dma_start(svb[:], row_bcast(sv, R, P)).then_inc(q_c, 16)
                e.dma_start(Us[:], U.rearrange("(c p) n -> p c n", p=P)).then_inc(q_c, 16)
                load_hb(0)
                load_xb(0)
                load_ag(1)
                load_ag(2)
                load_hb(2)
                load_xb(1)
                load_hb(1)
                load_xb(2)
                for b in range(NB):
                    store_S(b)
                for i in range(2):
                    e.wait_ge(q_S[i], 32 * (NCH // 2))

            @blk.gpsimd
            def _(e):
                e.wait_ge(q_c, 6 * 16)
                for b in range(NB):
                    e.wait_ge(q_h[b], 16)
                    for c in range(len(BLK[b])):
                        e.tensor_tensor(HB[b][:, c, :], HB[b][:, c, :], b4b[:], ALU.add).then_inc(s_hb, 1)
                    e.wait_ge(q_x[b], 16 if b < NB - 1 else 32)
                    for c in range(len(BLK[b])):
                        r = NTAIL if first(b) + c == NCH - 1 else P
                        e.tensor_tensor(XB[b][0:r, c, :], XB[b][0:r, c, :], beb[0:r, :], ALU.add).then_inc(s_xb, 1)

            @blk.scalar
            def _(e):
                def stats_chain(i):
                    e.wait_ge(s_var, i + 1)
                    n = len(BLK[i // 2])
                    e.activation(lnv[:, 0:n], var[:, 0:n], ACT.Ln).then_inc(s_r, 1)
                    e.wait_ge(s_r, 2 * i + 1)
                    e.activation(rstd[:, 0:n], lnv[:, 0:n], ACT.Exp, scale=-0.5).then_inc(s_r, 1)

                def evac_agg(b):
                    for i, c in enumerate(BLK[b]):
                        e.wait_ge(s_tr, c + 1)
                        if i == 0 and b:
                            e.wait_ge(s_u, KC * b)
                        e.activation(aTh[:, :, i * P:(i + 1) * P], pt[c % 2][:, :].rearrange("p (k n) -> p k n", k=KC),
                                     ACT.Copy).then_inc(s_ah, 1)

                def chain(b, fs):
                    w = len(BLK[b]) * P
                    for f in fs:
                        i = KC * b + f
                        t = rho[i % 2][:, 0:w]
                        e.wait_ge(s_xf, 5 * i + 1)
                        e.activation(t, t, ACT.Exp).then_inc(s_rho, 1)
                        e.wait_ge(s_rho, 4 * i + 1)
                        e.activation(t, t, ACT.Square, bias=SQ, scale=SQ).then_inc(s_rho, 1)
                        e.wait_ge(s_rho, 4 * i + 2)
                        e.activation(t, t, ACT.Ln, bias=0.5, scale=0.5 / (SQ * SQ)).then_inc(s_rho, 1)
                        e.wait_ge(s_rho, 4 * i + 3)
                        e.activation(t, t, ACT.Exp, scale=-1.0).then_inc(s_rho, 1)

                def h2(b):
                    e.wait_ge(s_nm, b + 1)
                    for i, c in enumerate(BLK[b]):
                        e.activation(XB[b][:, i, :], x1[:, c, :], ACT.Relu, bias=nmr[:, i:i + 1], scale=rstd[:, i:i + 1])\
                         .then_inc(s_h2, 1)

                def evac_h2(b):
                    for c in BLK[b]:
                        e.wait_ge(s_t2, c + 1)
                        if c >= 2:
                            e.wait_ge(s_S, c - 1)
                        e.activation(h2T[c % 2][:], pt[c % 2][:, :].rearrange("p (k n) -> p k n", k=KC), ACT.Copy)\
                         .then_inc(s_e2, 1)

                for i, (hi, raw) in enumerate(((W3h[:, KC:, :], W3raw[:, KC:, :]), (W4h[:], W4raw[:]))):
                    e.wait_ge(q_w3[i + 1], 16)
                    e.activation(hi, raw, ACT.Copy, scale=-1.0).then_inc(s_wh, 1)
                    if i == 0:
                        evac_agg(0)
                chain(0, (0, 1, 2))
                evac_agg(1)
                chain(0, (3,))
                chain(1, (0, 1))
                stats_chain(0)
                chain(1, (2,))
                evac_agg(2)
                chain(1, (3,))
                stats_chain(1)
                h2(0)
                chain(2, (0, 1))
                stats_chain(2)
                chain(2, (2, 3))
                evac_h2(0)
                stats_chain(3)
                h2(1)
                stats_chain(4)
                evac_h2(1)
                stats_chain(5)
                h2(2)
                evac_h2(2)

            @blk.vector
            def _(e):
                s_v = sem("n_v")
                cnt = [0]

                def mark(ins):
                    cnt[0] += 1
                    ins.then_inc(s_v, 1)
                    return cnt[0]

                def link(ins):
                    e.wait_ge(s_v, mark(ins))

                def lo_agg(b):
                    for i, c in enumerate(BLK[b]):
                        e.wait_ge(s_ah, c + 1)
                        e.tensor_tensor(aTl[:, :, i * P:(i + 1) * P], pt[c % 2][:, :].rearrange("p (k n) -> p k n", k=KC),
                                        aTh[:, :, i * P:(i + 1) * P], ALU.subtract).then_inc(s_al, 1)

                def load_x(b, f):
                    i, w = KC * b + f, len(BLK[b]) * P
                    e.wait_ge(s_u, i + 1)
                    e.tensor_scalar(rho[i % 2][:, 0:w], pu[i % 2][:, 0:w], b3c[:, f:f + 1], XMAX, ALU.add, ALU.min)\
                     .then_inc(s_xf, 1)
                    e.tensor_scalar(xf[i % 2][:, 0:w], pu[i % 2][:, 0:w], b3c[:, f:f + 1], None, ALU.add).then_inc(s_xf, 1)

                def mish(b, f):
                    i, w = KC * b + f, len(BLK[b]) * P
                    t, (hi, lo) = um[i % 2][:, 0:w], uT(b, f, slice(0, w))
                    e.wait_ge(s_xf, 5 * i + 2)
                    e.wait_ge(s_rho, 4 * i + 4)
                    e.scalar_tensor_tensor(t, rho[i % 2][:, 0:w], 1.0, xf[i % 2][:, 0:w], ALU.subtract, ALU.mult)\
                     .then_inc(s_xf, 1)
                    e.wait_ge(s_xf, 5 * i + 3)
                    e.tensor_copy(hi, t).then_inc(s_xf, 1)
                    e.wait_ge(s_xf, 5 * i + 4)
                    e.tensor_tensor(lo, t, hi, ALU.subtract).then_inc(s_xf, 1)

                def units(b, fs):
                    for f in fs:
                        load_x(b, f)
                        mish(b, f)

                def norm(i, n):
                    for j in range(n):
                        (link if j == n - 1 else lambda ins: None)(e.bn_aggr(mv[:, j, :], stats[:, j, :]))
                    e.tensor_scalar(var[:, 0:n], mv[:, 0:n, 1], LN_EPS, None, ALU.add).then_inc(s_var, 1)
                    e.wait_ge(s_r, 2 * i + 2)
                    newton(e, link, var[:, 0:n], rstd[:, 0:n], tmp[:, 0:n])

                def add_out(b):
                    n = len(BLK[b])
                    for j, c in enumerate(BLK[b]):
                        e.wait_ge(s_o, c + 1)
                        e.wait_ge(s_hb, c + 1)
                        e.tensor_tensor(x1[:, c, :], po[c % 2][:, :], HB[b][:, j, :], ALU.add).then_inc(s_ln, 1)
                        e.wait_ge(s_ln, c + 1)
                        (link if j == n - 1 else lambda ins: None)(e.bn_stats(stats[:, j, :], x1[:, c, :]))
                    norm(2 * b, n)

                def scale_x1(b):
                    for j, c in enumerate(BLK[b]):
                        last = mark(e.scalar_tensor_tensor(x1[:, c, :], x1[:, c, :], mv[:, j, 0:1], gab[:],
                                                           ALU.subtract, ALU.mult))
                    return last

                def finish_x1(b, scaled):
                    done = []
                    e.wait_ge(s_v, scaled)
                    for j, c in enumerate(BLK[b]):
                        r = NTAIL if c == NCH - 1 else P
                        e.wait_ge(s_xb, c + 1)
                        done.append(mark(e.scalar_tensor_tensor(
                            x1[0:r, c, :], x1[0:r, c, :], rstd[0:r, j:j + 1], XB[b][0:r, j, :], ALU.mult, ALU.add)))
                    for j, c in enumerate(BLK[b]):
                        e.wait_ge(s_v, done[j])
                        last = mark(e.bn_stats(stats[:, j, :], x1[:, c, :]))
                    return last

                def second_norm(b, summed):
                    n = len(BLK[b])
                    e.wait_ge(s_v, summed)
                    norm(2 * b + 1, n)
                    e.scalar_tensor_tensor(nmr[:, 0:n], mv[:, 0:n, 0], -1.0, rstd[:, 0:n], ALU.mult, ALU.mult)\
                     .then_inc(s_nm, 1)

                def store_S(b):
                    for c in BLK[b]:
                        i = c % 2
                        e.wait_ge(s_S, c + 1)
                        if c >= 2:
                            e.wait_ge(q_S[i], 32 * (c // 2))
                        e.tensor_tensor(Ss[i][:], psS[i][:, 0:R], svb[:], ALU.mult).then_inc(s_Sv, 1)
                        e.wait_ge(s_Sv, 3 * c + 1)
                        e.tensor_copy(Sh[i][:], Ss[i][:]).then_inc(s_Sv, 1)
                        e.wait_ge(s_Sv, 3 * c + 2)
                        e.tensor_tensor(Sl[i][:], Ss[i][:], Sh[i][:], ALU.subtract).then_inc(s_Sv, 1)

                def lo_w(i, raw, hi, lo, sign):
                    if i:
                        e.wait_ge(s_wh, i)
                    e.scalar_tensor_tensor(lo, raw, sign, hi, ALU.mult, ALU.subtract).then_inc(s_wl, 1)

                e.wait_ge(q_w3[0], 16)
                link(e.tensor_copy(W3h[:, 0:KC, :], W3raw[:, 0:KC, :]))
                lo_w(0, W3raw[:, 0:KC, :], W3h[:, 0:KC, :], W3l[:, 0:KC, :], 1.0)
                lo_w(1, W3raw[:, KC:, :], W3h[:, KC:, :], W3l[:, KC:, :], -1.0)
                lo_agg(0)
                lo_w(2, W4raw[:], W4h[:], W4l[:], -1.0)
                e.wait_ge(q_c, 6 * 16)
                units(0, (0, 1, 2))
                load_x(0, 3)
                lo_agg(1)
                mish(0, 3)
                units(1, (0, 1))
                add_out(0)
                load_x(1, 2)
                scaled = scale_x1(0)
                mish(1, 2)
                summed = finish_x1(0, scaled)
                load_x(1, 3)
                lo_agg(2)
                mish(1, 3)
                second_norm(0, summed)
                units(2, (0, 1))
                add_out(1)
                load_x(2, 2)
                scaled = scale_x1(1)
                mish(2, 2)
                load_x(2, 3)
                summed = finish_x1(1, scaled)
                mish(2, 3)
                store_S(0)
                second_norm(1, summed)
                add_out(2)
                store_S(1)
                second_norm(2, finish_x1(2, scale_x1(2)))
                store_S(2)

            @blk.tensor
            def _(e):
                def agg_T(b):
                    e.wait_ge(q_ag[b], 16)
                    for i, c in enumerate(BLK[b]):
                        if c >= 2:
                            e.wait_ge(s_al, c - 1)
                        for f in range(KC):
                            last = e.transpose(pt[c % 2][:, f * P:(f + 1) * P], ag[:, i, f * P:(f + 1) * P], ident[:])
                        last.then_inc(s_tr, 1)

                def u_units(b, fs):
                    n0, w = first(b) * P, len(BLK[b]) * P
                    for f in fs:
                        i = KC * b + f
                        if i >= 2:
                            e.wait_ge(s_xf, 5 * (i - 2) + 2)
                        m = 0
                        for c in range(2 * KC):
                            if i == 0 and c in (0, KC):
                                e.wait_ge(s_wl, 1 + c // KC)
                            if f == 0 and c == KC:
                                e.wait_ge(s_al, BLK[b][-1] + 1)
                            ah, al = ((nTh[:, c, n0:n0 + w], nTl[:, c, n0:n0 + w]) if c < KC else
                                      (aTh[:, c - KC, 0:w], aTl[:, c - KC, 0:w]))
                            for wt, a in ((W3h, ah), (W3h, al), (W3l, ah)):
                                last = e.matmul(pu[i % 2][:, 0:w], wt[:, c, f * P:(f + 1) * P], a,
                                                start=m == 0, stop=m == 6 * KC - 1)
                                m += 1
                        last.then_inc(s_u, 1)

                def out_chunks(b):
                    if b == 0:
                        e.wait_ge(s_wl, 3)
                    for i, c in enumerate(BLK[b]):
                        if c >= 2:
                            e.wait_ge(s_ln, c - 1)
                        m = 0
                        for f in range(KC):
                            if i == 0:
                                e.wait_ge(s_xf, 5 * (KC * b + f) + 5)
                            uh, ul = uT(b, f, slice(i * P, (i + 1) * P))
                            for a, w in ((uh, W4h), (ul, W4h), (uh, W4l)):
                                last = e.matmul(po[c % 2][:, :], a, w[:, f, :], start=m == 0, stop=m == 3 * KC - 1)
                                m += 1
                        last.then_inc(s_o, 1)

                def S_chunks(b):
                    def transposes(i, c):
                        e.wait_ge(s_h2, c + 1)
                        if i == 0:
                            e.wait_ge(s_al, NCH)
                        if c >= 2:
                            e.wait_ge(s_e2, c - 1)
                        for f in range(KC):
                            last = e.transpose(pt[c % 2][:, f * P:(f + 1) * P], XB[b][:, i, f * P:(f + 1) * P], ident[:])
                        last.then_inc(s_t2, 1)

                    def product(c):
                        if c >= 2:
                            e.wait_ge(s_Sv, 3 * (c - 2) + 1)
                        e.wait_ge(s_e2, c + 1)
                        for f in range(KC):
                            last = e.matmul(psS[c % 2][:, 0:R], h2T[c % 2][:, f, :], Us[:, f, :], start=f == 0, stop=f == KC - 1)
                        last.then_inc(s_S, 1)

                    for i, c in enumerate(BLK[b]):
                        transposes(i, c)
                        if i:
                            product(c - 1)
                    product(BLK[b][-1])

                agg_T(0)
                e.wait_ge(q_c, 6 * 16)
                u_units(0, range(KC))
                agg_T(1)
                u_units(1, (0, 1))
                out_chunks(0)
                u_units(1, (2, 3))
                agg_T(2)
                u_units(2, (0, 1))
                out_chunks(1)
                u_units(2, (2, 3))
                S_chunks(0)
                out_chunks(2)
                S_chunks(1)
                S_chunks(2)


def conv_phase(nc, scope, sem, k):
    x1, row_bcast, wide_i = (k[n] for n in ("x1", "row_bcast", "wide_i"))
    src_cols, ew_cols, Vt, bias, out = (k[n] for n in ("src_cols", "ew_cols", "Vt", "bias", "out"))
    st, sb, ps = scope()
    with st:
        iota_ni = sb("iota_ni", [P, NP], I32)
        iota_n = sb("iota_n", [P, NP])
        scoli = sb("scoli", [P, NG * SUB], I32)
        paii = sb("paii", [P, NG * SUB], I32)
        scol = sb("scol", [P, NG * SUB])
        nscol = sb("nscol", [P, NG * SUB])
        odd = sb("odd", [P, NG * SUB])
        ewc = sb("ewc", [P, NG * SUB])
        ew2 = sb("ew2", [P, NG * SUB, 2])
        VV = sb("VV", [P, H])
        bib = sb("bib", [P, H])
        sums = sb("sums", [P, NP])
        res = [sb(f"res{i}", [P, H]) for i in range(2)]
        pc = [[ps(f"pc{odd}{i}") for i in range(2)] for odd in range(2)]
        pf = [ps(f"pf{i}") for i in range(2)]

        q_k = sem("k_k")
        q_v = sem("k_v")
        q_o = sem("k_o")
        s_c = sem("k_c")
        s_sum = sem("k_sum")
        s_f = sem("k_f")
        s_r = sem("k_r")

        def prelude(engine, e):
            if engine == "sync":
                e.dma_start(scoli[:], src_cols).then_inc(q_k, 16)
                e.dma_start(ewc[:], ew_cols).then_inc(q_k, 16)
                for a, b in HALF:
                    e.dma_start(VV[a:b, :], Vt).then_inc(q_v, 16)
                e.dma_start(bib[:], row_bcast(bias, H, P)).then_inc(q_v, 16)
            elif engine == "gpsimd":
                e.iota(iota_ni[:], pattern=[[1, NP]], base=0, channel_multiplier=0).then_inc(s_c, 1)
            elif engine == "vector":
                e.wait_ge(q_k, 2 * 16)
                e.tensor_scalar(paii[:], scoli[:], 1, None, ALU.arith_shift_right).then_inc(s_c, 1)
                e.tensor_scalar(scoli[:], scoli[:], 1, None, ALU.bitwise_and).then_inc(s_c, 1)
                e.wait_ge(s_c, 3)
                e.tensor_copy(scol[:], paii[:]).then_inc(s_c, 1)
                e.tensor_scalar(nscol[:], paii[:], -1.0, None, ALU.mult).then_inc(s_c, 1)
                e.tensor_copy(odd[:], scoli[:]).then_inc(s_c, 1)
                e.tensor_copy(iota_n[:], iota_ni[:]).then_inc(s_c, 1)
                e.wait_ge(s_c, 7)
                e.tensor_tensor(ew2[:, :, 1], ewc[:], odd[:], ALU.mult).then_inc(s_c, 1)
                e.wait_ge(s_c, 8)
                e.tensor_tensor(ew2[:, :, 0], ewc[:], ew2[:, :, 1], ALU.subtract).then_inc(s_c, 1)
                e.wait_ge(s_c, 9)

        narrow, general = Work(), Work()
        conv_narrow(narrow, scope, sem, k, locals())
        conv_general(general, scope, sem, k, locals())
        phase(nc, wide_i, narrow, general)

        with nc.Block() as blk:
            def evacuate(odd, i, copy):
                (c0, w) = SBLK[i]
                w = min(w, N // 2 - c0)
                nodes = sums[:].rearrange("p (n two) -> p n two", two=2)[:, c0:c0 + w, odd]
                copy(nodes, pc[odd][i][:, 0:w]).then_inc(s_sum, 1)

            @blk.scalar
            def _(e):
                for i in range(2):
                    evacuate(0, i, lambda out, src: e.activation(out, src, ACT.Copy))

            @blk.vector
            def _(e):
                for i in range(2):
                    evacuate(1, i, lambda out, src: e.tensor_copy(out, src))
                e.wait_ge(q_v, 3 * 16)
                for c in range(NCH):
                    r, t = min(P, N - c * P), res[c % 2]
                    e.wait_ge(s_f, c + 1)
                    e.tensor_tensor(t[0:r, :], pf[c % 2][0:r, :], bib[0:r, :], ALU.add).then_inc(s_r, 1)
                    e.wait_ge(s_r, 2 * c + 1)
                    e.scalar_tensor_tensor(x1[0:r, c, :], t[0:r, :], 0.0, x1[0:r, c, :], ALU.max, ALU.add).then_inc(s_r, 1)

            @blk.tensor
            def _(e):
                e.wait_ge(q_v, 3 * 16)
                e.wait_ge(s_sum, 4)
                for c in range(NCH):
                    r = min(P, N - c * P)
                    if c >= 2:
                        e.wait_ge(s_r, 2 * (c - 2) + 1)
                    e.matmul(pf[c % 2][0:r, :], sums[:, c * P:c * P + r], VV[:], start=True, stop=True).then_inc(s_f, 1)

            @blk.sync
            def _(e):
                for c in range(NCH):
                    r = min(P, N - c * P)
                    e.wait_ge(s_r, 2 * c + 2)
                    e.dma_start(out[c * P:c * P + r, :], x1[0:r, c, :]).then_inc(q_o, 16)
                e.wait_ge(q_o, 16 * NCH)


def conv_narrow(work, scope, sem, k, c):
    iota_p, base_b, base_i, Sh_d, Sl_d, dst_rows = (
        k[n] for n in ("iota_p", "base_b", "base_i", "Sh_d", "Sl_d", "dst_rows"))
    iota_n, scol, nscol, ew2, pc, prelude, s_c = (
        c[n] for n in ("iota_n", "scol", "nscol", "ew2", "pc", "prelude", "s_c"))
    BY_ACT = SUB // 2
    st, sb, ps = scope()
    with st:
        db = [sb(f"c_db{i}", [64, G], I32) for i in range(2)]
        oT = [sb(f"c_oT{i}", [64, G], F32R) for i in range(2)]
        Sw = [sb(f"c_Sw{i}", [64, R], F32R) for i in range(2)]
        gw = [sb(f"c_gw{i}", [P, SUB, 2, R]) for i in range(2)]
        ghl = [sb(f"c_ghl{i}", [P, SUB, 2, 2 * R], F32R) for i in range(2)]
        so = [sb(f"c_so{i}", [P, NPAIR], F32R) for i in range(SUB)]
        d2 = [sb(f"c_d2_{i}", [P, NPAIR]) for i in range(2 * (SUB - BY_ACT))]
        pg = [ps(f"pg{i}") for i in range(2)]

        q_in = [sem(f"k_in{i}") for i in range(2)]
        q_w = [sem(f"k_w{i}") for i in range(2)]
        s_oT = sem("k_oT")
        s_g = sem("k_g")
        s_gw = sem("k_gw")
        s_hi = sem("k_hi")
        s_lo = sem("k_lo")
        s_so = sem("k_so")
        s_sa = sem("k_sa")
        s_sc = sem("k_sc")

        def tail(u):
            return u.reg is None and u.const >= 4 * FULL

        def wait(e, s, val):
            if not (isinstance(val, int) and val < 1):
                e.wait_ge(s, val)

        def groups(e, step):
            for g in (0, 1):
                step(At(None, 4 * g))
            with e.Fori(1, FULL // 2 - 1) as i:
                for g in (0, 1):
                    step(At(i, 4 * g))
            for g in range(FULL - 2, NG):
                step(At(None, 4 * g))

        @work.on("sync")
        def _(e):
            prelude("sync", e)

            def loads(u):
                p, n = u.par, ETAIL if tail(u) else G
                wait(e, s_oT, u.group(1, -1))
                e.dma_start(db[p][:, 0:n], dst_rows[bass.ds(u.group(), 1), 0:n].to_broadcast([64, n]))\
                 .then_inc(q_in[p], 16)
                b = e.value_load(base_i[0:1, bass.ds(u.group(), 1)], min_val=0, max_val=NP - WIN)
                wait(e, s_g, u.group(1, -1))
                e.dma_start(Sw[p][0:32, :].bitcast(F32), Sh_d[bass.ds(b, WIN), :]).then_inc(q_w[p], 16)
                e.dma_start(Sw[p][32:64, :].bitcast(F32), Sl_d[bass.ds(b, WIN), :]).then_inc(q_w[p], 16)

            groups(e, loads)

        @work.on("gpsimd")
        def _(e):
            prelude("gpsimd", e)

        @work.on("scalar")
        def _(e):
            def step(u):
                if tail(u):
                    return
                for i, j in enumerate(range(BY_ACT, SUB)):
                    wait(e, s_sa, u.group(4, i - 5))
                    e.activation(d2[2 * u.par + i][:], iota_n[:, 0:NPAIR], ACT.Square, bias=nscol[:, bass.ds(u.val(1, j), 1)])\
                     .then_inc(s_sa, 1)
                for i, j in enumerate(range(BY_ACT, SUB)):
                    e.wait_ge(s_sa, u.group(4, i + 1))
                    wait(e, s_sc, u.val(1, j + 1 - SUB))
                    e.activation(so[j][:], d2[2 * u.par + i][:], ACT.Relu, bias=1.0, scale=-1.0).then_inc(s_sa, 1)

            e.wait_ge(s_c, 9)
            groups(e, step)

        @work.on("vector")
        def _(e):
            prelude("vector", e)

            def oneT(u):
                p, n = u.par, ETAIL if tail(u) else G
                e.wait_ge(q_in[p], u.pair(16, 16))
                wait(e, s_g, u.group(1, -1))
                e.tensor_scalar(oT[p][:, 0:n], db[p][:, 0:n], base_b[0:64, bass.ds(u.group(), 1), 0], iota_p[0:64, :],
                                ALU.subtract, ALU.is_equal).then_inc(s_oT, 1)

            def weigh(u):
                p, n, r = u.par, 1 if tail(u) else SUB, ETAIL if tail(u) else P
                e.wait_ge(s_g, u.group(1, 1))
                wait(e, s_lo, u.group(1, -1))
                rows = pg[p][0:r, 0:n * R].rearrange("p (s b a) -> p s b a", s=n, b=1).to_broadcast([r, n, 2, R])
                w = ew2[0:r, bass.ds(u.val(), n), :].rearrange("p s (b a) -> p s b a", a=1).to_broadcast([r, n, 2, R])
                e.tensor_tensor(gw[p][0:r, 0:n, :, :], rows, w, ALU.mult).then_inc(s_gw, 1)

            def hi(u):
                p, n, r = u.par, 1 if tail(u) else SUB, ETAIL if tail(u) else P
                e.wait_ge(s_gw, u.group(1, 1))
                wait(e, s_sc, u.val(1, -4))
                e.tensor_copy(ghl[p][0:r, 0:n, :, 0:R], gw[p][0:r, 0:n, :, :]).then_inc(s_hi, 1)

            def lo(u):
                p, n, r = u.par, 1 if tail(u) else SUB, ETAIL if tail(u) else P
                e.wait_ge(s_hi, u.group(1, 1))
                e.tensor_tensor(ghl[p][0:r, 0:n, :, R:2 * R], gw[p][0:r, 0:n, :, :], ghl[p][0:r, 0:n, :, 0:R], ALU.subtract)\
                 .then_inc(s_lo, 1)

            def onehot(u, j):
                r = ETAIL if tail(u) else P
                wait(e, s_sc, u.val(1, j + 1 - SUB))
                e.tensor_scalar(so[j][0:r, :], iota_n[0:r, 0:NPAIR], scol[0:r, bass.ds(u.val(1, j), 1)], None,
                                ALU.is_equal).then_inc(s_so, 1)

            def step(u):
                onehot(u, 0)
                if tail(u):
                    return
                weigh(u + 4)
                onehot(u, 1)
                if (u + 8).has(4 * NG):
                    oneT(u + 8)
                hi(u + 4)
                lo(u + 4)

            oneT(At(None, 0))
            oneT(At(None, 4))
            weigh(At(None, 0))
            hi(At(None, 0))
            lo(At(None, 0))
            groups(e, step)

        @work.on("tensor")
        def _(e):
            def rows_of(u):
                p, n, r = u.par, 1 if tail(u) else SUB, ETAIL if tail(u) else P
                e.wait_ge(q_w[p], u.pair(32, 32))
                e.wait_ge(s_oT, u.group(1, 1))
                wait(e, s_gw, u.group(1, -1))
                for j in range(n):
                    m = e.matmul(pg[p][0:r, j * R:(j + 1) * R], oT[p][:, j * P:j * P + r], Sw[p][:], start=j == 0,
                                 stop=j == n - 1, skip_group_check=True)
                m.then_inc(s_g, 1)

            def scatter(u):
                p, last = u.par, tail(u)
                r = ETAIL if last else P
                for j in range(1 if last else SUB):
                    if j == 0:
                        e.wait_ge(s_lo, u.group(1, 1))
                    if j == BY_ACT and (u + 8).has(4 * NG):
                        rows_of(u + 8)
                    if j >= BY_ACT:
                        e.wait_ge(s_sa, u.group(4, j + 1))
                    else:
                        e.wait_ge(s_so, u.group(BY_ACT, j + 1))
                    first = u.reg is None and u.const + j == 0
                    for odd in range(2):
                        for i, (c0, w) in enumerate(SBLK):
                            m = e.matmul(pc[odd][i][:, 0:w], ghl[p][0:r, j, odd, :], so[j][0:r, c0:c0 + w], start=first,
                                         stop=last, skip_group_check=True)
                    m.then_inc(s_sc, 1)

            rows_of(At(None, 0))
            rows_of(At(None, 4))
            groups(e, scatter)


def conv_general(work, scope, sem, k, c):
    Sh_d, Sl_d, dst_cols = (k[n] for n in ("Sh_d", "Sl_d", "dst_cols"))
    iota_n, scol, ew2, pc, prelude, s_c = (c[n] for n in ("iota_n", "scol", "ew2", "pc", "prelude", "s_c"))
    st, sb, _ = scope()
    with st:
        idx_all = sb("h_idx_all", [P, NG * SUB], I32)
        idx = sb("h_idx", [P, 1], I32)
        S = sb("h_S", [P, 2, R])
        g = sb("h_g", [P, 2, R])
        ghl = sb("h_ghl", [P, 2, 2 * R], F32R)
        so = sb("h_so", [P, NPAIR], F32R)
        q_k = sem("h_k")
        chain = Chain(sem("h_s"), sem("h_ga"), sem("h_go"))

        def subtile(i, r, first=False, last=False):
            def copy_idx(e, s):
                e.tensor_copy(idx[:], idx_all[:, bass.ds(i, 1)]).then_inc(s, 1)

            def gather(e, s):
                for n, tab in enumerate((Sh_d, Sl_d)):
                    e.indirect_dma_start(out=S[0:r, n, :], out_offset=None, in_=tab, in_offset=bass.IndirectOffsetOnAxis(
                        ap=idx[0:r, 0:1], axis=0)).then_inc(s, 16)

            def add(e, s):
                e.tensor_tensor(S[0:r, 0, :], S[0:r, 0, :], S[0:r, 1, :], ALU.add).then_inc(s, 1)

            def weigh(e, s):
                w = ew2[0:r, bass.ds(i, 1), :].rearrange("p a b -> p (a b)")
                for odd in range(2):
                    e.tensor_scalar(g[0:r, odd, :], S[0:r, 0, :], w[:, odd:odd + 1], None, ALU.mult).then_inc(s, 1)

            def hi(e, s):
                e.tensor_copy(ghl[0:r, :, 0:R], g[0:r, :, :]).then_inc(s, 1)

            def lo(e, s):
                e.tensor_tensor(ghl[0:r, :, R:2 * R], g[0:r, :, :], ghl[0:r, :, 0:R], ALU.subtract).then_inc(s, 1)

            def onehot(e, s):
                e.tensor_scalar(so[0:r, :], iota_n[0:r, 0:NPAIR], scol[0:r, bass.ds(i, 1)], None, ALU.is_equal)\
                 .then_inc(s, 1)

            def scatter(e, s):
                for odd in range(2):
                    for b, (c0, w) in enumerate(SBLK):
                        m = e.matmul(pc[odd][b][:, 0:w], ghl[0:r, odd, :], so[0:r, c0:c0 + w], start=first, stop=last,
                                     skip_group_check=True)
                m.then_inc(s, 1)

            return [("vector", 1, copy_idx), ("gather", 32, gather), ("vector", 1, add), ("vector", 2, weigh),
                    ("vector", 1, hi), ("vector", 1, lo), ("vector", 1, onehot), ("tensor", 1, scatter)]

        def program(engine, e):
            prelude(engine, e)
            if engine == "vector":
                e.wait_ge(q_k, 16)
            chain.n = chain.g = 0
            chain.run(engine, e, subtile(0, P, first=True))
            with e.Fori(1, SUB * FULL) as i:
                chain.run(engine, e, subtile(i, P), i)
            chain.done(subtile(0, P), SUB * FULL)
            chain.run(engine, e, subtile(SUB * FULL, ETAIL, last=True))

        @work.on("sync")
        def _(e):
            e.dma_start(idx_all[:], dst_cols).then_inc(q_k, 16)
            prelude("sync", e)

        @work.on("gpsimd")
        def _(e):
            program("gpsimd", e)

        @work.on("scalar")
        def _(e):
            e.wait_ge(s_c, 9)

        @work.on("vector")
        def _(e):
            program("vector", e)

        @work.on("tensor")
        def _(e):
            program("tensor", e)


def kernel(x, src, dst, edge_attr_64, edge_weight, L0_gnn_W1, L0_gnn_b1, L0_gnn_W2, L0_gnn_b2, L0_gnn_W3,
           L0_gnn_b3, L0_gnn_W4, L0_gnn_b4, L0_gnn_gamma, L0_gnn_beta, L1_gnn_U, L1_gnn_s, L1_gnn_Vt, L1_gnn_bias):
    import numpy as np
    import concourse.bacc as bacc
    from concourse.bass_utils import run_bass_kernel_spmd

    def groups(a):
        a = np.asarray(a)
        return np.concatenate([a, np.repeat(a[-1:], NG * G - E)]).reshape(NG, SUB, P)

    w = np.asarray(edge_weight)
    arrays = {
        "x": x,
        "src_idx": groups(src).transpose(0, 2, 1),
        "dst_rows": groups(dst).reshape(NG, G),
        "src_cols": groups(src).reshape(NG * SUB, P).T,
        "dst_cols": groups(dst).reshape(NG * SUB, P).T,
        "eaT": np.asarray(edge_attr_64).T,
        "ew_cols": groups(w).reshape(NG * SUB, P).T,
        "W1": L0_gnn_W1, "b1": L0_gnn_b1, "W2": L0_gnn_W2, "b2": L0_gnn_b2, "W3": L0_gnn_W3, "b3": L0_gnn_b3,
        "W4": L0_gnn_W4, "b4": L0_gnn_b4, "gamma": L0_gnn_gamma, "beta": L0_gnn_beta,
        "U": L1_gnn_U, "sv": L1_gnn_s, "Vt": L1_gnn_Vt, "bias": L1_gnn_bias,
    }
    arrays = {n: np.ascontiguousarray(a) for n, a in arrays.items()}
    nc = bacc.Bacc("TRN2", target_bir_lowering=False, num_devices=1)
    args = {n: nc.dram_tensor(f"in_{n}", a.shape, mybir.dt.from_np(a.dtype), kind="ExternalInput").ap()
            for n, a in arrays.items()}
    out = nc.dram_tensor("out_0", (N, H), F32, kind="ExternalOutput").ap()
    gnn_two_layers(nc, out=out, **args)
    r = run_bass_kernel_spmd(nc, [{f"in_{n}": a for n, a in arrays.items()}], core_ids=[0])
    return r.results[0]["out_0"]
```
